# Optimizing a Trainium2 kernel written in Bass

```python
import numpy as np
import jax
import jax.numpy as jnp

def _softmax(x, axis=-1):
    return jax.nn.softmax(x, axis=axis)

def _gelu(x):
    return jax.nn.gelu(x, approximate=True)

def _silu(x):
    return jax.nn.silu(x)

def _sigmoid(x):
    return jax.nn.sigmoid(x)

def _layernorm(x, axis=-1, eps=1e-05):
    m = jnp.mean(x, axis=axis, keepdims=True)
    v = jnp.var(x, axis=axis, keepdims=True)
    return (x - m) / jnp.sqrt(v + eps)

def _scatter_add(tgt, idx, src, axis=0):
    return tgt.at[idx].add(src)

def _segment_sum(src, seg, n):
    return jax.ops.segment_sum(src, seg, n)
kernel_name = 'mk_sandwich_d1_jaxref_r8_8b87e7'

def setup_inputs(seed: int=0):
    np.random.seed(seed)
    _w = jnp.asarray

    def _L0_attn_setup():
        import jax, jax.numpy as jnp
        import numpy as np
        B, S, D = (1, 256, 512)
        H = 32
        Q_RANK, KV_RANK = (192, 64)
        NOPE, ROPE, VD = (128, 64, 128)
        QD = NOPE + ROPE
        EPS = 1e-06
        THETA = 10000.0

        def _rmsnorm(x, w):
            return x * jax.lax.rsqrt(jnp.mean(x * x, axis=-1, keepdims=True) + EPS) * w

        def _rotate_half(x):
            h = x.shape[-1] // 2
            return jnp.concatenate([-x[..., h:], x[..., :h]], axis=-1)

        def _apply_rope(x, cos, sin):
            xp = jnp.concatenate([x[..., 0::2], x[..., 1::2]], axis=-1)
            return xp * cos + _rotate_half(xp) * sin

        def _mla_forward(hidden_states, Wq_a, q_a_ln_w, Wq_b, Wkv_a, kv_a_ln_w, Wkv_b, Wo):
            b, s, _ = hidden_states.shape
            q = _rmsnorm(hidden_states @ Wq_a, q_a_ln_w) @ Wq_b
            q = q.reshape(b, s, H, QD).transpose(0, 2, 1, 3)
            q_nope, q_pe = (q[..., :NOPE], q[..., NOPE:])
            ckv = hidden_states @ Wkv_a
            compressed, k_pe = (ckv[..., :KV_RANK], ckv[..., KV_RANK:])
            kv = _rmsnorm(compressed, kv_a_ln_w) @ Wkv_b
            kv = kv.reshape(b, s, H, NOPE + VD).transpose(0, 2, 1, 3)
            k_nope, v = (kv[..., :NOPE], kv[..., NOPE:])
            k_pe = k_pe[:, None, :, :]
            inv_freq = 1.0 / THETA ** (jnp.arange(0, ROPE, 2, dtype=jnp.float32) / ROPE)
            freqs = jnp.outer(jnp.arange(s, dtype=jnp.float32), inv_freq)
            emb = jnp.concatenate([freqs, freqs], axis=-1)
            cos = jnp.cos(emb)[None, None].astype(hidden_states.dtype)
            sin = jnp.sin(emb)[None, None].astype(hidden_states.dtype)
            q_pe = _apply_rope(q_pe, cos, sin)
            k_pe = _apply_rope(k_pe, cos, sin)
            qf = jnp.concatenate([q_nope, q_pe], axis=-1)
            kf = jnp.concatenate([k_nope, jnp.broadcast_to(k_pe, (b, H, s, ROPE))], axis=-1)
            scale = QD ** (-0.5)
            scores = jnp.einsum('bhqd,bhkd->bhqk', qf, kf) * scale
            causal = jnp.tril(jnp.ones((s, s), dtype=bool))
            scores = jnp.where(causal, scores, jnp.finfo(scores.dtype).min)
            probs = jax.nn.softmax(scores, axis=-1)
            o = jnp.einsum('bhqk,bhkd->bhqd', probs, v)
            o = o.transpose(0, 2, 1, 3).reshape(b, s, H * VD)
            return o @ Wo
        key = jax.random.key(seed)
        ks = jax.random.split(key, 8)
        std = 0.02
        return {'hidden_states': jax.random.normal(ks[0], (B, S, D), jnp.float32), 'Wq_a': jax.random.normal(ks[1], (D, Q_RANK), jnp.float32) * std, 'q_a_ln_w': jnp.ones((Q_RANK,), jnp.float32), 'Wq_b': jax.random.normal(ks[2], (Q_RANK, H * QD), jnp.float32) * std, 'Wkv_a': jax.random.normal(ks[3], (D, KV_RANK + ROPE), jnp.float32) * std, 'kv_a_ln_w': jnp.ones((KV_RANK,), jnp.float32), 'Wkv_b': jax.random.normal(ks[4], (KV_RANK, H * (NOPE + VD)), jnp.float32) * std, 'Wo': jax.random.normal(ks[5], (H * VD, D), jnp.float32) * std}
    _L0_attn_in = _L0_attn_setup()

    def _L0_ffn_setup():
        import jax, jax.numpy as jnp
        import numpy as np
        LORA_SCALING = 1.0 / 2.0

        def _qlora_linear(x, wq, A, B):
            w = jnp.tile(wq, (1, 4))
            base = x @ w.T
            lora = x @ A.T @ B.T
            return base + lora * LORA_SCALING
        key = jax.random.key(seed)
        ks = jax.random.split(key, 10)
        d, h, r = (512, 1376, 2)
        return {'x': jax.random.normal(ks[0], (16, 1, d), dtype=jnp.float32), 'w1q': jax.random.normal(ks[1], (h, d // 4), dtype=jnp.float32) * 0.02, 'a1': jax.random.normal(ks[2], (r, d), dtype=jnp.float32) * 0.02, 'b1': jax.random.normal(ks[3], (h, r), dtype=jnp.float32) * 0.02, 'w3q': jax.random.normal(ks[4], (h, d // 4), dtype=jnp.float32) * 0.02, 'a3': jax.random.normal(ks[5], (r, d), dtype=jnp.float32) * 0.02, 'b3': jax.random.normal(ks[6], (h, r), dtype=jnp.float32) * 0.02, 'w2q': jax.random.normal(ks[7], (d, h // 4), dtype=jnp.float32) * 0.02, 'a2': jax.random.normal(ks[8], (r, h), dtype=jnp.float32) * 0.02, 'b2': jax.random.normal(ks[9], (d, r), dtype=jnp.float32) * 0.02}
    _L0_ffn_in = _L0_ffn_setup()
    _d = {'L0_attn_hidden_states': _L0_attn_in['hidden_states'], 'L0_attn_Wq_a': _L0_attn_in['Wq_a'], 'L0_attn_q_a_ln_w': _L0_attn_in['q_a_ln_w'], 'L0_attn_Wq_b': _L0_attn_in['Wq_b'], 'L0_attn_Wkv_a': _L0_attn_in['Wkv_a'], 'L0_attn_kv_a_ln_w': _L0_attn_in['kv_a_ln_w'], 'L0_attn_Wkv_b': _L0_attn_in['Wkv_b'], 'L0_attn_Wo': _L0_attn_in['Wo'], 'L0_ffn_w1q': _L0_ffn_in['w1q'], 'L0_ffn_a1': _L0_ffn_in['a1'], 'L0_ffn_b1': _L0_ffn_in['b1'], 'L0_ffn_w3q': _L0_ffn_in['w3q'], 'L0_ffn_a3': _L0_ffn_in['a3'], 'L0_ffn_b3': _L0_ffn_in['b3'], 'L0_ffn_w2q': _L0_ffn_in['w2q'], 'L0_ffn_a2': _L0_ffn_in['a2'], 'L0_ffn_b2': _L0_ffn_in['b2']}
    _x0 = _d['L0_attn_hidden_states']
    _d['L0_attn_hidden_states'] = jax.random.normal(jax.random.fold_in(jax.random.key(seed), 1), (2, 512, 512), dtype=_x0.dtype)
    del _x0
    return _d

def reference(L0_attn_hidden_states, L0_attn_Wq_a, L0_attn_q_a_ln_w, L0_attn_Wq_b, L0_attn_Wkv_a, L0_attn_kv_a_ln_w, L0_attn_Wkv_b, L0_attn_Wo, L0_ffn_w1q, L0_ffn_a1, L0_ffn_b1, L0_ffn_w3q, L0_ffn_a3, L0_ffn_b3, L0_ffn_w2q, L0_ffn_a2, L0_ffn_b2):

    def _L0_attn_ref(hidden_states, Wq_a, q_a_ln_w, Wq_b, Wkv_a, kv_a_ln_w, Wkv_b, Wo):
        import jax, jax.numpy as jnp
        import numpy as np
        B, S, D = (1, 256, 512)
        H = 32
        Q_RANK, KV_RANK = (192, 64)
        NOPE, ROPE, VD = (128, 64, 128)
        QD = NOPE + ROPE
        EPS = 1e-06
        THETA = 10000.0

        def _rmsnorm(x, w):
            return x * jax.lax.rsqrt(jnp.mean(x * x, axis=-1, keepdims=True) + EPS) * w

        def _rotate_half(x):
            h = x.shape[-1] // 2
            return jnp.concatenate([-x[..., h:], x[..., :h]], axis=-1)

        def _apply_rope(x, cos, sin):
            xp = jnp.concatenate([x[..., 0::2], x[..., 1::2]], axis=-1)
            return xp * cos + _rotate_half(xp) * sin

        def _mla_forward(hidden_states, Wq_a, q_a_ln_w, Wq_b, Wkv_a, kv_a_ln_w, Wkv_b, Wo):
            b, s, _ = hidden_states.shape
            q = _rmsnorm(hidden_states @ Wq_a, q_a_ln_w) @ Wq_b
            q = q.reshape(b, s, H, QD).transpose(0, 2, 1, 3)
            q_nope, q_pe = (q[..., :NOPE], q[..., NOPE:])
            ckv = hidden_states @ Wkv_a
            compressed, k_pe = (ckv[..., :KV_RANK], ckv[..., KV_RANK:])
            kv = _rmsnorm(compressed, kv_a_ln_w) @ Wkv_b
            kv = kv.reshape(b, s, H, NOPE + VD).transpose(0, 2, 1, 3)
            k_nope, v = (kv[..., :NOPE], kv[..., NOPE:])
            k_pe = k_pe[:, None, :, :]
            inv_freq = 1.0 / THETA ** (jnp.arange(0, ROPE, 2, dtype=jnp.float32) / ROPE)
            freqs = jnp.outer(jnp.arange(s, dtype=jnp.float32), inv_freq)
            emb = jnp.concatenate([freqs, freqs], axis=-1)
            cos = jnp.cos(emb)[None, None].astype(hidden_states.dtype)
            sin = jnp.sin(emb)[None, None].astype(hidden_states.dtype)
            q_pe = _apply_rope(q_pe, cos, sin)
            k_pe = _apply_rope(k_pe, cos, sin)
            qf = jnp.concatenate([q_nope, q_pe], axis=-1)
            kf = jnp.concatenate([k_nope, jnp.broadcast_to(k_pe, (b, H, s, ROPE))], axis=-1)
            scale = QD ** (-0.5)
            scores = jnp.einsum('bhqd,bhkd->bhqk', qf, kf) * scale
            causal = jnp.tril(jnp.ones((s, s), dtype=bool))
            scores = jnp.where(causal, scores, jnp.finfo(scores.dtype).min)
            probs = jax.nn.softmax(scores, axis=-1)
            o = jnp.einsum('bhqk,bhkd->bhqd', probs, v)
            o = o.transpose(0, 2, 1, 3).reshape(b, s, H * VD)
            return o @ Wo
        return _mla_forward(hidden_states, Wq_a, q_a_ln_w, Wq_b, Wkv_a, kv_a_ln_w, Wkv_b, Wo)

    def _L0_ffn_ref(x, w1q, a1, b1, w3q, a3, b3, w2q, a2, b2):
        import jax, jax.numpy as jnp
        import numpy as np
        LORA_SCALING = 1.0 / 2.0

        def _qlora_linear(x, wq, A, B):
            w = jnp.tile(wq, (1, 4))
            base = x @ w.T
            lora = x @ A.T @ B.T
            return base + lora * LORA_SCALING
        gate = jax.nn.silu(_qlora_linear(x, w1q, a1, b1))
        up = _qlora_linear(x, w3q, a3, b3)
        return _qlora_linear(gate * up, w2q, a2, b2)
    x = L0_attn_hidden_states
    x = x + _layernorm(_L0_attn_ref(_layernorm(x, axis=-1), L0_attn_Wq_a, L0_attn_q_a_ln_w, L0_attn_Wq_b, L0_attn_Wkv_a, L0_attn_kv_a_ln_w, L0_attn_Wkv_b, L0_attn_Wo), axis=-1)
    x = x + _layernorm(_L0_ffn_ref(_layernorm(x, axis=-1), L0_ffn_w1q, L0_ffn_a1, L0_ffn_b1, L0_ffn_w3q, L0_ffn_a3, L0_ffn_b3, L0_ffn_w2q, L0_ffn_a2, L0_ffn_b2), axis=-1)
    return x

_drawn_inputs = setup_inputs


def setup_inputs(seed=0):
    import zlib

    import numpy as np

    out = dict(_drawn_inputs(seed))
    spreads = {'L0_attn_q_a_ln_w': (1.0, 0.6), 'L0_attn_kv_a_ln_w': (1.0, 0.2)}
    factors = {'L0_ffn_a1': 5.914,
     'L0_ffn_b1': 5.606,
     'L0_ffn_a3': 6.138,
     'L0_ffn_b3': 6.686,
     'L0_ffn_a2': 6.834,
     'L0_ffn_b2': 6.939}
    for name, (base, spread) in spreads.items():
        noise = np.random.default_rng([zlib.crc32(name.encode()), seed]).standard_normal(out[name].shape)
        drawn = base * np.exp(spread * noise) if base else spread * noise
        out[name] = jnp.asarray(drawn.astype(out[name].dtype))
    for name, factor in factors.items():
        out[name] = (out[name] * factor).astype(out[name].dtype)
    return out
```

```python
import concourse.bass as bass
from concourse import mybir
import numpy as np

F32 = mybir.dt.float32
F32R = mybir.dt.float32r
ALU = mybir.AluOpType
ACT = mybir.ActivationFunctionType
AX = mybir.AxisListType

P = 128
BATCH, SEQ, D = 2, 512, 512
TOK = BATCH * SEQ
TB = TOK // P
QB = SEQ // P
DC = D // P
H, PAIRS = 32, 16
RQ, RKV = 192, 64
NOPE, ROPE, VD = 128, 64, 128
HR = ROPE // 2
LAT = RQ + RKV + ROPE
SCALE = float(NOPE + ROPE) ** -0.5
LN_EPS, RMS_EPS = 1e-5, 1e-6
BIG = 3.0e38
XB = 5
UNITS = 2 * QB
PU = BATCH * UNITS
HID, RANK = 1376, 2
FOLD = 4
W2C = HID // FOLD
RT = (W2C + P - 1) // P
RROWS = [min(P, W2C - P * r) for r in range(RT)]
SQ_COLS = 2 * 2 * P + 2 * RKV + 2 * 2 * ROPE
SV_COLS = 2 * RKV + 2 * D
LORA_SCALE = 0.5
CST_BYTES = 4 * (3 * SEQ + 8)


class Semaphores(dict):

    __getattr__ = dict.__getitem__


class Map:

    def __init__(self, nc, start, end):
        self.nc, self.at, self.end = nc, start, end

    def take(self, name, shape, dt=F32):
        t = self.nc.alloc_sbuf_tensor_at(name, shape, dt, offset=self.at)
        self.at += (4 * int(np.prod(shape[1:])) + 31) // 32 * 32
        assert self.at <= self.end, (name, self.at, self.end)
        return t


def build(nc, x_d, wa_d, lnw_d, cst_d, kcs_d, sq_d, sv_d, w13_d, bs_d, a13_d, a2_d, w2_d, b2_d, out_d):
    wvo_d = nc.dram_tensor("wvo_scratch", [PAIRS, P, D], F32, kind="Internal").ap()
    top = nc.sbuf_usable_end // 32 * 32
    start = (nc.sbuf_base + 63) // 64 * 64

    keep = Map(nc, start, top)
    ident = keep.take("ident", [P, P])
    cst = keep.take("cst", [P, 3 * SEQ + 8])
    ot = keep.take("ot", [P, PAIRS, TOK])
    late = keep.at
    mask = cst[:, 0:SEQ]
    cos1 = cst[:, SEQ:2 * SEQ]
    sin1 = cst[:, 2 * SEQ:3 * SEQ]
    eps_ln = cst[:, 3 * SEQ + 2:3 * SEQ + 3]
    eps_rms = cst[:, 3 * SEQ + 3:3 * SEQ + 4]

    att = Map(nc, late, top)
    ql_hi = att.take("ql_hi", [P, 2, TOK], F32R)
    ql_lo = att.take("ql_lo", [P, 2, TOK], F32R)
    kt_hi = att.take("kt_hi", [P, TOK], F32R)
    kt_lo = att.take("kt_lo", [P, TOK], F32R)
    kvn = att.take("kvn", [P, TB, P])
    sq = att.take("sq", [P, SQ_COLS])
    sv = att.take("sv", [P, SV_COLS])
    w1_hi = att.take("w1_hi", [P, 2, P], F32R)
    w1_lo = att.take("w1_lo", [P, 2, P], F32R)
    w2 = att.take("w2", [P, 2, P], F32R)
    qt_hi = att.take("qt_hi", [P, BATCH, 2, SEQ], F32R)
    qt_lo = att.take("qt_lo", [P, BATCH, 2, SEQ], F32R)
    small = att.take("small", [P, 64])
    early_end = att.at
    qrot = att.take("qrot", [P, 2, SEQ])
    qswp = att.take("qswp", [P, 2, SEQ])
    ss = att.take("ss", [P, 2, SEQ])
    pr = att.take("pr", [P, 4, SEQ])
    pt = att.take("pt", [P, 2, 2, QB, SEQ])
    rb = att.take("rb", [P, QB, 2, RKV])
    rsb = att.take("rsb", [P, SEQ])
    vs = att.take("vs", [P, D])
    negmax = small[:, 0:8]
    rsum = small[:, 8:24]
    rinv = small[:, 24:32]

    fir = Map(nc, start + 4 * P + CST_BYTES, late)
    xa = fir.take("xa", [P, TB, D])
    xn = fir.take("xn", [P, TB, D])
    xt_hi = fir.take("xt_hi", [P, 4, DC, P], F32R)
    xt_lo = fir.take("xt_lo", [P, 4, DC, P], F32R)
    qn = fir.take("qn", [P, TB, 2 * P])
    fi2 = Map(nc, early_end, top)
    wa = fi2.take("wa", [P, DC, LAT])
    wa_hi = fi2.take("wa_hi", [P, DC, LAT], F32R)
    wa_lo = fi2.take("wa_lo", [P, DC, LAT], F32R)
    lnw = fi2.take("lnw", [P, RQ + RKV])
    kcs = fi2.take("kcs", [P, QB, 2, ROPE])
    kra = fi2.take("kra", [P, TB, ROPE])
    krb = fi2.take("krb", [P, TB, ROPE])
    sqj = fi2.take("sqj", [P, 2, RQ])
    st1 = fi2.take("st1", [P, TB, 16])

    pro = Map(nc, late, top)
    o_hi = pro.take("o_hi", [P, 2, PAIRS // 2, P], F32R)
    o_lo = pro.take("o_lo", [P, 2, PAIRS // 2, P], F32R)
    wv_raw = pro.take("wv_raw", [P, 2, 2, D])
    wv_hi = pro.take("wv_hi", [P, PAIRS, D], F32R)
    wv_lo = pro.take("wv_lo", [P, PAIRS, D], F32R)
    x1 = pro.take("x1", [P, TB, D])
    zt = pro.take("zt", [P, D])
    xn2 = pro.take("xn2", [P, D])
    fold = pro.take("fold", [P, P])
    xn2t = pro.take("xn2t", [P, DC, P])
    xft = pro.take("xft", [P, TOK])
    a13 = pro.take("a13", [P, DC, 96])
    lg = pro.take("lg", [P, TOK], F32R)
    lu = pro.take("lu", [P, TOK], F32R)
    w13 = pro.take("w13", [P, 2, HID])
    st2 = pro.take("st2", [P, 16])
    bs = nc.alloc_sbuf_tensor_at("bs", [96, HID], F32, offset=start + 4 * P)

    ffn = Map(nc, start + 4 * P + CST_BYTES, late)
    w13_hi = ffn.take("w13_hi", [P, 2, HID], F32R)
    w13_lo = ffn.take("w13_lo", [P, 2, HID], F32R)
    bs_s = ffn.take("bs_s", [96, HID], F32R)
    xf_hi = ffn.take("xf_hi", [P, TOK], F32R)
    xf_lo = ffn.take("xf_lo", [P, TOK], F32R)
    b2 = ffn.take("b2", [P, D])
    a2 = ffn.take("a2", [P, RT, FOLD, 32])
    l2 = ffn.take("l2", [P, 2, SEQ])
    sg = ffn.take("sg", [P, 2, SEQ])
    ff2 = Map(nc, late, late + 4 * 40960 // 2)
    gu = ff2.take("gu", [P, 8, SEQ])
    fs = ff2.take("fs", [P, 2, RT, SEQ])
    fs_hi = ff2.take("fs_hi", [P, 2, RT, SEQ], F32R)
    fs_lo = ff2.take("fs_lo", [P, 2, RT, SEQ], F32R)
    wd = ff2.take("wd", [P, RT, D])
    wd_hi = ff2.take("wd_hi", [P, RT, D], F32R)
    wd_lo = ff2.take("wd_lo", [P, RT, D], F32R)
    z2 = ff2.take("z2", [P, 2, D])
    yo = ff2.take("yo", [P, 2, D])
    st3 = ff2.take("st3", [P, 2, 16])

    bank = [nc.alloc_psum_tensor(f"bank{i}", [P, 512], F32) for i in range(8)]

    def sems(phase, words):
        return Semaphores((n, nc.alloc_semaphore(f"{phase}_{n}")) for n in words.split())

    f = sems("first", """stats_made_raw ident_zero ident_made wa_in lnw_in cst_in kcs_in stats_made std_made rstd_made xn_made
        x_turned xt_hi_made xt_split wa_hi_made wa_split lat_made squares_summed std_rms_made rstd_rms_made
        qn_made krot_parts kvn_made qk_turned qk_hi_made qk_split""")
    x_in = [nc.alloc_semaphore(f"x_in{t}") for t in range(TB)]
    a = sems("attention", """s_seen rinv_seen sq_in sv_in wq_made wq_hi_made wq_split q_made q_rotated pe_added qt_hi_made qt_split
        s_made s_masked exp_made p_turned p_moved o_made rinv_made rb_made r_made r_moved o_scaled
        wvo_made wvo_moved wvo_out""")
    c = sems("projection", """wv_in0 wv_in1 wv_hi_made wv_split o_hi_made o_split o_used y_made x1_in w13_in bs_in a13_in
        dve_step act_step std1_made z_made std2_made fold_made y_turned xt2_moved xf_moved lp_made lp_hi_made lp_split""")
    g = sems("forward", """wd_in b2_in a2_in w_hi_made w_split xf_hi_made xf_split bs_hi_made bs_split bs_fixed wd_hi_made wd_split
        gate_made up_made silu_made gu_made la_made fold_added fs_hi_made fs_split l2_made
        y_made std_made z_made dve_step out_made out_sent""")

    xb = x_d.rearrange("b (t p) d -> (b t) p d", p=P)
    ob = out_d.rearrange("b (t p) d -> (b t) p d", p=P)
    block = nc.Block()
    with block:
        @block.sync
        def _(sp):
            for t in range(2):
                sp.dma_start(xa[:, t, :], xb[t]).then_inc(x_in[t], 16)
            sp.dma_start(cst[:, :], cst_d).then_inc(f.cst_in, 16)
            sp.dma_start(wa[:, :, :], wa_d).then_inc(f.wa_in, 16)
            for t in range(2, TB):
                sp.dma_start(xa[:, t, :], xb[t]).then_inc(x_in[t], 16)
            sp.dma_start(lnw[:, :], lnw_d).then_inc(f.lnw_in, 16)
            sp.dma_start(kcs[:, :, :, :], kcs_d).then_inc(f.kcs_in, 16)
            sp.dma_start(sq[:, :], sq_d[0]).then_inc(a.sq_in, 16)
            sp.dma_start(sv[:, :], sv_d[0]).then_inc(a.sv_in, 16)
            with nc.sync.Fori(0, PAIRS - 1) as p:
                sp.wait_ge(a.wq_split, p + 1)
                sp.dma_start(sq[:, :], sq_d[bass.ds(p + 1, 1)].rearrange("a p n -> p (a n)")).then_inc(a.sq_in, 16)
                sp.wait_ge(a.wvo_made, p + 1)
                sp.dma_start(sv[:, :], sv_d[bass.ds(p + 1, 1)].rearrange("a p n -> p (a n)")).then_inc(a.sv_in, 16)
                sp.wait_ge(a.wvo_moved, p + 1)
                sp.dma_start(wvo_d[bass.ds(p, 1)].rearrange("a p n -> p (a n)"), vs[:, :]).then_inc(a.wvo_out, 16)
            sp.wait_ge(a.wvo_moved, PAIRS)
            sp.dma_start(wvo_d[PAIRS - 1], vs[:, :]).then_inc(a.wvo_out, 16)

            sp.wait_ge(a.o_scaled, 2 * PAIRS)
            sp.wait_ge(a.wvo_out, 16 * PAIRS)
            for k in range(PAIRS // 2):
                if k >= 2:
                    sp.wait_ge(c.wv_split, k - 1)
                sp.dma_start(wv_raw[:, k % 2, :, :], wvo_d[2 * k:2 * k + 2].rearrange("a p n -> p a n"))\
                  .then_inc((c.wv_in0, c.wv_in1)[k % 2], 16)
                if k == 1:
                    sp.dma_start(x1[:, :, :], xb.rearrange("t p d -> p t d")).then_inc(c.x1_in, 16)
                    sp.dma_start(a13[:, :, :], a13_d).then_inc(c.a13_in, 16)
            sp.dma_start(w13[:, :, :], w13_d).then_inc(c.w13_in, 16)
            sp.dma_start(bs[:, :], bs_d).then_inc(c.bs_in, 16)
            sp.wait_ge(c.o_used, 2 * TB)
            sp.dma_start(a2[:, :, :, :], a2_d).then_inc(g.a2_in, 16)
            sp.dma_start(wd[:, :, :], w2_d).then_inc(g.wd_in, 16)
            sp.dma_start(b2[:, :], b2_d).then_inc(g.b2_in, 16)
            for t in range(TB):
                sp.wait_ge(g.out_made, t + 1)
                sp.dma_start(ob[t], yo[:, t % 2, :]).then_inc(g.out_sent, 16)
                if t + 1 < TB:
                    sp.wait_ge(g.out_sent, 16 * (t + 1))
            sp.wait_ge(g.out_sent, 16 * TB)

        @block.gpsimd
        def _(pool):
            nc.gpsimd.memset(ident[:, :], 0.0).then_inc(f.ident_zero, 1)
            pool.wait_ge(f.ident_zero, 1)
            nc.gpsimd.affine_select(out=ident[:, :], in_=ident[:, :], compare_op=ALU.not_equal, fill=1.0,
                                    base=0, pattern=[[-1, P]], channel_multiplier=1).then_inc(f.ident_made, 1)

            def add_rotated(gi, h, spread_before=None):
                if spread_before is not None:
                    pool.wait_ge(a.rb_made, spread_before)
                pool.wait_ge(a.q_rotated, gi + 1)
                nc.gpsimd.tensor_tensor(qrot[RKV:P, h, :], qrot[RKV:P, h, :], qswp[RKV:P, h, :], ALU.add)\
                  .then_inc(a.pe_added, 1)

            def spread(m, added, first=False):
                pool.wait_ge(a.pe_added, added)
                pool.wait_ge(a.rinv_made, m + 1)
                if not first:
                    pool.wait_ge(a.r_made, m)
                pool.sem_inc(a.rinv_seen, 1)
                nc.gpsimd.tensor_copy(rb[:, :, :, :],
                                      rinv.rearrange("p (h i) -> p i h", h=2).unsqueeze(3).to_broadcast([P, QB, 2, RKV]))\
                  .then_inc(a.rb_made, 1)

            def body(p, first=False, last=False):
                for h in range(2):
                    add_rotated(4 * p + 2 + h, h, 2 * p if h == 0 and not first else None)
                spread(2 * p, 4 * p + 4, first)
                if not last:
                    for h in range(2):
                        add_rotated(4 * p + 4 + h, h, 2 * p + 1 if h == 0 else None)
                spread(2 * p + 1, 4 * p + (4 if last else 6))

            for h in range(2):
                add_rotated(h, h)
            body(0, first=True)
            with nc.gpsimd.Fori(1, PAIRS - 1) as p:
                body(p)
            body(PAIRS - 1, last=True)

            for hf in range(2):
                for r in range(RT):
                    n = RROWS[r]
                    for k in range(1, FOLD):
                        pool.wait_ge(g.gu_made, 12 * hf + 4 * r + k + 1)
                        if (hf, r, k) != (0, 0, 1):
                            pool.wait_ge(g.fold_added, 3 * (3 * hf + r) + k - 1)
                        at = lambda q: (12 * hf + 4 * r + q) % 8
                        nc.gpsimd.tensor_tensor(fs[0:n, hf, r, :], gu[0:n, at(0), :] if k == 1 else fs[0:n, hf, r, :],
                                                gu[0:n, at(k), :], ALU.add).then_inc(g.fold_added, 1)

        @block.scalar
        def _(act):
            def lat_view(t):
                return bank[2 + t % 3]

            act.wait_ge(f.cst_in, 16)
            for t in range(TB + 4):
                if t < TB:
                    act.wait_ge(f.stats_made, t + 1)
                    nc.scalar.activation(st1[:, t, 8:9], st1[:, t, 7:8], ACT.Sqrt, bias=eps_ln).then_inc(f.std_made, 1)
                if 0 <= t - 1 < TB:
                    u = t - 1
                    act.wait_ge(f.x_turned, u + 1)
                    if u >= 4:
                        act.wait_ge(f.lat_made, u - 3)
                    nc.scalar.activation(xt_hi[:, u % 4, :, :], bank[u % 2][:, :].rearrange("p (c n) -> p c n", c=DC),
                                         ACT.Copy).then_inc(f.xt_hi_made, 1)
                if t == 1:
                    act.wait_ge(f.wa_in, 16)
                    nc.scalar.activation(wa_hi[:, :, :], wa[:, :, :], ACT.Copy).then_inc(f.wa_hi_made, 1)
                if 0 <= t - 2 < TB:
                    u = t - 2
                    act.wait_ge(f.lat_made, u + 1)
                    nc.scalar.activation(sqj[:, 0, :], lat_view(u)[:, 0:RQ], ACT.Square, scale=RQ ** -0.5,
                                         accum_out=st1[:, u, 10:11]).then_inc(f.squares_summed, 1)
                    nc.scalar.activation(sqj[:, 1, 0:RKV], lat_view(u)[:, RQ:RQ + RKV], ACT.Square, scale=RKV ** -0.5,
                                         accum_out=st1[:, u, 11:12]).then_inc(f.squares_summed, 1)
                    act.wait_ge(f.squares_summed, 2 * (u + 1))
                    nc.scalar.activation(st1[:, u, 12:14], st1[:, u, 10:12], ACT.Sqrt, bias=eps_rms)\
                      .then_inc(f.std_rms_made, 1)
                if 0 <= t - 4 < TB:
                    u = t - 4
                    tq = bank[5 + u % 2]
                    act.wait_ge(f.qk_turned, u + 1)
                    nc.scalar.activation(ql_hi[:, :, u * P:(u + 1) * P],
                                         tq[:, 0:2 * P].rearrange("p (c n) -> p c n", c=2), ACT.Copy)
                    nc.scalar.activation(kt_hi[:, u * P:(u + 1) * P], tq[:, 2 * P:3 * P], ACT.Copy)\
                      .then_inc(f.qk_hi_made, 1)

            def weights_hi(w, first=False):
                act.wait_ge(a.wq_made, w + 1)
                if not first:
                    act.wait_ge(a.q_made, 4 * w)
                pv = bank[XB][:, 0:4 * RKV].rearrange("p (k h n) -> p k h n", k=2, h=2)
                rv = sq[:, SQ_COLS - 4 * ROPE:SQ_COLS].rearrange("p (k h n) -> p k h n", k=2, h=2)
                nc.scalar.activation(w1_hi[:, :, 0:RKV], pv[:, 0], ACT.Copy)
                nc.scalar.activation(w1_hi[:, :, RKV:P], rv[:, 0], ACT.Copy)
                nc.scalar.activation(w2[:, :, 0:RKV], pv[:, 1], ACT.Copy)
                nc.scalar.activation(w2[:, :, RKV:P], rv[:, 1], ACT.Copy).then_inc(a.wq_hi_made, 1)

            def query_hi(gi, b, h, s_done=None):
                act.wait_ge(a.pe_added, gi + 1)
                if s_done is not None:
                    act.wait_ge(a.s_made, s_done)
                nc.scalar.activation(qt_hi[:, b, h, :], qrot[:, h, :], ACT.Copy).then_inc(a.qt_hi_made, 1)

            def exponent(U, k, s_first=False, old=None):
                n = P * (k % QB + 1)
                act.wait_ge(a.s_masked, U + 1)
                if not s_first:
                    act.wait_ge(a.p_turned, U - 3)
                if old is not None:
                    act.wait_ge(a.rinv_made, old)
                nc.scalar.activation(pr[:, k % 4, 0:n], ss[:, k % 2, 0:n], ACT.Exp, bias=negmax[:, k % 8:k % 8 + 1],
                                     scale=-1.0, accum_out=rsum[:, k:k + 1]).then_inc(a.exp_made, 1)

            def move_p(U, k, old=None):
                i, h, b = k % QB, k // QB % 2, k // UNITS
                act.wait_ge(a.p_turned, U + 1)
                if old is not None:
                    act.wait_ge(a.o_made, old)
                nc.scalar.activation(pt[:, b, h, 0:i + 1, i * P:(i + 1) * P],
                                     bank[2 + k % 2][:, 0:(i + 1) * P].rearrange("p (j q) -> p j q", q=P),
                                     ACT.Copy).then_inc(a.p_moved, 1)

            def move_r(m, first=False):
                act.wait_ge(a.r_made, m + 1)
                if not first:
                    act.wait_ge(a.o_scaled, m)
                nc.scalar.activation(rsb[:, :], bank[XB][:, :], ACT.Copy).then_inc(a.r_moved, 1)

            def body(p, first=False, last=False):
                for k in range(PU):
                    move_p(PU * p + k, k, 2 * p - 1 + k // UNITS if k % UNITS == 0 and not first else None)
                    n = k + 2
                    if n < PU:
                        exponent(PU * p + n, n, first and n < 4, 2 * p if n == UNITS and not first else None)
                    elif not last:
                        exponent(PU * p + n, n - PU, False, 2 * p + 1 if n == PU else None)
                    if k == 1 and not last:
                        weights_hi(p + 1)
                    if k in (3, 5):
                        h = (k - 3) // 2
                        query_hi(4 * p + 2 + h, 1, h, None if first else PU * (p - 1) + UNITS + QB * (h + 1))
                    if k in (11, 13) and not last:
                        h = (k - 11) // 2
                        query_hi(4 * p + 4 + h, 0, h, PU * p + QB * (h + 1))
                    if k == 4 and not first:
                        move_r(2 * p - 1)
                    if k == 12:
                        move_r(2 * p, first)
                    if k == 6:
                        act.wait_ge(a.wvo_made, p + 1)
                        if not first:
                            act.wait_ge(a.wvo_out, 16 * p)
                        nc.scalar.activation(vs[:, :], bank[XB][:, :], ACT.Copy).then_inc(a.wvo_moved, 1)

            weights_hi(0, first=True)
            for h in range(2):
                query_hi(h, 0, h)
            exponent(0, 0, True)
            exponent(1, 1, True)
            body(0, first=True)
            with nc.scalar.Fori(1, PAIRS - 1) as p:
                body(p)
            body(PAIRS - 1, last=True)
            move_r(2 * PAIRS - 1)

            def o_part(t, hh):
                if t:
                    act.wait_ge(c.o_used, 2 * t + hh - 1)
                nc.scalar.activation(o_hi[:, hh, :, :], ot[:, 8 * hh:8 * hh + 8, t * P:(t + 1) * P], ACT.Copy)\
                  .then_inc(c.o_hi_made, 1)

            act.wait_ge(a.o_scaled, 2 * PAIRS)
            o_part(0, 0)
            for k in range(PAIRS // 2):
                act.wait_ge((c.wv_in0, c.wv_in1)[k % 2], 16 * (k // 2 + 1))
                nc.scalar.activation(wv_hi[:, 2 * k:2 * k + 2, :], wv_raw[:, k % 2, :, :], ACT.Copy)\
                  .then_inc(c.wv_hi_made, 1)
            for t in range(TB + 2):
                if t < TB:
                    o_part(t, 1)
                if 0 <= t - 2:
                    u = t - 2
                    act.wait_ge(c.lp_made, u + 1)
                    nc.scalar.activation(lg[0:96, u * P:(u + 1) * P], bank[4][0:96, 0:P], ACT.Copy,
                                         scale=cst[0:96, 3 * SEQ:3 * SEQ + 1])
                    nc.scalar.activation(lu[0:96, u * P:(u + 1) * P], bank[4][0:96, 0:P], ACT.Copy,
                                         scale=cst[0:96, 3 * SEQ + 1:3 * SEQ + 2]).then_inc(c.lp_hi_made, 1)
                if 0 <= t - 1 < TB:
                    u = t - 1
                    act.wait_ge(c.dve_step, 8 * u + 2)
                    nc.scalar.activation(st2[:, 8:9], st2[:, 7:8], ACT.Sqrt, bias=eps_ln).then_inc(c.std1_made, 1)
                    act.wait_ge(c.dve_step, 8 * u + 4)
                    nc.scalar.activation(zt[:, :], bank[u % 2][:, :], ACT.Identity, scale=st2[:, 9:10],
                                         bias=st2[:, 10:11]).then_inc(c.z_made, 1)
                    act.wait_ge(c.dve_step, 8 * u + 7)
                    nc.scalar.activation(st2[:, 8:9], st2[:, 7:8], ACT.Sqrt, bias=eps_ln).then_inc(c.std2_made, 1)
                if t + 1 < TB:
                    o_part(t + 1, 0)
                if 0 <= t - 1 < TB:
                    u = t - 1
                    act.wait_ge(c.y_turned, u + 1)
                    if u:
                        act.wait_ge(c.lp_made, u)
                    nc.scalar.activation(xn2t[:, :, :], bank[2][:, :].rearrange("p (c n) -> p c n", c=DC), ACT.Copy)
                    nc.scalar.activation(xft[:, u * P:(u + 1) * P], bank[3][:, 0:P], ACT.Copy).then_inc(c.xt2_moved, 1)

            act.wait_ge(c.o_used, 2 * TB)
            act.wait_ge(c.xt2_moved, TB)
            act.wait_ge(c.w13_in, 16)
            nc.scalar.activation(xf_hi[:, :], xft[:, :], ACT.Copy).then_inc(g.xf_hi_made, 1)
            for k in range(2):
                nc.scalar.activation(w13_hi[:, k, :], w13[:, k, :], ACT.Copy).then_inc(g.w_hi_made, 1)
            act.wait_ge(c.bs_in, 16)
            nc.scalar.activation(bs_s[:, :], bs[:, :], ACT.Copy).then_inc(g.bs_hi_made, 1)

            def down_hi(hf, r):
                n = RROWS[r]
                act.wait_ge(g.fold_added, 3 * (3 * hf + r + 1))
                nc.scalar.activation(fs_hi[0:n, hf, r, :], fs[0:n, hf, r, :], ACT.Copy).then_inc(g.fs_hi_made, 1)

            for hf in range(2):
                for n in range(12):
                    G, rows = 12 * hf + n, RROWS[n // FOLD]
                    act.wait_ge(g.gate_made, G + 1)
                    if G >= 2:
                        act.wait_ge(g.gu_made, G - 1)
                    nc.scalar.activation(sg[0:rows, G % 2, :], bank[5 + G % 2][0:rows, :], ACT.Silu)\
                      .then_inc(g.silu_made, 1)
                    if G == 3:
                        act.wait_ge(g.wd_in, 16)
                        nc.scalar.activation(wd_hi[:, :, :], wd[:, :, :], ACT.Copy).then_inc(g.wd_hi_made, 1)
                    if n in (7, 11):
                        down_hi(hf, n // FOLD - 1)
                down_hi(hf, RT - 1)
                act.wait_ge(g.la_made, RT * (hf + 1))
                nc.scalar.activation(l2[:, hf, :], bank[3][:, :], ACT.Copy, scale=LORA_SCALE).then_inc(g.l2_made, 1)
            for t in range(TB):
                act.wait_ge(g.dve_step, 5 * t + 2)
                nc.scalar.activation(st3[:, t % 2, 8:9], st3[:, t % 2, 7:8], ACT.Sqrt, bias=eps_ln)\
                  .then_inc(g.std_made, 1)
                act.wait_ge(g.dve_step, 5 * t + 4)
                nc.scalar.activation(z2[:, t % 2, :], bank[t % 2][:, :], ACT.Identity, scale=st3[:, t % 2, 9:10],
                                     bias=st3[:, t % 2, 10:11]).then_inc(g.z_made, 1)

        @block.vector
        def _(dve):
            for t in range(TB + 5):
                if t < TB:
                    dve.wait_ge(x_in[t], 16)
                    nc.vector.bn_stats(st1[:, t, 0:6], xa[:, t, :]).then_inc(f.stats_made_raw, 1)
                    dve.wait_ge(f.stats_made_raw, t + 1)
                    nc.vector.bn_aggr(st1[:, t, 6:8], st1[:, t, 0:6]).then_inc(f.stats_made, 1)
                if 0 <= t - 1 < TB:
                    u = t - 1
                    dve.wait_ge(f.std_made, u + 1)
                    nc.vector.reciprocal(st1[:, u, 9:10], st1[:, u, 8:9]).then_inc(f.rstd_made, 1)
                    dve.wait_ge(f.rstd_made, u + 1)
                    nc.vector.tensor_scalar(xn[:, u, :], xa[:, u, :], st1[:, u, 6:7], st1[:, u, 9:10],
                                            ALU.subtract, ALU.mult).then_inc(f.xn_made, 1)
                if t == 1:
                    dve.wait_ge(f.wa_hi_made, 1)
                    nc.vector.tensor_tensor(wa_lo[:, :, :], wa[:, :, :], wa_hi[:, :, :].bitcast(F32), ALU.subtract)\
                      .then_inc(f.wa_split, 1)
                if 0 <= t - 2 < TB:
                    u = t - 2
                    dve.wait_ge(f.xt_hi_made, u + 1)
                    nc.vector.tensor_tensor(xt_lo[:, u % 4, :, :], bank[u % 2][:, :].rearrange("p (c n) -> p c n", c=DC),
                                            xt_hi[:, u % 4, :, :].bitcast(F32), ALU.subtract).then_inc(f.xt_split, 1)
                if 0 <= t - 3 < TB:
                    u = t - 3
                    lat, q = bank[2 + u % 3], u % QB
                    if u == 0:
                        dve.wait_ge(f.lnw_in, 16)
                        dve.wait_ge(f.kcs_in, 16)
                    dve.wait_ge(f.std_rms_made, u + 1)
                    nc.vector.reciprocal(st1[:, u, 14:16], st1[:, u, 12:14]).then_inc(f.rstd_rms_made, 1)
                    nc.vector.tensor_tensor(kra[:, u, :], lat[:, RQ + RKV:LAT], kcs[:, q, 0, :], ALU.mult)\
                      .then_inc(f.krot_parts, 1)
                    nc.vector.tensor_tensor(krb[:, u, 0:HR], lat[:, LAT - HR:LAT], kcs[:, q, 1, 0:HR], ALU.mult)\
                      .then_inc(f.krot_parts, 1)
                    nc.vector.tensor_tensor(krb[:, u, HR:ROPE], lat[:, RQ + RKV:LAT - HR], kcs[:, q, 1, HR:ROPE],
                                            ALU.mult).then_inc(f.krot_parts, 1)
                    dve.wait_ge(f.rstd_rms_made, u + 1)
                    rq, rc = st1[:, u, 14:15], st1[:, u, 15:16]
                    nc.vector.scalar_tensor_tensor(qn[:, u, 0:RQ], lat[:, 0:RQ], rq, lnw[:, 0:RQ], ALU.mult, ALU.mult)
                    nc.vector.scalar_tensor_tensor(qn[:, u, RQ:2 * P], lat[:, P:RQ], rq, lnw[:, P:RQ], ALU.mult, ALU.mult)\
                      .then_inc(f.qn_made, 1)
                    nc.vector.scalar_tensor_tensor(kvn[:, u, 0:RKV], lat[:, RQ:RQ + RKV], rc, lnw[:, RQ:RQ + RKV],
                                                   ALU.mult, ALU.mult)
                    dve.wait_ge(f.krot_parts, 3 * (u + 1))
                    nc.vector.tensor_tensor(kvn[:, u, RKV:P], kra[:, u, :], krb[:, u, :], ALU.add).then_inc(f.kvn_made, 1)
                if 0 <= t - 5 < TB:
                    u = t - 5
                    tq = bank[5 + u % 2]
                    dve.wait_ge(f.qk_hi_made, u + 1)
                    nc.vector.tensor_tensor(ql_lo[:, :, u * P:(u + 1) * P],
                                            tq[:, 0:2 * P].rearrange("p (c n) -> p c n", c=2),
                                            ql_hi[:, :, u * P:(u + 1) * P].bitcast(F32), ALU.subtract)
                    nc.vector.tensor_tensor(kt_lo[:, u * P:(u + 1) * P], tq[:, 2 * P:3 * P],
                                            kt_hi[:, u * P:(u + 1) * P].bitcast(F32), ALU.subtract)\
                      .then_inc(f.qk_split, 1)

            def weights_lo(w):
                dve.wait_ge(a.wq_hi_made, w + 1)
                pv = bank[XB][:, 0:4 * RKV].rearrange("p (k h n) -> p k h n", k=2, h=2)
                rv = sq[:, SQ_COLS - 4 * ROPE:SQ_COLS].rearrange("p (k h n) -> p k h n", k=2, h=2)
                for cols, src in ((slice(0, RKV), pv), (slice(RKV, P), rv)):
                    nc.vector.tensor_tensor(w1_lo[:, :, cols], src[:, 0], w1_hi[:, :, cols].bitcast(F32), ALU.subtract)
                    last = nc.vector.tensor_tensor(w2[64:P, :, cols], src[64:P, 1], w2[64:P, :, cols].bitcast(F32),
                                                   ALU.subtract)
                last.then_inc(a.wq_split, 1)

            def rotate_swapped(gi, h, first=False):
                dve.wait_ge(a.q_made, gi + 1)
                if not first:
                    dve.wait_ge(a.pe_added, gi - 1)
                G = bank[6 + h]
                nc.vector.tensor_tensor(qswp[64:96, h, :], G[96:128, :], sin1[96:128, :], ALU.mult)
                nc.vector.tensor_tensor(qswp[96:128, h, :], G[64:96, :], sin1[64:96, :], ALU.mult)

            def rotate_own(gi, h, first=False):
                if not first:
                    dve.wait_ge(a.qt_split, gi - 1)
                nc.vector.tensor_tensor(qrot[:, h, :], bank[6 + h][:, :], cos1, ALU.mult).then_inc(a.q_rotated, 1)

            def query_lo(gi, b, h):
                dve.wait_ge(a.qt_hi_made, gi + 1)
                nc.vector.tensor_tensor(qt_lo[:, b, h, :], qrot[:, h, :], qt_hi[:, b, h, :].bitcast(F32), ALU.subtract)\
                  .then_inc(a.qt_split, 1)

            def mask_and_max(U, k, first=False):
                n = P * (k % QB + 1)
                dve.wait_ge(a.s_made, U + 1)
                if not first:
                    dve.wait_ge(a.exp_made, U - 1)
                dve.sem_inc(a.s_seen, 1)
                nc.vector.tensor_tensor_reduce(out=ss[:, k % 2, 0:n], in0=bank[k % 2][:, 0:n], in1=mask[:, SEQ - n:SEQ],
                                               scale=-SCALE, scalar=3.4e38, op0=ALU.add, op1=ALU.min,
                                               accum_out=negmax[:, k % 8:k % 8 + 1]).then_inc(a.s_masked, 1)

            def invert(m, b, first=False):
                dve.wait_ge(a.exp_made, UNITS * (m + 1))
                if not first:
                    dve.wait_ge(a.rb_made, m)
                nc.vector.reciprocal(rinv, rsum[:, UNITS * b:UNITS * (b + 1)]).then_inc(a.rinv_made, 1)

            def scale_o(m, p, b):
                dve.wait_ge(a.r_moved, m + 1)
                dve.wait_ge(a.o_made, m + 1)
                nc.vector.tensor_tensor(ot[:, bass.ds(p, 1), b * SEQ:(b + 1) * SEQ].rearrange("p a n -> p (a n)"),
                                        bank[4][:, :], rsb[:, :], ALU.mult).then_inc(a.o_scaled, 1)

            def body(p, first=False, last=False):
                for k in range(PU):
                    n = k + 2
                    if n < PU or not last:
                        mask_and_max(PU * p + n, n % PU)
                    if k == 2 and not last:
                        weights_lo(p + 1)
                    b, r = (1, k) if k < UNITS else (0, k - UNITS)
                    gi = 4 * p + (2 if b else 4)
                    if b or not last:
                        if r in (0, 2):
                            rotate_swapped(gi + r // 2, r // 2)
                        if r in (1, 3):
                            rotate_own(gi + r // 2, r // 2)
                        if r in (4, 6):
                            query_lo(gi + r // 2 - 2, b, r // 2 - 2)
                    if k == 5 and not first:
                        scale_o(2 * p - 1, p - 1, 1)
                    if k == 13:
                        scale_o(2 * p, p, 0)
                    if k == 7:
                        invert(2 * p, 0, first)
                    if k == 15:
                        invert(2 * p + 1, 1)

            weights_lo(0)
            for h in range(2):
                rotate_swapped(h, h, first=True)
                rotate_own(h, h, first=True)
            for h in range(2):
                query_lo(h, 0, h)
            mask_and_max(0, 0, first=True)
            mask_and_max(1, 1, first=True)
            body(0, first=True)
            with nc.vector.Fori(1, PAIRS - 1) as p:
                body(p)
            body(PAIRS - 1, last=True)
            scale_o(2 * PAIRS - 1, PAIRS - 1, 1)

            def o_part(t, hh):
                dve.wait_ge(c.o_hi_made, 2 * t + hh + 1)
                nc.vector.tensor_tensor(o_lo[:, hh, :, :], ot[:, 8 * hh:8 * hh + 8, t * P:(t + 1) * P],
                                        o_hi[:, hh, :, :].bitcast(F32), ALU.subtract).then_inc(c.o_split, 1)

            steps = [0]

            def step(ins, sem):
                steps[0] += 1
                ins.then_inc(sem, 1)
                dve.wait_ge(sem, steps[0])

            def statistics(st, src, sem):
                step(nc.vector.bn_stats(st[:, 0:6], src), sem)
                step(nc.vector.bn_aggr(st[:, 6:8], st[:, 0:6]), sem)

            o_part(0, 0)
            for k in range(PAIRS // 2):
                dve.wait_ge(c.wv_hi_made, k + 1)
                nc.vector.tensor_tensor(wv_lo[:, 2 * k:2 * k + 2, :], wv_raw[:, k % 2, :, :],
                                        wv_hi[:, 2 * k:2 * k + 2, :].bitcast(F32), ALU.subtract).then_inc(c.wv_split, 1)
            for t in range(TB + 2):
                if t < TB:
                    o_part(t, 1)
                if 0 <= t - 2:
                    u = t - 2
                    dve.wait_ge(c.lp_hi_made, u + 1)
                    for k, l in enumerate((lg, lu)):
                        last = nc.vector.scalar_tensor_tensor(l[64:96, u * P:(u + 1) * P], bank[4][64:96, 0:P],
                                                              cst[64:96, 3 * SEQ + k:3 * SEQ + k + 1],
                                                              l[64:96, u * P:(u + 1) * P].bitcast(F32),
                                                              ALU.mult, ALU.subtract)
                    last.then_inc(c.lp_split, 1)
                if 0 <= t - 1 < TB:
                    u = t - 1
                    dve.wait_ge(c.y_made, u + 1)
                    statistics(st2, bank[u % 2][:, :], c.dve_step)
                    dve.wait_ge(c.std1_made, u + 1)
                    step(nc.vector.reciprocal(st2[:, 9:10], st2[:, 8:9]), c.dve_step)
                    step(nc.vector.tensor_scalar(st2[:, 10:11], st2[:, 6:7], st2[:, 9:10], -1.0, ALU.mult, ALU.mult),
                         c.dve_step)
                    dve.wait_ge(c.z_made, u + 1)
                    if u == 0:
                        dve.wait_ge(c.x1_in, 16)
                    step(nc.vector.tensor_tensor(x1[:, u, :], x1[:, u, :], zt[:, :], ALU.add), c.dve_step)
                    statistics(st2, x1[:, u, :], c.dve_step)
                    dve.wait_ge(c.std2_made, u + 1)
                    step(nc.vector.reciprocal(st2[:, 9:10], st2[:, 8:9]), c.dve_step)
                    if u:
                        dve.wait_ge(c.y_turned, u)
                    nc.vector.tensor_scalar(xn2[:, :], x1[:, u, :], st2[:, 6:7], st2[:, 9:10],
                                            ALU.subtract, ALU.mult).then_inc(c.act_step, 1)
                    dve.wait_ge(c.act_step, u + 1)
                    nc.vector.tensor_reduce(fold[:, :], xn2[:, :].rearrange("p (c n) -> p n c", c=DC), AX.X, ALU.add)\
                      .then_inc(c.fold_made, 1)
                if t + 1 < TB:
                    o_part(t + 1, 0)

            dve.wait_ge(g.xf_hi_made, 1)
            nc.vector.tensor_tensor(xf_lo[:, :], xft[:, :], xf_hi[:, :].bitcast(F32), ALU.subtract).then_inc(g.xf_split, 1)
            for k in range(2):
                dve.wait_ge(g.w_hi_made, k + 1)
                nc.vector.tensor_tensor(w13_lo[:, k, :], w13[:, k, :], w13_hi[:, k, :].bitcast(F32), ALU.subtract)\
                  .then_inc(g.w_split, 1)
            dve.wait_ge(g.bs_hi_made, 1)
            nc.vector.tensor_tensor(bs_s[32:64, :], bs[32:64, :], bs_s[32:64, :].bitcast(F32), ALU.subtract)\
              .then_inc(g.bs_split, 1)

            def down_lo(hf, r):
                n = RROWS[r]
                dve.wait_ge(g.fs_hi_made, 3 * hf + r + 1)
                nc.vector.tensor_tensor(fs_lo[0:n, hf, r, :], fs[0:n, hf, r, :], fs_hi[0:n, hf, r, :].bitcast(F32),
                                        ALU.subtract).then_inc(g.fs_split, 1)

            for hf in range(2):
                for n in range(12):
                    G, rows = 12 * hf + n, RROWS[n // FOLD]
                    dve.wait_ge(g.silu_made, G + 1)
                    dve.wait_ge(g.up_made, G + 1)
                    if G >= 8:
                        dve.wait_ge(g.la_made, G // 4 - 1)
                        dve.wait_ge(g.fold_added, 3 * (G // 4 - 1))
                    nc.vector.tensor_tensor(gu[0:rows, G % 8, :], bank[(7, 2)[G % 2]][0:rows, :], sg[0:rows, G % 2, :],
                                            ALU.mult).then_inc(g.gu_made, 1)
                    if G == 4:
                        dve.wait_ge(g.wd_hi_made, 1)
                        nc.vector.tensor_tensor(wd_lo[:, :, :], wd[:, :, :], wd_hi[:, :, :].bitcast(F32), ALU.subtract)\
                          .then_inc(g.wd_split, 1)
                    if n in (8,):
                        down_lo(hf, 0)
                down_lo(hf, 1)
                down_lo(hf, 2)
            steps[0] = 0
            for t in range(TB):
                st = st3[:, t % 2, :]
                dve.wait_ge(g.y_made, t + 1)
                statistics(st, bank[t % 2][:, :], g.dve_step)
                dve.wait_ge(g.std_made, t + 1)
                step(nc.vector.reciprocal(st[:, 9:10], st[:, 8:9]), g.dve_step)
                step(nc.vector.tensor_scalar(st[:, 10:11], st[:, 6:7], st[:, 9:10], -1.0, ALU.mult, ALU.mult), g.dve_step)
                dve.wait_ge(g.z_made, t + 1)
                if t >= 2:
                    dve.wait_ge(g.out_sent, 16 * (t - 1))
                nc.vector.tensor_tensor(yo[:, t % 2, :], x1[:, t, :], z2[:, t % 2, :], ALU.add).then_inc(g.out_made, 1)
                step(nc.vector.memset(st[:, 15:16], 0.0), g.dve_step)

        @block.tensor
        def _(pe):
            def three(out, w_hi, w_lo, x_hi, x_lo, start, stop):
                nc.tensor.matmul(out, w_hi, x_hi, start=start, stop=False)
                nc.tensor.matmul(out, w_hi, x_lo, start=False, stop=False)
                return nc.tensor.matmul(out, w_lo, x_hi, start=False, stop=stop)

            pe.wait_ge(f.ident_made, 1)
            for t in range(TB + 4):
                if 0 <= t - 1 < TB:
                    u = t - 1
                    pe.wait_ge(f.xn_made, u + 1)
                    if u >= 2:
                        pe.wait_ge(f.xt_split, u - 1)
                    for k in range(DC):
                        last = nc.tensor.transpose(bank[u % 2][:, k * P:(k + 1) * P], xn[:, u, k * P:(k + 1) * P],
                                                   ident[:, :])
                    last.then_inc(f.x_turned, 1)
                if 0 <= t - 2 < TB:
                    u = t - 2
                    pe.wait_ge(f.wa_split, 1)
                    pe.wait_ge(f.xt_split, u + 1)
                    if u >= 3:
                        pe.wait_ge(f.kvn_made, u - 2)
                    for k in range(DC):
                        last = three(bank[2 + u % 3][:, 0:LAT], xt_hi[:, u % 4, k, :], xt_lo[:, u % 4, k, :],
                                     wa_hi[:, k, :], wa_lo[:, k, :], k == 0, k == DC - 1)
                    last.then_inc(f.lat_made, 1)
                if 0 <= t - 4 < TB:
                    u = t - 4
                    tq = bank[5 + u % 2]
                    pe.wait_ge(f.qn_made, u + 1)
                    pe.wait_ge(f.kvn_made, u + 1)
                    if u >= 2:
                        pe.wait_ge(f.qk_split, u - 1)
                    nc.tensor.transpose(tq[:, 0:P], qn[:, u, 0:P], ident[:, :])
                    nc.tensor.transpose(tq[:, P:2 * P], qn[:, u, P:2 * P], ident[:, :])
                    nc.tensor.transpose(tq[:, 2 * P:3 * P], kvn[:, u, :], ident[:, :]).then_inc(f.qk_turned, 1)

            def absorb_query(w):
                pe.wait_ge(a.sq_in, 16 * (w + 1))
                for k in range(2):
                    for h in range(2):
                        last = nc.tensor.matmul(bank[XB][:, (2 * k + h) * RKV:(2 * k + h + 1) * RKV],
                                                sq[:, (2 * h + k) * P:(2 * h + k + 1) * P],
                                                sq[:, 4 * P + h * RKV:4 * P + (h + 1) * RKV], start=True, stop=True)
                last.then_inc(a.wq_made, 1)

            def query(gi, b, h, w=None, first=False):
                if w is not None:
                    pe.wait_ge(a.wq_split, w + 1)
                if not first:
                    pe.wait_ge(a.q_rotated, gi - 1)
                out, tok = bank[6 + h][:, :], slice(b * SEQ, (b + 1) * SEQ)
                three(out, w1_hi[:, h, :], w1_lo[:, h, :], ql_hi[:, 0, tok], ql_lo[:, 0, tok], True, False)
                nc.tensor.matmul(out, w2[:, h, :], ql_hi[:, 1, tok], start=False, stop=False)
                nc.tensor.matmul(out, w2[:, h, :], ql_lo[:, 1, tok], start=False, stop=True).then_inc(a.q_made, 1)

            def scores(U, k, gi, first=False):
                i, h, b = k % QB, k // QB % 2, k // UNITS
                if i == 0:
                    pe.wait_ge(a.qt_split, gi + 1)
                if not first:
                    pe.wait_ge(a.s_masked, U - 1)
                keys = slice(b * SEQ, b * SEQ + (i + 1) * P)
                three(bank[k % 2][:, 0:(i + 1) * P], qt_hi[:, b, h, i * P:(i + 1) * P], qt_lo[:, b, h, i * P:(i + 1) * P],
                      kt_hi[:, keys], kt_lo[:, keys], True, True).then_inc(a.s_made, 1)

            def turn_p(U, k, first=False):
                pe.wait_ge(a.exp_made, U + 1)
                if not first:
                    pe.wait_ge(a.p_moved, U - 1)
                for j in range(k % QB + 1):
                    last = nc.tensor.transpose(bank[2 + k % 2][:, j * P:(j + 1) * P], pr[:, k % 4, j * P:(j + 1) * P],
                                               ident[:, :])
                last.then_inc(a.p_turned, 1)

            def output(m, b, js, first=False):
                if 0 in js:
                    pe.wait_ge(a.p_moved, UNITS * (m + 1))
                    if not first:
                        pe.wait_ge(a.o_scaled, m)
                for j in js:
                    for h in range(2):
                        last = nc.tensor.matmul(bank[4][RKV * h:RKV * (h + 1), j * P:SEQ], kvn[:, QB * b + j, 0:RKV],
                                                pt[:, b, h, j, j * P:SEQ], start=(j == 0), stop=(j == QB - 1),
                                                skip_group_check=True)
                if QB - 1 in js:
                    last.then_inc(a.o_made, 1)

            def turn_r(m):
                pe.wait_ge(a.rb_made, m + 1)
                for i in range(QB):
                    last = nc.tensor.transpose(bank[XB][:, i * P:(i + 1) * P], rb[:, i, :, :].rearrange("p h n -> p (h n)"),
                                               ident[:, :])
                last.then_inc(a.r_made, 1)

            def absorb_output(p):
                pe.wait_ge(a.sv_in, 16 * (p + 1))
                for h in range(2):
                    last = nc.tensor.matmul(bank[XB][RKV * h:RKV * (h + 1), :], sv[:, h * RKV:(h + 1) * RKV],
                                            sv[:, 2 * RKV + h * D:2 * RKV + (h + 1) * D], start=True, stop=True)
                last.then_inc(a.wvo_made, 1)

            def body(p, first=False, last=False):
                for k in range(PU):
                    n = k + 2
                    if n < PU:
                        scores(PU * p + n, n, 4 * p + n // QB)
                    elif not last:
                        scores(PU * p + n, n - PU, 4 * p + 4)
                    if k == 0 and not last:
                        if not first:
                            pe.wait_ge(a.r_moved, 2 * p - 1)
                        absorb_query(p + 1)
                    if k == 1 and not first:
                        output(2 * p - 1, 1, [0])
                    if k == 2 and not first:
                        output(2 * p - 1, 1, [1, 2, 3])
                    if k == 3 and not first:
                        if last:
                            pe.wait_ge(a.r_moved, 2 * p - 1)
                        else:
                            pe.wait_ge(a.wq_split, p + 2)
                        turn_r(2 * p - 1)
                    if k == 5:
                        if first:
                            pe.wait_ge(a.wq_split, p + 2)
                        else:
                            pe.wait_ge(a.r_moved, 2 * p)
                        absorb_output(p)
                    if k in (6, 7) and not last:
                        query(4 * p + 4 + k - 6, 0, k - 6, p + 1)
                    if k == 9:
                        output(2 * p, 0, [0], first)
                    if k == 10:
                        output(2 * p, 0, [1, 2, 3])
                    if k == 11:
                        pe.wait_ge(a.wvo_moved, p + 1)
                        turn_r(2 * p)
                    if k in (14, 15) and not last:
                        query(4 * p + 6 + k - 14, 1, k - 14)
                    turn_p(PU * p + k, k, first and k < 2)

            pe.wait_ge(f.qk_split, TB)
            absorb_query(0)
            for h in range(2):
                query(h, 0, h, 0 if h == 0 else None, first=True)
            for h in range(2):
                query(2 + h, 1, h)
            scores(0, 0, 0, first=True)
            scores(1, 1, 0, first=True)
            body(0, first=True)
            with nc.tensor.Fori(1, PAIRS - 1) as p:
                body(p)
            body(PAIRS - 1, last=True)
            output(2 * PAIRS - 1, 1, [0, 1, 2, 3])
            pe.wait_ge(a.r_moved, 2 * PAIRS - 1)
            turn_r(2 * PAIRS - 1)

            def lora_latents(u):
                pe.wait_ge(c.xt2_moved, u + 1)
                if u:
                    pe.wait_ge(c.lp_split, u)
                else:
                    pe.wait_ge(c.a13_in, 16)
                for k in range(DC):
                    last = nc.tensor.matmul(bank[4][0:96, 0:P], a13[:, k, :], xn2t[:, k, :], start=(k == 0), stop=(k == DC - 1))
                last.then_inc(c.lp_made, 1)

            for t in range(TB + 1):
                for hh in range(2):
                    if t < TB:
                        pe.wait_ge(c.o_split, 2 * t + hh + 1)
                        if t >= 2 and hh == 0:
                            pe.wait_ge(c.z_made, t - 1)
                        for k in range(PAIRS // 2):
                            q = 8 * hh + k
                            if t == 0 and k % 2 == 0:
                                pe.wait_ge(c.wv_split, q // 2 + 1)
                            last = three(bank[t % 2][:, :], o_hi[:, hh, k, :], o_lo[:, hh, k, :], wv_hi[:, q, :],
                                         wv_lo[:, q, :], q == 0, q == PAIRS - 1)
                        last.then_inc(c.o_used, 1)
                        if hh:
                            pe.nop().then_inc(c.y_made, 1)
                    if hh == 0 and t >= 1:
                        u = t - 1
                        pe.wait_ge(c.fold_made, u + 1)
                        if u:
                            pe.wait_ge(c.xt2_moved, u)
                        for k in range(DC):
                            nc.tensor.transpose(bank[2][:, k * P:(k + 1) * P], xn2[:, k * P:(k + 1) * P], ident[:, :])
                        nc.tensor.transpose(bank[3][:, 0:P], fold[:, :], ident[:, :]).then_inc(c.y_turned, 1)
                if t >= 1:
                    lora_latents(t - 1)

            def gate_or_up(which, G, n, hf):
                r, k = n // FOLD, n % FOLD
                rows, j, tok = RROWS[r], k * W2C + r * P, slice(hf * SEQ, (hf + 1) * SEQ)
                out = bank[5 + G % 2 if which == 0 else (7, 2)[G % 2]][0:rows, :]
                three(out, w13_hi[:, which, j:j + rows], w13_lo[:, which, j:j + rows], xf_hi[:, tok], xf_lo[:, tok],
                      True, False)
                return nc.tensor.matmul(out, bs_s[:, j:j + rows], (lg, lu)[which][0:96, tok], start=False, stop=True)

            def lora_down(hf, r):
                G, rows = 12 * hf + 4 * r, RROWS[r]
                pe.wait_ge(g.gu_made, G + 4)
                if hf and r == 0:
                    pe.wait_ge(g.l2_made, 1)
                for k in range(FOLD):
                    last = nc.tensor.matmul(bank[3][32 * k:32 * k + 32, :], a2[0:rows, r, k, :], gu[0:rows, (G + k) % 8, :],
                                            start=(r == 0), stop=(r == RT - 1), tile_position=(0, 32 * k),
                                            skip_group_check=True)
                last.then_inc(g.la_made, 1)

            pe.wait_ge(g.xf_split, 1)
            pe.wait_ge(g.bs_split, 1)
            pe.wait_ge(c.lp_split, TB)
            pe.wait_ge(g.a2_in, 16)
            for hf in range(2):
                for n in range(12):
                    G = 12 * hf + n
                    if G < 1:
                        pe.wait_ge(g.w_split, 2)
                    if G >= 2:
                        pe.wait_ge(g.silu_made, G - 1)
                    gate_or_up(0, G, n, hf).then_inc(g.gate_made, 1)
                    if G >= 2:
                        pe.wait_ge(g.gu_made, G - 1)
                    gate_or_up(1, G, n, hf).then_inc(g.up_made, 1)
                    if n in (5, 9):
                        lora_down(hf, n // FOLD - 1)
                lora_down(hf, RT - 1)
            pe.wait_ge(g.wd_split, 1)
            pe.wait_ge(g.b2_in, 16)
            for t in range(TB):
                hf, q = t // QB, t % QB * P
                pe.wait_ge(g.fs_split, 3 * (hf + 1))
                pe.wait_ge(g.l2_made, hf + 1)
                if t >= 2:
                    pe.wait_ge(g.z_made, t - 1)
                for r in range(RT):
                    n = RROWS[r]
                    three(bank[t % 2][:, :], fs_hi[0:n, hf, r, q:q + P], fs_lo[0:n, hf, r, q:q + P], wd_hi[0:n, r, :],
                          wd_lo[0:n, r, :], r == 0, False)
                nc.tensor.matmul(bank[t % 2][:, :], l2[:, hf, q:q + P], b2[:, :], start=False, stop=True)\
                  .then_inc(g.y_made, 1)


def kernel(**inputs):
    import concourse.bacc as bacc
    from concourse.bass_utils import run_bass_kernel_spmd

    I = {k.removeprefix("L0_"): np.asarray(v) for k, v in inputs.items()}
    x = I["attn_hidden_states"]
    f32 = np.float32
    evens_odds = np.r_[0:ROPE:2, 1:ROPE:2]

    def put(shape, *parts):
        a = np.zeros(shape, f32)
        for at, v in parts:
            a[at] = v
        return a

    wkv_a = np.concatenate([I["attn_Wkv_a"][:, :RKV], I["attn_Wkv_a"][:, RKV:][:, evens_odds]], 1)
    wa = np.concatenate([I["attn_Wq_a"], wkv_a], 1).reshape(DC, P, LAT).transpose(1, 0, 2)
    lnw = np.broadcast_to(np.concatenate([I["attn_q_a_ln_w"], I["attn_kv_a_ln_w"]]), (P, RQ + RKV))

    inv = (1.0 / f32(10000.0) ** (np.arange(0, ROPE, 2, dtype=f32) / f32(ROPE))).astype(f32)
    ang = np.outer(np.arange(SEQ, dtype=f32), inv).astype(f32)
    cos, sin = np.cos(ang).astype(f32), np.sin(ang).astype(f32)
    cst = np.zeros((P, 3 * SEQ + 8), f32)
    cst[:, SEQ - P:SEQ] = np.where(np.arange(P)[None, :] > np.arange(P)[:, None], f32(-BIG), f32(0))
    cst[:64, SEQ:2 * SEQ] = 1
    cst[64:, SEQ:2 * SEQ] = np.concatenate([cos.T, cos.T])
    cst[64:96, 2 * SEQ:3 * SEQ] = sin.T
    cst[96:128, 2 * SEQ:3 * SEQ] = -sin.T
    for g in range(3):
        cst[32 * g:32 * g + 2, 3 * SEQ] = LORA_SCALE
        cst[32 * g + 2:32 * g + 4, 3 * SEQ + 1] = LORA_SCALE
    cst[:, 3 * SEQ + 2] = LN_EPS
    cst[:, 3 * SEQ + 3] = RMS_EPS
    kcs = np.concatenate([cos, cos, -sin, sin], 1).reshape(QB, P, 2, ROPE).transpose(1, 0, 2, 3)

    wq = I["attn_Wq_b"].reshape(RQ, H, NOPE + ROPE)
    wkv = I["attn_Wkv_b"].reshape(RKV, H, NOPE + VD)
    qT = wq[:, :, :NOPE].transpose(1, 2, 0)
    qT = np.concatenate([qT, qT[:, :, P:]], 2).reshape(PAIRS, 2, NOPE, 2 * P).transpose(0, 2, 1, 3)
    kT = wkv[:, :, :NOPE].transpose(1, 2, 0).reshape(PAIRS, 2, NOPE, RKV).transpose(0, 2, 1, 3)
    pe = wq[:, :, NOPE:][:, :, evens_odds].reshape(RQ, PAIRS, 2, ROPE).transpose(1, 0, 2, 3)
    sq = np.concatenate([qT.reshape(PAIRS, P, -1), kT.reshape(PAIRS, P, -1), pe[:, :P].reshape(PAIRS, P, -1),
                         np.concatenate([pe[:, P:], pe[:, P:]], 1).reshape(PAIRS, P, -1)], 2)
    vT = wkv[:, :, NOPE:].transpose(1, 2, 0).reshape(PAIRS, 2, VD, RKV).transpose(0, 2, 1, 3)
    wo = I["attn_Wo"].reshape(PAIRS, 2, VD, D).transpose(0, 2, 1, 3)
    sv = np.concatenate([vT.reshape(PAIRS, P, -1), wo.reshape(PAIRS, P, -1)], 2)

    w13 = np.stack([I["ffn_w1q"].T, I["ffn_w3q"].T], 1)
    bs = put((96, HID), *[(slice(32 * g + 2 * k, 32 * g + 2 * k + 2), I[n].T)
                          for g in range(3) for k, n in enumerate(("ffn_b1", "ffn_b3"))])
    a13 = put((P, DC, 96), *[((slice(None), slice(None), slice(32 * g + 2 * k, 32 * g + 2 * k + 2)),
                              I[n].reshape(RANK, DC, P).transpose(2, 1, 0))
                             for g in range(3) for k, n in enumerate(("ffn_a1", "ffn_a3"))])
    a2r = I["ffn_a2"].reshape(RANK, FOLD, W2C)
    a2 = put((P, RT, FOLD, 32), *[((slice(0, RROWS[r]), r, slice(None), slice(0, RANK)),
                                   a2r[:, :, r * P:r * P + RROWS[r]].transpose(2, 1, 0)) for r in range(RT)])
    w2 = put((P, RT, D), *[((slice(0, RROWS[r]), r), I["ffn_w2q"].T[r * P:r * P + RROWS[r]]) for r in range(RT)])
    b2 = put((P, D), *[(slice(32 * k, 32 * k + RANK), I["ffn_b2"].T) for k in range(FOLD)])

    nc = bacc.Bacc("TRN2", target_bir_lowering=False, num_devices=1)
    arrays = dict(x=x, wa=wa, lnw=lnw, cst=cst, kcs=kcs, sq=sq, sv=sv, w13=w13, bs=bs, a13=a13, a2=a2, w2=w2, b2=b2)
    arrays = {k: np.ascontiguousarray(v) for k, v in arrays.items()}
    args = [nc.dram_tensor(k, v.shape, F32, kind="ExternalInput").ap() for k, v in arrays.items()]
    out = nc.dram_tensor("out", x.shape, F32, kind="ExternalOutput").ap()
    build(nc, *args, out)
    r = run_bass_kernel_spmd(nc, [arrays], core_ids=[0])
    return r.results[0]["out"]
```

```python
import concourse.bass as bass
from concourse import mybir
import numpy as np

F32 = mybir.dt.float32
F32R = mybir.dt.float32r
ALU = mybir.AluOpType
ACT = mybir.ActivationFunctionType
AX = mybir.AxisListType

P = 128
BATCH, SEQ, D = 2, 512, 512
TOK = BATCH * SEQ
TB = TOK // P
QB = SEQ // P
DC = D // P
H, PAIRS = 32, 16
RQ, RKV = 192, 64
NOPE, ROPE, VD = 128, 64, 128
HR = ROPE // 2
LAT = RQ + RKV + ROPE
SCALE = float(NOPE + ROPE) ** -0.5
LN_EPS, RMS_EPS = 1e-5, 1e-6
BIG = 3.0e38
XB = 5
UNITS = 2 * QB
PU = BATCH * UNITS
HID, RANK = 1376, 2
FOLD = 4
W2C = HID // FOLD
RT = (W2C + P - 1) // P
RROWS = [min(P, W2C - P * r) for r in range(RT)]
SQ_COLS = 2 * 2 * P + 2 * RKV + 2 * 2 * ROPE
SV_COLS = 2 * RKV + 2 * D
LORA_SCALE = 0.5
CST_BYTES = 4 * (3 * SEQ + 8)


class Semaphores(dict):

    __getattr__ = dict.__getitem__


class Map:

    def __init__(self, nc, start, end):
        self.nc, self.at, self.end = nc, start, end

    def take(self, name, shape, dt=F32):
        t = self.nc.alloc_sbuf_tensor_at(name, shape, dt, offset=self.at)
        self.at += (4 * int(np.prod(shape[1:])) + 31) // 32 * 32
        assert self.at <= self.end, (name, self.at, self.end)
        return t


def build(nc, x_d, wa_d, lnw_d, cst_d, kcs_d, sq_d, sv_d, w13_d, bs_d, a13_d, a2_d, w2_d, b2_d, out_d):
    wvo_d = nc.dram_tensor("wvo_scratch", [PAIRS, P, D], F32, kind="Internal").ap()
    top = nc.sbuf_usable_end // 32 * 32
    start = (nc.sbuf_base + 63) // 64 * 64

    keep = Map(nc, start, top)
    ident = keep.take("ident", [P, P])
    keep_eps = keep.take("eps", [P, 8])
    cst = keep.take("cst", [P, 3 * SEQ + 8])
    ot = keep.take("ot", [P, TB, PAIRS, P])
    late = keep.at
    mask = cst[:, 0:SEQ]
    cos1 = cst[:, SEQ:2 * SEQ]
    sin1 = cst[:, 2 * SEQ:3 * SEQ]
    eps = keep_eps
    eps_ln, eps_rms = eps[:, 0:1], eps[:, 1:2]

    att = Map(nc, late, top)
    ql_hi = att.take("ql_hi", [P, 2, TOK], F32R)
    ql_lo = att.take("ql_lo", [P, 2, TOK], F32R)
    sq = att.take("sq", [P, SQ_COLS])
    w1_hi = att.take("w1_hi", [P, 2, P], F32R)
    w1_lo = att.take("w1_lo", [P, 2, P], F32R)
    w2 = att.take("w2", [P, 2, P], F32R)
    kt_hi = att.take("kt_hi", [P, TOK], F32R)
    kt_lo = att.take("kt_lo", [P, TOK], F32R)
    kvn = att.take("kvn", [P, TB, P])
    sv = att.take("sv", [P, SV_COLS])
    qt_hi = att.take("qt_hi", [P, BATCH, 2, SEQ], F32R)
    qt_lo = att.take("qt_lo", [P, BATCH, 2, SEQ], F32R)
    small = att.take("small", [P, 64])
    early_end = att.at
    qrot = att.take("qrot", [P, 2, SEQ])
    qswp = att.take("qswp", [P, 2, SEQ])
    ss = att.take("ss", [P, 2, SEQ])
    pr = att.take("pr", [P, 4, SEQ])
    rb = att.take("rb", [P, QB, 2, RKV])
    rsb = att.take("rsb", [P, SEQ])
    vs = att.take("vs", [P, D])
    pt = att.take("pt", [P, 2, 2, QB, SEQ])
    negmax = small[:, 0:8]
    rsum = small[:, 8:24]
    rinv = small[:, 24:32]

    fir = Map(nc, start + 4 * P + 32 + CST_BYTES, late)
    xa = fir.take("xa", [P, TB, D])
    xn = fir.take("xn", [P, TB, D])
    xt_hi = fir.take("xt_hi", [P, 4, DC, P], F32R)
    xt_lo = fir.take("xt_lo", [P, 4, DC, P], F32R)
    qn = fir.take("qn", [P, TB, 2 * P])
    fi2 = Map(nc, early_end, top)
    wa = fi2.take("wa", [P, DC, LAT])
    wa_hi = fi2.take("wa_hi", [P, DC, LAT], F32R)
    wa_lo = fi2.take("wa_lo", [P, DC, LAT], F32R)
    lnw = fi2.take("lnw", [P, RQ + RKV])
    kcs = fi2.take("kcs", [P, QB, 2, ROPE])
    kra = fi2.take("kra", [P, TB, ROPE])
    krb = fi2.take("krb", [P, TB, ROPE])
    sqj = fi2.take("sqj", [P, 2, RQ])
    st1 = fi2.take("st1", [P, TB, 16])

    pro = Map(nc, late, top - 4 * 2 * PAIRS * D)
    wv_raw = pro.take("wv_raw", [P, 3, 2, D])
    o_s = pro.take("o_s", [P, 2, 2, PAIRS // 2, P], F32R)
    x1 = pro.take("x1", [P, TB, D])
    xn2 = pro.take("xn2", [P, D])
    fold = pro.take("fold", [P, P])
    xn2t = pro.take("xn2t", [P, DC, P])
    xft = pro.take("xft", [P, TOK])
    a13 = pro.take("a13", [P, DC, 96])
    lg = pro.take("lg", [P, TOK], F32R)
    lu = pro.take("lu", [P, TOK], F32R)
    w13 = pro.take("w13", [P, 2, HID])
    st2 = pro.take("st2", [P, 16])
    wv = Map(nc, top - 4 * 2 * PAIRS * D, top).take("wv", [P, PAIRS, 2, D], F32R)
    bs = nc.alloc_sbuf_tensor_at("bs", [96, HID], F32, offset=start + 4 * P + 32)

    ffn = Map(nc, start + 4 * P + 32 + CST_BYTES, late)
    w13_hi = ffn.take("w13_hi", [P, 2, HID], F32R)
    w13_lo = ffn.take("w13_lo", [P, 2, HID], F32R)
    bs_s = ffn.take("bs_s", [96, HID], F32R)
    xf_hi = ffn.take("xf_hi", [P, TOK], F32R)
    xf_lo = ffn.take("xf_lo", [P, TOK], F32R)
    b2 = ffn.take("b2", [P, D])
    a2 = ffn.take("a2", [P, RT, FOLD, 32])
    l2 = ffn.take("l2", [P, 2, SEQ])
    sg = ffn.take("sg", [P, 2, SEQ])
    ff2 = Map(nc, top - 4 * 2 * PAIRS * D, top)
    gu = ff2.take("gu", [P, 8, SEQ])
    fs = ff2.take("fs", [P, 2, RT, SEQ])
    fs_hi = ff2.take("fs_hi", [P, 2, RT, SEQ], F32R)
    fs_lo = ff2.take("fs_lo", [P, 2, RT, SEQ], F32R)
    ff3 = Map(nc, late, late + 28 * 1024)
    wd = ff3.take("wd", [P, RT, D])
    wd_hi = ff3.take("wd_hi", [P, RT, D], F32R)
    wd_lo = ff3.take("wd_lo", [P, RT, D], F32R)
    z2 = ff3.take("z2", [P, 2, D])
    yo = ff3.take("yo", [P, 2, D])
    st3 = ff3.take("st3", [P, 2, 16])

    bank = [nc.alloc_psum_tensor(f"bank{i}", [P, 512], F32) for i in range(8)]

    def sems(phase, words):
        return Semaphores((n, nc.alloc_semaphore(f"{phase}_{n}")) for n in words.split())

    f = sems("first", """eps_set table_set stats_made_raw ident_zero ident_made wa_in lnw_in cst_in kcs_in stats_made std_made rstd_made xn_made
        x_turned xt_hi_made xt_split wa_hi_made wa_split lat_made squares_summed std_rms_made rstd_rms_made
        qn_made krot_parts kvn_made qk_turned qk_hi_made qk_split""")
    x_in = [nc.alloc_semaphore(f"x_in{t}") for t in range(TB)]
    a = sems("attention", """s_seen rinv_seen sq_in sv_in wq_made wq_hi_made wq_split q_made q_rotated pe_added qt_hi_made qt_split
        s_made s_masked exp_made p_turned p_moved o_made rinv_made rb_made r_made r_moved o_scaled
        wvo_made wvo_moved wvo_out""")
    c = sems("projection", """rstd2_made xn2_made wv_in0 wv_in1 wv_in2 wv_hi_made wv_split o_hi_made o_split o_used y_made x1_in w13_in bs_in a13_in
        dve_step act_step std1_made z_made std2_made fold_made y_turned xt2_moved xf_moved lp_made lp_hi_made lp_split""")
    g = sems("forward", """wd_in b2_in a2_in w_hi_made w_split xf_hi_made xf_split bs_hi_made bs_split bs_fixed wd_hi_made wd_split
        gate_made up_made silu_made gu_made la_made fold_added fs_hi_made fs_split l2_made
        y_made std_made z_made dve_step out_made out_sent""")

    xb = x_d.rearrange("b (t p) d -> (b t) p d", p=P)
    ob = out_d.rearrange("b (t p) d -> (b t) p d", p=P)
    block = nc.Block()
    with block:
        @block.sync
        def _(sp):
            sp.dma_start(xa[:, 0, :], xb[0]).then_inc(x_in[0], 16)
            sp.dma_start(wa[:, :, :], wa_d).then_inc(f.wa_in, 16)
            for t in range(1, 4):
                sp.dma_start(xa[:, t, :], xb[t]).then_inc(x_in[t], 16)
            sp.dma_start(lnw[:, :], lnw_d).then_inc(f.lnw_in, 16)
            sp.dma_start(kcs[:, :, :, :], kcs_d).then_inc(f.kcs_in, 16)
            sp.dma_start(sq[:, :], sq_d[0]).then_inc(a.sq_in, 16)
            for t in range(4, TB):
                sp.dma_start(xa[:, t, :], xb[t]).then_inc(x_in[t], 16)
            sp.dma_start(cst[:, :], cst_d).then_inc(f.cst_in, 16)
            sp.dma_start(sv[:, :], sv_d[0]).then_inc(a.sv_in, 16)
            with nc.sync.Fori(0, PAIRS - 1) as p:
                sp.wait_ge(a.wq_split, p + 1)
                sp.dma_start(sq[:, :], sq_d[bass.ds(p + 1, 1)].rearrange("a p n -> p (a n)")).then_inc(a.sq_in, 16)
                sp.wait_ge(a.wvo_made, p + 1)
                sp.dma_start(sv[:, :], sv_d[bass.ds(p + 1, 1)].rearrange("a p n -> p (a n)")).then_inc(a.sv_in, 16)
                sp.wait_ge(a.wvo_moved, p + 1)
                sp.dma_start(wvo_d[bass.ds(p, 1)].rearrange("a p n -> p (a n)"), vs[:, :]).then_inc(a.wvo_out, 16)
            sp.wait_ge(a.q_made, 4 * PAIRS)
            for k in range(PAIRS // 2):
                if k == 3:
                    sp.wait_ge(a.wvo_moved, PAIRS)
                    sp.dma_start(wvo_d[PAIRS - 1], vs[:, :]).then_inc(a.wvo_out, 16)
                if k >= 3:
                    sp.wait_ge(c.wv_split, k - 2)
                if k == PAIRS // 2 - 1:
                    sp.wait_ge(a.wvo_out, 16 * PAIRS)
                sp.dma_start(wv_raw[:, k % 3, :, :], wvo_d[2 * k:2 * k + 2].rearrange("a p n -> p a n"))\
                  .then_inc((c.wv_in0, c.wv_in1, c.wv_in2)[k % 3], 16)
            sp.wait_ge(a.o_scaled, 2 * PAIRS)
            sp.dma_start(x1[:, :, :], xb.rearrange("t p d -> p t d")).then_inc(c.x1_in, 16)
            sp.dma_start(w13[:, :, :], w13_d).then_inc(c.w13_in, 16)
            sp.dma_start(a13[:, :, :], a13_d).then_inc(c.a13_in, 16)
            sp.dma_start(bs[:, :], bs_d).then_inc(c.bs_in, 16)
            sp.wait_ge(c.o_used, 2 * TB)
            sp.dma_start(a2[:, :, :, :], a2_d).then_inc(g.a2_in, 16)
            sp.dma_start(wd[:, :, :], w2_d).then_inc(g.wd_in, 16)
            sp.dma_start(b2[:, :], b2_d).then_inc(g.b2_in, 16)
            for t in range(TB):
                sp.wait_ge(g.out_made, t + 1)
                sp.dma_start(ob[t], yo[:, t % 2, :]).then_inc(g.out_sent, 16)
                if t + 1 < TB:
                    sp.wait_ge(g.out_sent, 16 * (t + 1))
            sp.wait_ge(g.out_sent, 16 * TB)

        @block.gpsimd
        def _(pool):
            nc.gpsimd.memset(ident[:, :], 0.0).then_inc(f.ident_zero, 1)
            pool.wait_ge(f.ident_zero, 1)
            nc.gpsimd.affine_select(out=ident[:, :], in_=ident[:, :], compare_op=ALU.not_equal, fill=1.0,
                                    base=0, pattern=[[-1, P]], channel_multiplier=1).then_inc(f.ident_made, 1)
            for t in range(TB):
                pool.wait_ge(f.rstd_made, t + 1)
                nc.gpsimd.tensor_scalar(xn[:, t, :], xa[:, t, :], st1[:, t, 6:7], st1[:, t, 9:10],
                                        ALU.subtract, ALU.mult).then_inc(f.xn_made, 1)
                if t == 0:
                    pool.wait_ge(f.wa_hi_made, 1)
                    nc.gpsimd.tensor_tensor(wa_lo[:, :, :], wa[:, :, :], wa_hi[:, :, :].bitcast(F32), ALU.subtract)\
                      .then_inc(f.wa_split, 1)

            def add_rotated(gi, h, spread_before=None):
                if spread_before is not None:
                    pool.wait_ge(a.rb_made, spread_before)
                pool.wait_ge(a.q_rotated, gi + 1)
                nc.gpsimd.tensor_tensor(qrot[RKV:P, h, :], qrot[RKV:P, h, :], qswp[RKV:P, h, :], ALU.add)\
                  .then_inc(a.pe_added, 1)

            def spread(m, added, first=False):
                pool.wait_ge(a.pe_added, added)
                pool.wait_ge(a.rinv_made, m + 1)
                if not first:
                    pool.wait_ge(a.r_made, m)
                pool.sem_inc(a.rinv_seen, 1)
                nc.gpsimd.tensor_copy(rb[:, :, :, :],
                                      rinv.rearrange("p (h i) -> p i h", h=2).unsqueeze(3).to_broadcast([P, QB, 2, RKV]))\
                  .then_inc(a.rb_made, 1)

            def body(p, first=False, last=False):
                for h in range(2):
                    add_rotated(4 * p + 2 + h, h, 2 * p if h == 0 and not first else None)
                spread(2 * p, 4 * p + 4, first)
                if not last:
                    for h in range(2):
                        add_rotated(4 * p + 4 + h, h, 2 * p + 1 if h == 0 else None)
                spread(2 * p + 1, 4 * p + (4 if last else 6))

            for h in range(2):
                add_rotated(h, h)
            body(0, first=True)
            with nc.gpsimd.Fori(1, PAIRS - 1) as p:
                body(p)
            body(PAIRS - 1, last=True)

            for hf in range(2):
                for r in range(RT):
                    n = RROWS[r]
                    for k in range(1, FOLD):
                        pool.wait_ge(g.gu_made, 12 * hf + 4 * r + k + 1)
                        if (hf, r, k) != (0, 0, 1):
                            pool.wait_ge(g.fold_added, 3 * (3 * hf + r) + k - 1)
                        at = lambda q: (12 * hf + 4 * r + q) % 8
                        nc.gpsimd.tensor_tensor(fs[0:n, hf, r, :], gu[0:n, at(0), :] if k == 1 else fs[0:n, hf, r, :],
                                                gu[0:n, at(k), :], ALU.add).then_inc(g.fold_added, 1)

        @block.scalar
        def _(act):
            def lat_view(t):
                return bank[2 + t % 2]

            def weights_hi(w, first=False):
                act.wait_ge(a.wq_made, w + 1)
                if not first:
                    act.wait_ge(a.q_made, 4 * w)
                pv = bank[XB][:, 0:4 * RKV].rearrange("p (k h n) -> p k h n", k=2, h=2)
                rv = sq[:, SQ_COLS - 4 * ROPE:SQ_COLS].rearrange("p (k h n) -> p k h n", k=2, h=2)
                nc.scalar.activation(w1_hi[:, :, 0:RKV], pv[:, 0], ACT.Copy)
                nc.scalar.activation(w1_hi[:, :, RKV:P], rv[:, 0], ACT.Copy)
                nc.scalar.activation(w2[:, :, 0:RKV], pv[:, 1], ACT.Copy)
                nc.scalar.activation(w2[:, :, RKV:P], rv[:, 1], ACT.Copy).then_inc(a.wq_hi_made, 1)

            def query_hi(gi, b, h, s_done=None):
                act.wait_ge(a.pe_added, gi + 1)
                if s_done is not None:
                    act.wait_ge(a.s_made, s_done)
                nc.scalar.activation(qt_hi[:, b, h, :], qrot[:, h, :], ACT.Copy).then_inc(a.qt_hi_made, 1)

            def exponent(U, k, s_first=False, old=None):
                n = P * (k % QB + 1)
                act.wait_ge(a.s_masked, U + 1)
                if not s_first:
                    act.wait_ge(a.p_turned, U - 3)
                if old is not None:
                    act.wait_ge(a.rinv_made, old)
                nc.scalar.activation(pr[:, k % 4, 0:n], ss[:, k % 2, 0:n], ACT.Exp, bias=negmax[:, k % 8:k % 8 + 1],
                                     scale=-1.0, accum_out=rsum[:, k:k + 1]).then_inc(a.exp_made, 1)

            def move_p(U, k, old=None):
                i, h, b = k % QB, k // QB % 2, k // UNITS
                act.wait_ge(a.p_turned, U + 1)
                if old is not None:
                    act.wait_ge(a.o_made, old)
                nc.scalar.activation(pt[:, b, h, 0:i + 1, i * P:(i + 1) * P],
                                     bank[2 + k % 2][:, 0:(i + 1) * P].rearrange("p (j q) -> p j q", q=P),
                                     ACT.Copy).then_inc(a.p_moved, 1)

            def move_r(m, first=False):
                act.wait_ge(a.r_made, m + 1)
                if not first:
                    act.wait_ge(a.o_scaled, m)
                nc.scalar.activation(rsb[:, :], bank[XB][:, :], ACT.Copy).then_inc(a.r_moved, 1)

            def split_weights(k):
                act.wait_ge((c.wv_in0, c.wv_in1, c.wv_in2)[k % 3], 16 * (k // 3 + 1))
                for q in (2 * k, 2 * k + 1):
                    last = nc.scalar.activation(wv[:, PAIRS - 1 - q, 0, :], wv_raw[:, k % 3, q % 2, :], ACT.Copy)
                last.then_inc(c.wv_hi_made, 1)

            def split_output(t, hh):
                if t:
                    act.wait_ge(c.o_used, 2 * t + hh - 1)
                if hh:
                    act.wait_ge(a.o_scaled, 2 * PAIRS - (1 if t < QB else 0))
                nc.scalar.activation(o_s[:, hh, 0, :, :], ot[:, t, 8 * hh:8 * hh + 8, :], ACT.Copy)\
                  .then_inc(c.o_hi_made, 1)

            def lora_hi(u):
                act.wait_ge(c.lp_made, u + 1)
                nc.scalar.activation(lg[0:96, u * P:(u + 1) * P], bank[4][0:96, 0:P], ACT.Copy,
                                     scale=cst[0:96, 3 * SEQ:3 * SEQ + 1])
                nc.scalar.activation(lu[0:96, u * P:(u + 1) * P], bank[4][0:96, 0:P], ACT.Copy,
                                     scale=cst[0:96, 3 * SEQ + 1:3 * SEQ + 2]).then_inc(c.lp_hi_made, 1)

            def body(p, first=False, last=False):
                for k in range(PU):
                    if last and k in (9, 10, 11):
                        split_weights(k - 9)
                    if last and k == 13:
                        split_output(0, 0)
                    move_p(PU * p + k, k, 2 * p - 1 + k // UNITS if k % UNITS == 0 and not first else None)
                    n = k + 2
                    if n < PU:
                        exponent(PU * p + n, n, first and n < 4, 2 * p if n == UNITS and not first else None)
                    elif not last:
                        exponent(PU * p + n, n - PU, False, 2 * p + 1 if n == PU else None)
                    if k == 1 and not last:
                        weights_hi(p + 1)
                    if k in (2, 4):
                        h = (k - 2) // 2
                        query_hi(4 * p + 2 + h, 1, h, None if first else PU * (p - 1) + UNITS + QB * (h + 1))
                    if k in (10, 12) and not last:
                        h = (k - 10) // 2
                        query_hi(4 * p + 4 + h, 0, h, PU * p + QB * (h + 1))
                    if k == 5 and not first:
                        move_r(2 * p - 1)
                    if k == 12:
                        move_r(2 * p, first)
                    if k == 9:
                        act.wait_ge(a.wvo_made, p + 1)
                        if not first:
                            act.wait_ge(a.wvo_out, 16 * p)
                        nc.scalar.activation(vs[:, :], bank[XB][:, :], ACT.Copy).then_inc(a.wvo_moved, 1)

            act.wait_ge(f.eps_set, 1)
            nc.scalar.activation(eps[:, 2:3], eps_ln, ACT.Sqrt).then_inc(f.table_set, 1)
            for t in range(TB + 4):
                if t < TB:
                    act.wait_ge(f.stats_made, t + 1)
                    nc.scalar.activation(st1[:, t, 8:9], st1[:, t, 7:8], ACT.Sqrt, bias=eps_ln).then_inc(f.std_made, 1)
                if t == 0:
                    act.wait_ge(f.wa_in, 16)
                    nc.scalar.activation(wa_hi[:, :, :], wa[:, :, :], ACT.Copy).then_inc(f.wa_hi_made, 1)
                if 0 <= t - 1 < TB:
                    u = t - 1
                    act.wait_ge(f.x_turned, u + 1)
                    if u >= 4:
                        act.wait_ge(f.lat_made, u - 3)
                    nc.scalar.activation(xt_hi[:, u % 4, :, :], bank[u % 2][:, :].rearrange("p (c n) -> p c n", c=DC),
                                         ACT.Copy).then_inc(f.xt_hi_made, 1)
                if 0 <= t - 2 < TB:
                    u = t - 2
                    act.wait_ge(f.lat_made, u + 1)
                    nc.scalar.activation(sqj[:, 0, :], lat_view(u)[:, 0:RQ], ACT.Square, scale=RQ ** -0.5,
                                         accum_out=st1[:, u, 10:11]).then_inc(f.squares_summed, 1)
                    nc.scalar.activation(sqj[:, 1, 0:RKV], lat_view(u)[:, RQ:RQ + RKV], ACT.Square, scale=RKV ** -0.5,
                                         accum_out=st1[:, u, 11:12]).then_inc(f.squares_summed, 1)
                    act.wait_ge(f.squares_summed, 2 * (u + 1))
                    nc.scalar.activation(st1[:, u, 12:14], st1[:, u, 10:12], ACT.Sqrt, bias=eps_rms)\
                      .then_inc(f.std_rms_made, 1)
                if 0 <= t - 4 < TB:
                    u = t - 4
                    tq = bank[4]
                    act.wait_ge(f.qk_turned, u + 1)
                    nc.scalar.activation(ql_hi[:, :, u * P:(u + 1) * P],
                                         tq[:, 0:2 * P].rearrange("p (c n) -> p c n", c=2), ACT.Copy)
                    nc.scalar.activation(kt_hi[:, u * P:(u + 1) * P], tq[:, 2 * P:3 * P], ACT.Copy)\
                      .then_inc(f.qk_hi_made, 1)
                if t == 4:
                    weights_hi(0, first=True)
                if t == TB + 3:
                    query_hi(0, 0, 0)

            query_hi(1, 0, 1)
            exponent(0, 0, True)
            exponent(1, 1, True)
            body(0, first=True)
            with nc.scalar.Fori(1, PAIRS - 1) as p:
                body(p)
            body(PAIRS - 1, last=True)
            act.wait_ge(a.o_made, 2 * PAIRS)
            split_weights(3)
            move_r(2 * PAIRS - 1)

            for k in range(4, PAIRS // 2):
                if k == PAIRS // 2 - 1:
                    act.wait_ge(a.o_scaled, 2 * PAIRS)
                split_weights(k)
            for t in range(TB + 2):
                if t < TB:
                    split_output(t, 1)
                if 0 <= t - 2:
                    u = t - 2
                    act.wait_ge(c.y_turned, u + 1)
                    if u:
                        act.wait_ge(c.lp_made, u)
                    nc.scalar.activation(xn2t[:, :, :], bank[2][:, :].rearrange("p (c n) -> p c n", c=DC), ACT.Copy)
                    nc.scalar.activation(xft[:, u * P:(u + 1) * P], bank[3][:, 0:P], ACT.Copy).then_inc(c.xt2_moved, 1)
                if 0 <= t - 1 < TB:
                    u = t - 1
                    act.wait_ge(c.dve_step, 7 * u + 2)
                    nc.scalar.activation(st2[:, 8:9], st2[:, 7:8], ACT.Sqrt, bias=eps_ln).then_inc(c.std1_made, 1)
                    act.wait_ge(c.dve_step, 7 * u + 4)
                    if u:
                        act.wait_ge(c.y_turned, u)
                    nc.scalar.activation(xn2[:, :], bank[u % 2][:, :], ACT.Identity, scale=st2[:, 9:10],
                                         bias=st2[:, 10:11]).then_inc(c.z_made, 1)
                    act.wait_ge(c.dve_step, 7 * u + 7)
                    nc.scalar.activation(st2[:, 8:9], st2[:, 7:8], ACT.Sqrt, bias=eps_ln).then_inc(c.std2_made, 1)
                if t + 1 < TB:
                    split_output(t + 1, 0)
                if 0 <= t - 3 < TB - 2:
                    lora_hi(t - 3)
                if t == 4:
                    act.wait_ge(c.o_used, 6)
                    act.wait_ge(c.o_split, 6)
                    act.wait_ge(c.w13_in, 16)
                if t in (4, 5):
                    nc.scalar.activation(w13_hi[:, t - 4, :], w13[:, t - 4, :], ACT.Copy).then_inc(g.w_hi_made, 1)
                if t == 6:
                    act.wait_ge(c.o_split, 10)
                    act.wait_ge(c.bs_in, 16)
                    nc.scalar.activation(bs_s[:, :], bs[:, :], ACT.Copy).then_inc(g.bs_hi_made, 1)
                    nc.scalar.activation(xf_hi[:, 0:SEQ], xft[:, 0:SEQ], ACT.Copy).then_inc(g.xf_hi_made, 1)

            lora_hi(TB - 2)
            def down_hi(hf, r):
                n = RROWS[r]
                act.wait_ge(g.fold_added, 3 * (3 * hf + r + 1))
                nc.scalar.activation(fs_hi[0:n, hf, r, :], fs[0:n, hf, r, :], ACT.Copy).then_inc(g.fs_hi_made, 1)

            for hf in range(2):
                for n in range(12):
                    G, rows = 12 * hf + n, RROWS[n // FOLD]
                    act.wait_ge(g.gate_made, G + 1)
                    if G >= 2:
                        act.wait_ge(g.gu_made, G - 1)
                    nc.scalar.activation(sg[0:rows, G % 2, :], bank[5 + G % 2][0:rows, :], ACT.Silu)\
                      .then_inc(g.silu_made, 1)
                    if G == 1:
                        lora_hi(TB - 1)
                        nc.scalar.activation(xf_hi[:, SEQ:TOK], xft[:, SEQ:TOK], ACT.Copy).then_inc(g.xf_hi_made, 1)
                    if G == 5:
                        act.wait_ge(g.wd_in, 16)
                        nc.scalar.activation(wd_hi[:, :, :], wd[:, :, :], ACT.Copy).then_inc(g.wd_hi_made, 1)
                    if n in (7, 11):
                        down_hi(hf, n // FOLD - 1)
                down_hi(hf, RT - 1)
                act.wait_ge(g.la_made, RT * (hf + 1))
                nc.scalar.activation(l2[:, hf, :], bank[3][:, :], ACT.Copy, scale=LORA_SCALE).then_inc(g.l2_made, 1)
            for t in range(TB):
                act.wait_ge(g.dve_step, 5 * t + 2)
                nc.scalar.activation(st3[:, t % 2, 8:9], st3[:, t % 2, 7:8], ACT.Sqrt, bias=eps_ln)\
                  .then_inc(g.std_made, 1)
                act.wait_ge(g.dve_step, 5 * t + 4)
                nc.scalar.activation(z2[:, t % 2, :], bank[t % 2][:, :], ACT.Identity, scale=st3[:, t % 2, 9:10],
                                     bias=st3[:, t % 2, 10:11]).then_inc(g.z_made, 1)

        @block.vector
        def _(dve):
            def weights_lo(w):
                dve.wait_ge(a.wq_hi_made, w + 1)
                pv = bank[XB][:, 0:4 * RKV].rearrange("p (k h n) -> p k h n", k=2, h=2)
                rv = sq[:, SQ_COLS - 4 * ROPE:SQ_COLS].rearrange("p (k h n) -> p k h n", k=2, h=2)
                for cols, src in ((slice(0, RKV), pv), (slice(RKV, P), rv)):
                    nc.vector.tensor_tensor(w1_lo[:, :, cols], src[:, 0], w1_hi[:, :, cols].bitcast(F32), ALU.subtract)
                    last = nc.vector.tensor_tensor(w2[64:P, :, cols], src[64:P, 1], w2[64:P, :, cols].bitcast(F32),
                                                   ALU.subtract)
                last.then_inc(a.wq_split, 1)

            def rotate_swapped(gi, h, first=False):
                dve.wait_ge(a.q_made, gi + 1)
                if not first:
                    dve.wait_ge(a.pe_added, gi - 1)
                G = bank[6 + h]
                nc.vector.tensor_tensor(qswp[64:96, h, :], G[96:128, :], sin1[96:128, :], ALU.mult)
                nc.vector.tensor_tensor(qswp[96:128, h, :], G[64:96, :], sin1[64:96, :], ALU.mult)

            def rotate_own(gi, h, first=False):
                if not first:
                    dve.wait_ge(a.qt_split, gi - 1)
                nc.vector.tensor_tensor(qrot[:, h, :], bank[6 + h][:, :], cos1, ALU.mult).then_inc(a.q_rotated, 1)

            def query_lo(gi, b, h):
                dve.wait_ge(a.qt_hi_made, gi + 1)
                nc.vector.tensor_tensor(qt_lo[:, b, h, :], qrot[:, h, :], qt_hi[:, b, h, :].bitcast(F32), ALU.subtract)\
                  .then_inc(a.qt_split, 1)

            def mask_and_max(U, k, first=False):
                n = P * (k % QB + 1)
                dve.wait_ge(a.s_made, U + 1)
                if not first:
                    dve.wait_ge(a.exp_made, U - 1)
                dve.sem_inc(a.s_seen, 1)
                nc.vector.tensor_tensor_reduce(out=ss[:, k % 2, 0:n], in0=bank[k % 2][:, 0:n], in1=mask[:, SEQ - n:SEQ],
                                               scale=-SCALE, scalar=3.4e38, op0=ALU.add, op1=ALU.min,
                                               accum_out=negmax[:, k % 8:k % 8 + 1]).then_inc(a.s_masked, 1)

            def invert(m, b, first=False):
                dve.wait_ge(a.exp_made, UNITS * (m + 1))
                if not first:
                    dve.wait_ge(a.rb_made, m)
                nc.vector.reciprocal(rinv, rsum[:, UNITS * b:UNITS * (b + 1)]).then_inc(a.rinv_made, 1)

            def scale_o(m, p, b):
                dve.wait_ge(a.r_moved, m + 1)
                dve.wait_ge(a.o_made, m + 1)
                nc.vector.tensor_tensor(ot[:, b * QB:(b + 1) * QB, bass.ds(p, 1), :].rearrange("p t a n -> p t (a n)"),
                                        bank[4][:, :].rearrange("p (t n) -> p t n", t=QB),
                                        rsb[:, :].rearrange("p (t n) -> p t n", t=QB), ALU.mult).then_inc(a.o_scaled, 1)

            def split_weights(k):
                dve.wait_ge(c.wv_hi_made, k + 1)
                for q in (2 * k, 2 * k + 1):
                    last = nc.vector.tensor_tensor(wv[:, PAIRS - 1 - q, 1, :], wv_raw[:, k % 3, q % 2, :],
                                                   wv[:, PAIRS - 1 - q, 0, :].bitcast(F32), ALU.subtract)
                last.then_inc(c.wv_split, 1)

            def split_output(t, hh):
                dve.wait_ge(c.o_hi_made, 2 * t + hh + 1)
                nc.vector.tensor_tensor(o_s[:, hh, 1, :, :], ot[:, t, 8 * hh:8 * hh + 8, :],
                                        o_s[:, hh, 0, :, :].bitcast(F32), ALU.subtract).then_inc(c.o_split, 1)

            def lora_lo(u):
                dve.wait_ge(c.lp_hi_made, u + 1)
                for k, l in enumerate((lg, lu)):
                    last = nc.vector.scalar_tensor_tensor(l[64:96, u * P:(u + 1) * P], bank[4][64:96, 0:P],
                                                          cst[64:96, 3 * SEQ + k:3 * SEQ + k + 1],
                                                          l[64:96, u * P:(u + 1) * P].bitcast(F32),
                                                          ALU.mult, ALU.subtract)
                last.then_inc(c.lp_split, 1)

            def body(p, first=False, last=False):
                for k in range(PU):
                    if last and k in (10, 11, 12):
                        split_weights(k - 10)
                    if last and k == 14:
                        split_output(0, 0)
                    n = k + 2
                    if n < PU or not last:
                        mask_and_max(PU * p + n, n % PU)
                    if k == 2 and not last:
                        weights_lo(p + 1)
                    b, r, gi = (1, k, 4 * p + 2) if k < UNITS else (0, k - UNITS, 4 * p + 4)
                    if k < UNITS or not last:
                        if r == 1:
                            rotate_swapped(gi + 1, 1)
                        if r in (0, 2):
                            rotate_own(gi + r // 2, r // 2)
                        if r in (3, 5):
                            query_lo(gi + r // 2 - 1, b, r // 2 - 1)
                        if r == 7 and not last:
                            rotate_swapped(gi + 2, 0)
                    if k == 6 and not first:
                        scale_o(2 * p - 1, p - 1, 1)
                    if k == 13:
                        scale_o(2 * p, p, 0)
                    if k == 7:
                        invert(2 * p, 0, first)
                    if k == 15:
                        invert(2 * p + 1, 1)

            nc.vector.memset(eps_ln, LN_EPS)
            nc.vector.memset(eps_rms, RMS_EPS).then_inc(f.eps_set, 1)
            for t in range(TB + 5):
                if t < TB:
                    dve.wait_ge(x_in[t], 16)
                    nc.vector.bn_stats(st1[:, t, 0:6], xa[:, t, :]).then_inc(f.stats_made_raw, 1)
                    dve.wait_ge(f.stats_made_raw, t + 1)
                    nc.vector.bn_aggr(st1[:, t, 6:8], st1[:, t, 0:6]).then_inc(f.stats_made, 1)
                if 0 <= t - 1 < TB:
                    u = t - 1
                    dve.wait_ge(f.std_made, u + 1)
                    nc.vector.reciprocal(st1[:, u, 9:10], st1[:, u, 8:9]).then_inc(f.rstd_made, 1)
                if 0 <= t - 2 < TB:
                    u = t - 2
                    dve.wait_ge(f.xt_hi_made, u + 1)
                    nc.vector.tensor_tensor(xt_lo[:, u % 4, :, :], bank[u % 2][:, :].rearrange("p (c n) -> p c n", c=DC),
                                            xt_hi[:, u % 4, :, :].bitcast(F32), ALU.subtract).then_inc(f.xt_split, 1)
                if 0 <= t - 3 < TB:
                    u = t - 3
                    lat, q = bank[2 + u % 2], u % QB
                    if u == 0:
                        dve.wait_ge(f.lnw_in, 16)
                        dve.wait_ge(f.kcs_in, 16)
                    dve.wait_ge(f.std_rms_made, u + 1)
                    nc.vector.reciprocal(st1[:, u, 14:16], st1[:, u, 12:14]).then_inc(f.rstd_rms_made, 1)
                    nc.vector.tensor_tensor(kra[:, u, :], lat[:, RQ + RKV:LAT], kcs[:, q, 0, :], ALU.mult)\
                      .then_inc(f.krot_parts, 1)
                    nc.vector.tensor_tensor(krb[:, u, 0:HR], lat[:, LAT - HR:LAT], kcs[:, q, 1, 0:HR], ALU.mult)\
                      .then_inc(f.krot_parts, 1)
                    nc.vector.tensor_tensor(krb[:, u, HR:ROPE], lat[:, RQ + RKV:LAT - HR], kcs[:, q, 1, HR:ROPE],
                                            ALU.mult).then_inc(f.krot_parts, 1)
                    dve.wait_ge(f.rstd_rms_made, u + 1)
                    rq, rc = st1[:, u, 14:15], st1[:, u, 15:16]
                    nc.vector.scalar_tensor_tensor(qn[:, u, 0:RQ], lat[:, 0:RQ], rq, lnw[:, 0:RQ], ALU.mult, ALU.mult)
                    nc.vector.scalar_tensor_tensor(qn[:, u, RQ:2 * P], lat[:, P:RQ], rq, lnw[:, P:RQ], ALU.mult, ALU.mult)\
                      .then_inc(f.qn_made, 1)
                    nc.vector.scalar_tensor_tensor(kvn[:, u, 0:RKV], lat[:, RQ:RQ + RKV], rc, lnw[:, RQ:RQ + RKV],
                                                   ALU.mult, ALU.mult)
                    dve.wait_ge(f.krot_parts, 3 * (u + 1))
                    nc.vector.tensor_tensor(kvn[:, u, RKV:P], kra[:, u, :], krb[:, u, :], ALU.add).then_inc(f.kvn_made, 1)
                if 0 <= t - 5 < TB:
                    u = t - 5
                    tq = bank[4]
                    dve.wait_ge(f.qk_hi_made, u + 1)
                    nc.vector.tensor_tensor(ql_lo[:, :, u * P:(u + 1) * P],
                                            tq[:, 0:2 * P].rearrange("p (c n) -> p c n", c=2),
                                            ql_hi[:, :, u * P:(u + 1) * P].bitcast(F32), ALU.subtract)
                    nc.vector.tensor_tensor(kt_lo[:, u * P:(u + 1) * P], tq[:, 2 * P:3 * P],
                                            kt_hi[:, u * P:(u + 1) * P].bitcast(F32), ALU.subtract)\
                      .then_inc(f.qk_split, 1)
                if t == 4:
                    weights_lo(0)
                if t == 9:
                    dve.wait_ge(f.cst_in, 16)
                if t in (10, 11):
                    rotate_swapped(t - 10, t - 10, first=True)
                    rotate_own(t - 10, t - 10, first=True)
                if t == TB + 4:
                    query_lo(0, 0, 0)

            query_lo(1, 0, 1)
            rotate_swapped(2, 0)
            mask_and_max(0, 0, first=True)
            mask_and_max(1, 1, first=True)
            body(0, first=True)
            with nc.vector.Fori(1, PAIRS - 1) as p:
                body(p)
            body(PAIRS - 1, last=True)
            split_weights(3)
            scale_o(2 * PAIRS - 1, PAIRS - 1, 1)

            steps = [0]

            def step(ins, sem):
                steps[0] += 1
                ins.then_inc(sem, 1)
                dve.wait_ge(sem, steps[0])

            def statistics(st, src, sem):
                step(nc.vector.bn_stats(st[:, 0:6], src), sem)
                step(nc.vector.bn_aggr(st[:, 6:8], st[:, 0:6]), sem)

            for k in range(4, PAIRS // 2):
                split_weights(k)
            for t in range(TB + 2):
                if 0 <= t - 1 < TB:
                    dve.wait_ge(c.y_made, t)
                    statistics(st2, bank[(t - 1) % 2][:, :], c.dve_step)
                if t < TB:
                    split_output(t, 1)
                if 0 <= t - 1 < TB:
                    u = t - 1
                    dve.wait_ge(c.std1_made, u + 1)
                    step(nc.vector.reciprocal(st2[:, 9:10], st2[:, 8:9]), c.dve_step)
                    step(nc.vector.tensor_scalar(st2[:, 10:11], st2[:, 6:7], st2[:, 9:10], -1.0, ALU.mult, ALU.mult),
                         c.dve_step)
                    dve.wait_ge(c.z_made, u + 1)
                    if u == 0:
                        dve.wait_ge(c.x1_in, 16)
                    step(nc.vector.tensor_tensor(x1[:, u, :], x1[:, u, :], xn2[:, :], ALU.add), c.dve_step)
                    statistics(st2, x1[:, u, :], c.dve_step)
                    dve.wait_ge(c.std2_made, u + 1)
                    nc.vector.reciprocal(st2[:, 11:12], st2[:, 8:9]).then_inc(c.rstd2_made, 1)
                    dve.wait_ge(c.rstd2_made, u + 1)
                    nc.vector.tensor_scalar(xn2[:, :], x1[:, u, :], st2[:, 6:7], st2[:, 11:12],
                                            ALU.subtract, ALU.mult).then_inc(c.xn2_made, 1)
                    dve.wait_ge(c.xn2_made, u + 1)
                    if u:
                        dve.wait_ge(c.y_turned, u)
                    nc.vector.tensor_reduce(fold[:, :], xn2[:, :].rearrange("p (c n) -> p n c", c=DC), AX.X, ALU.add)\
                      .then_inc(c.fold_made, 1)
                if t + 1 < TB:
                    split_output(t + 1, 0)
                if 0 <= t - 3 < TB - 2:
                    lora_lo(t - 3)
                if t in (4, 5):
                    dve.wait_ge(g.w_hi_made, t - 3)
                    nc.vector.tensor_tensor(w13_lo[:, t - 4, :], w13[:, t - 4, :], w13_hi[:, t - 4, :].bitcast(F32),
                                            ALU.subtract).then_inc(g.w_split, 1)
                if t == 6:
                    dve.wait_ge(g.bs_hi_made, 1)
                    nc.vector.tensor_tensor(bs_s[32:64, :], bs[32:64, :], bs_s[32:64, :].bitcast(F32), ALU.subtract)\
                      .then_inc(g.bs_split, 1)
                    dve.wait_ge(g.xf_hi_made, 1)
                    nc.vector.tensor_tensor(xf_lo[:, 0:SEQ], xft[:, 0:SEQ], xf_hi[:, 0:SEQ].bitcast(F32), ALU.subtract)\
                      .then_inc(g.xf_split, 1)

            lora_lo(TB - 2)

            def down_lo(hf, r):
                n = RROWS[r]
                dve.wait_ge(g.fs_hi_made, 3 * hf + r + 1)
                nc.vector.tensor_tensor(fs_lo[0:n, hf, r, :], fs[0:n, hf, r, :], fs_hi[0:n, hf, r, :].bitcast(F32),
                                        ALU.subtract).then_inc(g.fs_split, 1)

            for hf in range(2):
                for n in range(12):
                    G, rows = 12 * hf + n, RROWS[n // FOLD]
                    dve.wait_ge(g.silu_made, G + 1)
                    dve.wait_ge(g.up_made, G + 1)
                    if G >= 8:
                        dve.wait_ge(g.la_made, G // 4 - 1)
                        dve.wait_ge(g.fold_added, 3 * (G // 4 - 1))
                    nc.vector.tensor_tensor(gu[0:rows, G % 8, :], bank[(7, 2)[G % 2]][0:rows, :], sg[0:rows, G % 2, :],
                                            ALU.mult).then_inc(g.gu_made, 1)
                    if G == 2:
                        lora_lo(TB - 1)
                        dve.wait_ge(g.xf_hi_made, 2)
                        nc.vector.tensor_tensor(xf_lo[:, SEQ:TOK], xft[:, SEQ:TOK], xf_hi[:, SEQ:TOK].bitcast(F32),
                                                ALU.subtract).then_inc(g.xf_split, 1)
                    if G == 6:
                        dve.wait_ge(g.wd_hi_made, 1)
                        nc.vector.tensor_tensor(wd_lo[:, :, :], wd[:, :, :], wd_hi[:, :, :].bitcast(F32), ALU.subtract)\
                          .then_inc(g.wd_split, 1)
                    if n in (8,):
                        down_lo(hf, 0)
                down_lo(hf, 1)
                down_lo(hf, 2)
            steps[0] = 0
            for t in range(TB):
                st = st3[:, t % 2, :]
                dve.wait_ge(g.y_made, t + 1)
                statistics(st, bank[t % 2][:, :], g.dve_step)
                dve.wait_ge(g.std_made, t + 1)
                step(nc.vector.reciprocal(st[:, 9:10], st[:, 8:9]), g.dve_step)
                step(nc.vector.tensor_scalar(st[:, 10:11], st[:, 6:7], st[:, 9:10], -1.0, ALU.mult, ALU.mult), g.dve_step)
                dve.wait_ge(g.z_made, t + 1)
                if t >= 2:
                    dve.wait_ge(g.out_sent, 16 * (t - 1))
                nc.vector.tensor_tensor(yo[:, t % 2, :], x1[:, t, :], z2[:, t % 2, :], ALU.add).then_inc(g.out_made, 1)
                step(nc.vector.memset(st[:, 15:16], 0.0), g.dve_step)

        @block.tensor
        def _(pe):
            def three(out, w_hi, w_lo, x_hi, x_lo, start, stop):
                nc.tensor.matmul(out, w_hi, x_hi, start=start, stop=False)
                nc.tensor.matmul(out, w_hi, x_lo, start=False, stop=False)
                return nc.tensor.matmul(out, w_lo, x_hi, start=False, stop=stop)

            def absorb_query(w):
                pe.wait_ge(a.sq_in, 16 * (w + 1))
                for k in range(2):
                    for h in range(2):
                        last = nc.tensor.matmul(bank[XB][:, (2 * k + h) * RKV:(2 * k + h + 1) * RKV],
                                                sq[:, (2 * h + k) * P:(2 * h + k + 1) * P],
                                                sq[:, 4 * P + h * RKV:4 * P + (h + 1) * RKV], start=True, stop=True)
                last.then_inc(a.wq_made, 1)

            def query(gi, b, h, w=None, first=False):
                if w is not None:
                    pe.wait_ge(a.wq_split, w + 1)
                if not first:
                    pe.wait_ge(a.q_rotated, gi - 1)
                out, tok = bank[6 + h][:, :], slice(b * SEQ, (b + 1) * SEQ)
                three(out, w1_hi[:, h, :], w1_lo[:, h, :], ql_hi[:, 0, tok], ql_lo[:, 0, tok], True, False)
                nc.tensor.matmul(out, w2[:, h, :], ql_hi[:, 1, tok], start=False, stop=False)
                nc.tensor.matmul(out, w2[:, h, :], ql_lo[:, 1, tok], start=False, stop=True).then_inc(a.q_made, 1)

            def scores(U, k, gi, first=False):
                i, h, b = k % QB, k // QB % 2, k // UNITS
                if i == 0:
                    pe.wait_ge(a.qt_split, gi + 1)
                if not first:
                    pe.wait_ge(a.s_masked, U - 1)
                keys = slice(b * SEQ, b * SEQ + (i + 1) * P)
                three(bank[k % 2][:, 0:(i + 1) * P], qt_hi[:, b, h, i * P:(i + 1) * P], qt_lo[:, b, h, i * P:(i + 1) * P],
                      kt_hi[:, keys], kt_lo[:, keys], True, True).then_inc(a.s_made, 1)

            def turn_p(U, k, first=False):
                pe.wait_ge(a.exp_made, U + 1)
                if not first:
                    pe.wait_ge(a.p_moved, U - 1)
                for j in range(k % QB + 1):
                    last = nc.tensor.transpose(bank[2 + k % 2][:, j * P:(j + 1) * P], pr[:, k % 4, j * P:(j + 1) * P],
                                               ident[:, :])
                last.then_inc(a.p_turned, 1)

            def output(m, b, js, first=False):
                if 0 in js:
                    pe.wait_ge(a.p_moved, UNITS * (m + 1))
                    if not first:
                        pe.wait_ge(a.o_scaled, m)
                for j in js:
                    for h in range(2):
                        last = nc.tensor.matmul(bank[4][RKV * h:RKV * (h + 1), j * P:SEQ], kvn[:, QB * b + j, 0:RKV],
                                                pt[:, b, h, j, j * P:SEQ], start=(j == 0), stop=(j == QB - 1),
                                                skip_group_check=True)
                if QB - 1 in js:
                    last.then_inc(a.o_made, 1)

            def turn_r(m):
                pe.wait_ge(a.rb_made, m + 1)
                for i in range(QB):
                    last = nc.tensor.transpose(bank[XB][:, i * P:(i + 1) * P], rb[:, i, :, :].rearrange("p h n -> p (h n)"),
                                               ident[:, :])
                last.then_inc(a.r_made, 1)

            def absorb_output(p):
                pe.wait_ge(a.sv_in, 16 * (p + 1))
                for h in range(2):
                    last = nc.tensor.matmul(bank[XB][RKV * h:RKV * (h + 1), :], sv[:, h * RKV:(h + 1) * RKV],
                                            sv[:, 2 * RKV + h * D:2 * RKV + (h + 1) * D], start=True, stop=True)
                last.then_inc(a.wvo_made, 1)

            def body(p, first=False, last=False):
                for k in range(PU):
                    n = k + 2
                    if n < PU:
                        scores(PU * p + n, n, 4 * p + n // QB)
                    elif not last:
                        scores(PU * p + n, n - PU, 4 * p + 4)
                    if k == 0 and not last:
                        if not first:
                            pe.wait_ge(a.r_moved, 2 * p - 1)
                        absorb_query(p + 1)
                    if k == 1 and not first:
                        output(2 * p - 1, 1, [0])
                    if k == 2 and not first:
                        output(2 * p - 1, 1, [1, 2, 3])
                    if k == 4 and not first:
                        if last:
                            pe.wait_ge(a.r_moved, 2 * p - 1)
                        else:
                            pe.wait_ge(a.wq_split, p + 2)
                        turn_r(2 * p - 1)
                    if k == 8:
                        if first:
                            pe.wait_ge(a.wq_split, p + 2)
                        else:
                            pe.wait_ge(a.r_moved, 2 * p)
                        absorb_output(p)
                    if k in (6, 7) and not last:
                        query(4 * p + 4 + k - 6, 0, k - 6, p + 1)
                    if k == 9:
                        output(2 * p, 0, [0], first)
                    if k == 10:
                        output(2 * p, 0, [1, 2, 3])
                    if k == 11:
                        pe.wait_ge(a.wvo_moved, p + 1)
                        turn_r(2 * p)
                    if k in (14, 15) and not last:
                        query(4 * p + 6 + k - 14, 1, k - 14)
                    turn_p(PU * p + k, k, first and k < 2)

            pe.wait_ge(f.ident_made, 1)
            for t in range(TB + 4):
                if 0 <= t - 1 < TB:
                    u = t - 1
                    pe.wait_ge(f.xn_made, u + 1)
                    if u >= 2:
                        pe.wait_ge(f.xt_split, u - 1)
                    for k in range(DC):
                        last = nc.tensor.transpose(bank[u % 2][:, k * P:(k + 1) * P], xn[:, u, k * P:(k + 1) * P],
                                                   ident[:, :])
                    last.then_inc(f.x_turned, 1)
                if 0 <= t - 2 < TB:
                    u = t - 2
                    pe.wait_ge(f.wa_split, 1)
                    pe.wait_ge(f.xt_split, u + 1)
                    if u >= 2:
                        pe.wait_ge(f.kvn_made, u - 1)
                    for k in range(DC):
                        last = three(bank[2 + u % 2][:, 0:LAT], xt_hi[:, u % 4, k, :], xt_lo[:, u % 4, k, :],
                                     wa_hi[:, k, :], wa_lo[:, k, :], k == 0, k == DC - 1)
                    last.then_inc(f.lat_made, 1)
                if 0 <= t - 4 < TB:
                    u = t - 4
                    tq = bank[4]
                    pe.wait_ge(f.qn_made, u + 1)
                    pe.wait_ge(f.kvn_made, u + 1)
                    if u >= 1:
                        pe.wait_ge(f.qk_split, u)
                    nc.tensor.transpose(tq[:, 0:P], qn[:, u, 0:P], ident[:, :])
                    nc.tensor.transpose(tq[:, P:2 * P], qn[:, u, P:2 * P], ident[:, :])
                    nc.tensor.transpose(tq[:, 2 * P:3 * P], kvn[:, u, :], ident[:, :]).then_inc(f.qk_turned, 1)
                if t == 3:
                    absorb_query(0)
                if t == 9:
                    pe.wait_ge(f.qk_split, QB)
                    for h in range(2):
                        query(h, 0, h, 0 if h == 0 else None, first=True)

            pe.wait_ge(f.qk_split, TB)
            for h in range(2):
                query(2 + h, 1, h)
            scores(0, 0, 0, first=True)
            scores(1, 1, 0, first=True)
            body(0, first=True)
            with nc.tensor.Fori(1, PAIRS - 1) as p:
                body(p)
            body(PAIRS - 1, last=True)
            output(2 * PAIRS - 1, 1, [0, 1, 2, 3])

            def project(t, hh):
                pe.wait_ge(c.o_split, 2 * t + hh + 1)
                if t >= 2 and hh == 0:
                    pe.wait_ge(c.z_made, t - 1)
                for k in range(PAIRS // 2):
                    q = 8 * hh + k
                    if t == 0 and k % 2 == 0:
                        pe.wait_ge(c.wv_split, q // 2 + 1)
                    last = three(bank[t % 2][:, :], o_s[:, hh, 0, k, :], o_s[:, hh, 1, k, :],
                                 wv[:, PAIRS - 1 - q, 0, :], wv[:, PAIRS - 1 - q, 1, :], q == 0, q == PAIRS - 1)
                last.then_inc(c.o_used, 1)
                if hh:
                    pe.wait_ge(c.o_used, 2 * t + 2)
                    pe.sem_inc(c.y_made, 1)

            def turn_y(u):
                pe.wait_ge(c.fold_made, u + 1)
                if u:
                    pe.wait_ge(c.xt2_moved, u)
                for k in range(DC):
                    nc.tensor.transpose(bank[2][:, k * P:(k + 1) * P], xn2[:, k * P:(k + 1) * P], ident[:, :])
                nc.tensor.transpose(bank[3][:, 0:P], fold[:, :], ident[:, :]).then_inc(c.y_turned, 1)

            def lora_latents(u):
                pe.wait_ge(c.xt2_moved, u + 1)
                if u:
                    pe.wait_ge(c.lp_split, u)
                else:
                    pe.wait_ge(c.a13_in, 16)
                for k in range(DC):
                    last = nc.tensor.matmul(bank[4][0:96, 0:P], a13[:, k, :], xn2t[:, k, :], start=(k == 0), stop=(k == DC - 1))
                last.then_inc(c.lp_made, 1)

            pe.wait_ge(a.s_masked, PU * PAIRS)
            project(0, 0)
            pe.wait_ge(a.r_moved, 2 * PAIRS - 1)
            turn_r(2 * PAIRS - 1)
            project(0, 1)
            for t in range(1, TB):
                project(t, 0)
                project(t, 1)
                turn_y(t - 1)
                if t >= 2:
                    lora_latents(t - 2)

            def gate_or_up(which, G, n, hf):
                r, k = n // FOLD, n % FOLD
                rows, j, tok = RROWS[r], k * W2C + r * P, slice(hf * SEQ, (hf + 1) * SEQ)
                out = bank[5 + G % 2 if which == 0 else (7, 2)[G % 2]][0:rows, :]
                three(out, w13_hi[:, which, j:j + rows], w13_lo[:, which, j:j + rows], xf_hi[:, tok], xf_lo[:, tok],
                      True, False)
                return nc.tensor.matmul(out, bs_s[:, j:j + rows], (lg, lu)[which][0:96, tok], start=False, stop=True)

            def lora_down(hf, r):
                G, rows = 12 * hf + 4 * r, RROWS[r]
                pe.wait_ge(g.a2_in, 16)
                pe.wait_ge(g.gu_made, G + 4)
                if hf and r == 0:
                    pe.wait_ge(g.l2_made, 1)
                for k in range(FOLD):
                    last = nc.tensor.matmul(bank[3][32 * k:32 * k + 32, :], a2[0:rows, r, k, :], gu[0:rows, (G + k) % 8, :],
                                            start=(r == 0), stop=(r == RT - 1), tile_position=(0, 32 * k),
                                            skip_group_check=True)
                last.then_inc(g.la_made, 1)

            pe.wait_ge(g.xf_split, 1)
            pe.wait_ge(g.bs_split, 1)
            pe.wait_ge(c.lp_split, QB)
            for hf in range(2):
                for n in range(12):
                    G = 12 * hf + n
                    if G < 1:
                        pe.wait_ge(g.w_split, 2)
                        lora_latents(TB - 2)
                    if G == 1:
                        turn_y(TB - 1)
                        lora_latents(TB - 1)
                    if G == 12:
                        pe.wait_ge(g.xf_split, 2)
                        pe.wait_ge(c.lp_split, TB)
                    if G >= 2:
                        pe.wait_ge(g.silu_made, G - 1)
                    gate_or_up(0, G, n, hf).then_inc(g.gate_made, 1)
                    if G >= 2:
                        pe.wait_ge(g.gu_made, G - 1)
                    gate_or_up(1, G, n, hf).then_inc(g.up_made, 1)
                    if n in (5, 9):
                        lora_down(hf, n // FOLD - 1)
                lora_down(hf, RT - 1)
            pe.wait_ge(g.wd_split, 1)
            pe.wait_ge(g.b2_in, 16)
            for t in range(TB):
                hf, q = t // QB, t % QB * P
                pe.wait_ge(g.fs_split, 3 * (hf + 1))
                pe.wait_ge(g.l2_made, hf + 1)
                if t >= 2:
                    pe.wait_ge(g.z_made, t - 1)
                for r in range(RT):
                    n = RROWS[r]
                    three(bank[t % 2][:, :], fs_hi[0:n, hf, r, q:q + P], fs_lo[0:n, hf, r, q:q + P], wd_hi[0:n, r, :],
                          wd_lo[0:n, r, :], r == 0, False)
                nc.tensor.matmul(bank[t % 2][:, :], l2[:, hf, q:q + P], b2[:, :], start=False, stop=True)\
                  .then_inc(g.y_made, 1)


def kernel(**inputs):
    import concourse.bacc as bacc
    from concourse.bass_utils import run_bass_kernel_spmd

    I = {k.removeprefix("L0_"): np.asarray(v) for k, v in inputs.items()}
    x = I["attn_hidden_states"]
    f32 = np.float32
    evens_odds = np.r_[0:ROPE:2, 1:ROPE:2]

    def put(shape, *parts):
        a = np.zeros(shape, f32)
        for at, v in parts:
            a[at] = v
        return a

    wkv_a = np.concatenate([I["attn_Wkv_a"][:, :RKV], I["attn_Wkv_a"][:, RKV:][:, evens_odds]], 1)
    wa = np.concatenate([I["attn_Wq_a"], wkv_a], 1).reshape(DC, P, LAT).transpose(1, 0, 2)
    lnw = np.broadcast_to(np.concatenate([I["attn_q_a_ln_w"], I["attn_kv_a_ln_w"]]), (P, RQ + RKV))

    inv = (1.0 / f32(10000.0) ** (np.arange(0, ROPE, 2, dtype=f32) / f32(ROPE))).astype(f32)
    ang = np.outer(np.arange(SEQ, dtype=f32), inv).astype(f32)
    cos, sin = np.cos(ang).astype(f32), np.sin(ang).astype(f32)
    cst = np.zeros((P, 3 * SEQ + 8), f32)
    cst[:, SEQ - P:SEQ] = np.where(np.arange(P)[None, :] > np.arange(P)[:, None], f32(-BIG), f32(0))
    cst[:64, SEQ:2 * SEQ] = 1
    cst[64:, SEQ:2 * SEQ] = np.concatenate([cos.T, cos.T])
    cst[64:96, 2 * SEQ:3 * SEQ] = sin.T
    cst[96:128, 2 * SEQ:3 * SEQ] = -sin.T
    for g in range(3):
        cst[32 * g:32 * g + 2, 3 * SEQ] = LORA_SCALE
        cst[32 * g + 2:32 * g + 4, 3 * SEQ + 1] = LORA_SCALE
    kcs = np.concatenate([cos, cos, -sin, sin], 1).reshape(QB, P, 2, ROPE).transpose(1, 0, 2, 3)

    wq = I["attn_Wq_b"].reshape(RQ, H, NOPE + ROPE)
    wkv = I["attn_Wkv_b"].reshape(RKV, H, NOPE + VD)
    qT = wq[:, :, :NOPE].transpose(1, 2, 0)
    qT = np.concatenate([qT, qT[:, :, P:]], 2).reshape(PAIRS, 2, NOPE, 2 * P).transpose(0, 2, 1, 3)
    kT = wkv[:, :, :NOPE].transpose(1, 2, 0).reshape(PAIRS, 2, NOPE, RKV).transpose(0, 2, 1, 3)
    pe = wq[:, :, NOPE:][:, :, evens_odds].reshape(RQ, PAIRS, 2, ROPE).transpose(1, 0, 2, 3)
    sq = np.concatenate([qT.reshape(PAIRS, P, -1), kT.reshape(PAIRS, P, -1), pe[:, :P].reshape(PAIRS, P, -1),
                         np.concatenate([pe[:, P:], pe[:, P:]], 1).reshape(PAIRS, P, -1)], 2)
    vT = wkv[:, :, NOPE:].transpose(1, 2, 0).reshape(PAIRS, 2, VD, RKV).transpose(0, 2, 1, 3)
    wo = I["attn_Wo"].reshape(PAIRS, 2, VD, D).transpose(0, 2, 1, 3)
    sv = np.concatenate([vT.reshape(PAIRS, P, -1), wo.reshape(PAIRS, P, -1)], 2)

    w13 = np.stack([I["ffn_w1q"].T, I["ffn_w3q"].T], 1)
    bs = put((96, HID), *[(slice(32 * g + 2 * k, 32 * g + 2 * k + 2), I[n].T)
                          for g in range(3) for k, n in enumerate(("ffn_b1", "ffn_b3"))])
    a13 = put((P, DC, 96), *[((slice(None), slice(None), slice(32 * g + 2 * k, 32 * g + 2 * k + 2)),
                              I[n].reshape(RANK, DC, P).transpose(2, 1, 0))
                             for g in range(3) for k, n in enumerate(("ffn_a1", "ffn_a3"))])
    a2r = I["ffn_a2"].reshape(RANK, FOLD, W2C)
    a2 = put((P, RT, FOLD, 32), *[((slice(0, RROWS[r]), r, slice(None), slice(0, RANK)),
                                   a2r[:, :, r * P:r * P + RROWS[r]].transpose(2, 1, 0)) for r in range(RT)])
    w2 = put((P, RT, D), *[((slice(0, RROWS[r]), r), I["ffn_w2q"].T[r * P:r * P + RROWS[r]]) for r in range(RT)])
    b2 = put((P, D), *[(slice(32 * k, 32 * k + RANK), I["ffn_b2"].T) for k in range(FOLD)])

    nc = bacc.Bacc("TRN2", target_bir_lowering=False, num_devices=1)
    arrays = dict(x=x, wa=wa, lnw=lnw, cst=cst, kcs=kcs, sq=sq, sv=sv, w13=w13, bs=bs, a13=a13, a2=a2, w2=w2, b2=b2)
    arrays = {k: np.ascontiguousarray(v) for k, v in arrays.items()}
    args = [nc.dram_tensor(k, v.shape, F32, kind="ExternalInput").ap() for k, v in arrays.items()]
    out = nc.dram_tensor("out", x.shape, F32, kind="ExternalOutput").ap()
    build(nc, *args, out)
    r = run_bass_kernel_spmd(nc, [arrays], core_ids=[0])
    return r.results[0]["out"]
```

```python
import concourse.bass as bass
from concourse import mybir
import numpy as np

F32 = mybir.dt.float32
F32R = mybir.dt.float32r
ALU = mybir.AluOpType
ACT = mybir.ActivationFunctionType
AX = mybir.AxisListType

P = 128
BATCH, SEQ, D = 2, 512, 512
TOK = BATCH * SEQ
TB = TOK // P
QB = SEQ // P
DC = D // P
H, PAIRS = 32, 16
RQ, RKV = 192, 64
NOPE, ROPE, VD = 128, 64, 128
HR = ROPE // 2
LAT = RQ + RKV + ROPE
SCALE = float(NOPE + ROPE) ** -0.5
LN_EPS, RMS_EPS = 1e-5, 1e-6
BIG = 3.0e38
XB = 5
YB = (0, 1, 4)
TQ = (XB, 4)
UNITS = 2 * QB
PU = BATCH * UNITS
HID, RANK = 1376, 2
FOLD = 4
W2C = HID // FOLD
RT = (W2C + P - 1) // P
RROWS = [min(P, W2C - P * r) for r in range(RT)]
SQ_COLS = 2 * 2 * P + 2 * RKV + 2 * 2 * ROPE
SV_COLS = 2 * RKV + 2 * D
LORA_SCALE = 0.5
CST_BYTES = 4 * (3 * SEQ + 8)


class Semaphores(dict):

    __getattr__ = dict.__getitem__


class Map:

    def __init__(self, nc, start, end):
        self.nc, self.at, self.end = nc, start, end

    def take(self, name, shape, dt=F32):
        t = self.nc.alloc_sbuf_tensor_at(name, shape, dt, offset=self.at)
        self.at += (4 * int(np.prod(shape[1:])) + 31) // 32 * 32
        assert self.at <= self.end, (name, self.at, self.end)
        return t


def build(nc, x_d, wa_d, lnw_d, cst_d, kcs_d, sq_d, sv_d, w13_d, bs_d, a13_d, a2_d, w2_d, b2_d, out_d):
    wvo_d = nc.dram_tensor("wvo_scratch", [PAIRS, P, D], F32, kind="Internal").ap()
    top = nc.sbuf_usable_end // 32 * 32
    start = (nc.sbuf_base + 63) // 64 * 64

    keep = Map(nc, start, top)
    ident = keep.take("ident", [P, P])
    keep_eps = keep.take("eps", [P, 8])
    cst = keep.take("cst", [P, 3 * SEQ + 8])
    ot = keep.take("ot", [P, TB, PAIRS, P])
    late = keep.at
    mask = cst[:, 0:SEQ]
    cos1 = cst[:, SEQ:2 * SEQ]
    sin1 = cst[:, 2 * SEQ:3 * SEQ]
    eps = keep_eps
    eps_ln, eps_rms = eps[:, 0:1], eps[:, 1:2]

    att = Map(nc, late, top)
    ql_hi = att.take("ql_hi", [P, 2, TOK], F32R)
    ql_lo = att.take("ql_lo", [P, 2, TOK], F32R)
    sq = att.take("sq", [P, SQ_COLS])
    w1_hi = att.take("w1_hi", [P, 2, P], F32R)
    w1_lo = att.take("w1_lo", [P, 2, P], F32R)
    w2 = att.take("w2", [P, 2, P], F32R)
    kt_hi = att.take("kt_hi", [P, TOK], F32R)
    kt_lo = att.take("kt_lo", [P, TOK], F32R)
    kvn = att.take("kvn", [P, TB, P])
    sv = att.take("sv", [P, SV_COLS])
    qt_hi = att.take("qt_hi", [P, BATCH, 2, SEQ], F32R)
    qt_lo = att.take("qt_lo", [P, BATCH, 2, SEQ], F32R)
    small = att.take("small", [P, 64])
    qrot = att.take("qrot", [P, 2, SEQ])
    qswp = att.take("qswp", [P, 2, SEQ])
    ss = att.take("ss", [P, 2, SEQ])
    pr = att.take("pr", [P, 4, SEQ])
    rb = att.take("rb", [P, QB, 2, RKV])
    rsb = att.take("rsb", [P, SEQ])
    vs = att.take("vs", [P, D])
    att.at += 32
    pt = att.take("pt", [P, 2, 2, QB, SEQ])
    negmax = small[:, 0:8]
    rsum = small[:, 8:24]
    rinv = small[:, 24:32]

    fir = Map(nc, start + 4 * P + 32 + CST_BYTES, late)
    xa = fir.take("xa", [P, TB, D])
    xn = fir.take("xn", [P, TB, D])
    xt_hi = fir.take("xt_hi", [P, 4, DC, P], F32R)
    xt_lo = fir.take("xt_lo", [P, 4, DC, P], F32R)
    qn = fir.take("qn", [P, TB, 2 * P])
    fi2 = Map(nc, att.at, top)
    wa = fi2.take("wa", [P, DC, LAT])
    wa_hi = fi2.take("wa_hi", [P, DC, LAT], F32R)
    wa_lo = fi2.take("wa_lo", [P, DC, LAT], F32R)
    lnw = fi2.take("lnw", [P, RQ + RKV])
    kcs = fi2.take("kcs", [P, QB, 2, ROPE])
    kra = fi2.take("kra", [P, TB, ROPE])
    krb = fi2.take("krb", [P, TB, ROPE])
    sqj = fi2.take("sqj", [P, 2, RQ])
    st1 = fi2.take("st1", [P, TB, 16])

    pro = Map(nc, late, top - 4 * 2 * PAIRS * D)
    wv_raw = pro.take("wv_raw", [P, 3, 2, D])
    o_s = pro.take("o_s", [P, 2, 2, PAIRS // 2, P], F32R)
    x1 = pro.take("x1", [P, TB, D])
    xn2 = pro.take("xn2", [P, D])
    fold = pro.take("fold", [P, P])
    lt = pro.take("lt", [P, 96])
    xft = pro.take("xft", [P, TOK])
    lg = pro.take("lg", [P, TOK], F32R)
    lu = pro.take("lu", [P, TOK], F32R)
    w13 = pro.take("w13", [P, 2, HID])
    st2 = pro.take("st2", [P, 16])
    pr2 = Map(nc, late, late + 4 * 6 * D)
    a13 = pr2.take("a13", [P, 2 * RANK, D])
    dot = pr2.take("dot", [P, 2, D])
    wv = Map(nc, top - 4 * 2 * PAIRS * D, top).take("wv", [P, PAIRS, 2, D], F32R)
    bs = nc.alloc_sbuf_tensor_at("bs", [96, HID], F32, offset=start + 4 * P + 32)

    ffn = Map(nc, start + 4 * P + 32 + CST_BYTES, late)
    w13_hi = ffn.take("w13_hi", [P, 2, HID], F32R)
    w13_lo = ffn.take("w13_lo", [P, 2, HID], F32R)
    bs_s = ffn.take("bs_s", [96, HID], F32R)
    xf_hi = ffn.take("xf_hi", [P, TOK], F32R)
    xf_lo = ffn.take("xf_lo", [P, TOK], F32R)
    b2 = ffn.take("b2", [P, D])
    a2 = ffn.take("a2", [P, RT, FOLD, 32])
    b2_s = ffn.take("b2_s", [P, D], F32R)
    l2 = ffn.take("l2", [P, 2, SEQ], F32R)
    sg = ffn.take("sg", [P, 2, SEQ])
    ff2 = Map(nc, top - 4 * 2 * PAIRS * D, top)
    gu = ff2.take("gu", [P, 8, SEQ])
    fs = ff2.take("fs", [P, 2, RT, SEQ])
    fs_hi = ff2.take("fs_hi", [P, 2, RT, SEQ], F32R)
    fs_lo = ff2.take("fs_lo", [P, 2, RT, SEQ], F32R)
    ff3 = Map(nc, late, late + 28 * 1024)
    wd = ff3.take("wd", [P, RT, D])
    wd_hi = ff3.take("wd_hi", [P, RT, D], F32R)
    wd_lo = ff3.take("wd_lo", [P, RT, D], F32R)
    z2 = ff3.take("z2", [P, 2, D])
    yo = ff3.take("yo", [P, 2, D])
    st3 = ff3.take("st3", [P, 2, 16])

    bank = [nc.alloc_psum_tensor(f"bank{i}", [P, 512], F32) for i in range(8)]

    def slot(q):
        return (15, 14, 13, 12, 11, 10, 5, 4, 3, 2, 9, 8, 7, 6, 1, 0)[q]

    def product(t):
        return t % 2 if t else 6

    def sems(phase, words):
        return Semaphores((n, nc.alloc_semaphore(f"{phase}_{n}")) for n in words.split())

    f = sems("first", """eps_set table_set stats_made_raw ident_zero ident_made wa_in lnw_in cst_in kcs_in stats_made std_made rstd_made xn_made
        x_turned xt_hi_made xt_split wa_hi_made wa_split lat_made squares_summed std_rms_made rstd_rms_made
        qn_made krot_parts kvn_made qk_turned qk_hi_made qk_split""")
    x_in = [nc.alloc_semaphore(f"x_in{t}") for t in range(TB)]
    a = sems("attention", """s_seen rinv_seen sq_in sv_in wq_made wq_hi_made wq_split q_made q_rotated pe_added qt_hi_made qt_split
        s_made s_masked exp_made p_turned p_moved o_made rinv_made rb_made r_made r_moved o_scaled
        wvo_made wvo_moved wvo_out""")
    c = sems("projection", """rstd2_made xn2_made wv_in0 wv_in1 wv_in2 wv_copied wv_hi_made wv_split o_hi_made o_split o_used x1_in w13_in bs_in a13_in
        dve_step std1_made z_made std2_made fold_made dots_raw dots_made o_lo_made lt_zero y_turned xt2_moved lp_hi_made lp_split""")
    g = sems("forward", """wd_in b2_in a2_in w_hi_made w_split xf_hi_made xf_split bs_hi_made bs_split bs_fixed wd_hi_made wd_split
        gate_made up_made silu_made gu_made la_made fold_added fs_hi_made fs_split l2_hi_made l2_split
        b2_hi_made b2_lo_made b2_split y_made moments_raw moments_made std_made rstd_made shift_made z_made out_made
        out_sent0 out_sent1""")

    xb = x_d.rearrange("b (t p) d -> (b t) p d", p=P)
    ob = out_d.rearrange("b (t p) d -> (b t) p d", p=P)
    block = nc.Block()
    with block:
        @block.sync
        def _(sp):
            sp.dma_start(xa[:, 0, :], xb[0]).then_inc(x_in[0], 16)
            sp.dma_start(wa[:, :, :], wa_d).then_inc(f.wa_in, 16)
            for t in range(1, 4):
                sp.dma_start(xa[:, t, :], xb[t]).then_inc(x_in[t], 16)
            sp.dma_start(lnw[:, :], lnw_d).then_inc(f.lnw_in, 16)
            sp.dma_start(kcs[:, :, :, :], kcs_d).then_inc(f.kcs_in, 16)
            sp.dma_start(sq[:, :], sq_d[0]).then_inc(a.sq_in, 16)
            for t in range(4, TB):
                sp.dma_start(xa[:, t, :], xb[t]).then_inc(x_in[t], 16)
            sp.dma_start(cst[:, :], cst_d).then_inc(f.cst_in, 16)
            sp.dma_start(sv[:, :], sv_d[0]).then_inc(a.sv_in, 16)
            with nc.sync.Fori(0, PAIRS - 1) as p:
                sp.wait_ge(a.wq_split, p + 1)
                sp.dma_start(sq[:, :], sq_d[bass.ds(p + 1, 1)].rearrange("a p n -> p (a n)")).then_inc(a.sq_in, 16)
                sp.wait_ge(a.wvo_made, p + 1)
                sp.dma_start(sv[:, :], sv_d[bass.ds(p + 1, 1)].rearrange("a p n -> p (a n)")).then_inc(a.sv_in, 16)
                sp.wait_ge(a.wvo_moved, p + 1)
                sp.dma_start(wvo_d[bass.ds(p, 1)].rearrange("a p n -> p (a n)"), vs[:, :]).then_inc(a.wvo_out, 16)
            sp.wait_ge(a.q_made, 4 * PAIRS)
            for k in range(PAIRS // 2):
                if k == 4:
                    sp.wait_ge(a.wvo_moved, PAIRS)
                    sp.dma_start(wvo_d[PAIRS - 1], vs[:, :]).then_inc(a.wvo_out, 16)
                if k >= 3:
                    sp.wait_ge(c.wv_split, 2 * (k - 2))
                if k == PAIRS // 2 - 1:
                    sp.wait_ge(a.wvo_out, 16 * PAIRS)
                sp.dma_start(wv_raw[:, k % 3, :, :], wvo_d[2 * k:2 * k + 2].rearrange("a p n -> p a n"))\
                  .then_inc((c.wv_in0, c.wv_in1, c.wv_in2)[k % 3], 16)
            sp.wait_ge(a.o_scaled, 2 * PAIRS)
            sp.dma_start(x1[:, :, :], xb.rearrange("t p d -> p t d")).then_inc(c.x1_in, 16)
            sp.wait_ge(c.wv_split, PAIRS)
            sp.dma_start(a13[:, :, :], a13_d).then_inc(c.a13_in, 16)
            sp.dma_start(w13[:, :, :], w13_d).then_inc(c.w13_in, 16)
            sp.dma_start(bs[:, :], bs_d).then_inc(c.bs_in, 16)
            sp.wait_ge(c.o_used, 2 * TB)
            sp.dma_start(a2[:, :, :, :], a2_d).then_inc(g.a2_in, 16)
            sp.dma_start(b2[:, :], b2_d).then_inc(g.b2_in, 16)
            sp.wait_ge(c.dots_made, TB)
            sp.dma_start(wd[:, :, :], w2_d).then_inc(g.wd_in, 16)
            for t in range(TB):
                sp.wait_ge(g.out_made, t + 1)
                sp.dma_start(ob[t], yo[:, t % 2, :]).then_inc((g.out_sent0, g.out_sent1)[t % 2], 16)
            for sent in (g.out_sent0, g.out_sent1):
                sp.wait_ge(sent, 16 * (TB // 2))

        @block.gpsimd
        def _(pool):
            nc.gpsimd.memset(ident[:, :], 0.0).then_inc(f.ident_zero, 1)
            pool.wait_ge(f.ident_zero, 1)
            nc.gpsimd.affine_select(out=ident[:, :], in_=ident[:, :], compare_op=ALU.not_equal, fill=1.0,
                                    base=0, pattern=[[-1, P]], channel_multiplier=1).then_inc(f.ident_made, 1)
            for k in range(DC):
                pool.wait_ge(f.wa_hi_made, k + 1)
                nc.gpsimd.tensor_tensor(wa_lo[:, k, :], wa[:, k, :], wa_hi[:, k, :].bitcast(F32), ALU.subtract)\
                  .then_inc(f.wa_split, 1)

            def add_rotated(gi, h, spread_before=None):
                if spread_before is not None:
                    pool.wait_ge(a.rb_made, spread_before)
                pool.wait_ge(a.q_rotated, gi + 1)
                nc.gpsimd.tensor_tensor(qrot[RKV:P, h, :], qrot[RKV:P, h, :], qswp[RKV:P, h, :], ALU.add)\
                  .then_inc(a.pe_added, 1)

            def spread(m, added, first=False):
                pool.wait_ge(a.pe_added, added)
                pool.wait_ge(a.rinv_made, m + 1)
                if not first:
                    pool.wait_ge(a.r_made, m)
                pool.sem_inc(a.rinv_seen, 1)
                nc.gpsimd.tensor_copy(rb[:, :, :, :],
                                      rinv.rearrange("p (h i) -> p i h", h=2).unsqueeze(3).to_broadcast([P, QB, 2, RKV]))\
                  .then_inc(a.rb_made, 1)

            def body(p, first=False, last=False):
                for h in range(2):
                    add_rotated(4 * p + 2 + h, h, 2 * p if h == 0 and not first else None)
                spread(2 * p, 4 * p + 4, first)
                if not last:
                    for h in range(2):
                        add_rotated(4 * p + 4 + h, h, 2 * p + 1 if h == 0 else None)
                spread(2 * p + 1, 4 * p + (4 if last else 6))

            for h in range(2):
                add_rotated(h, h)
            body(0, first=True)
            with nc.gpsimd.Fori(1, PAIRS - 1) as p:
                body(p)
            body(PAIRS - 1, last=True)

            for t in range(1, TB):
                for hh in (1,) if t == 1 else (0, 1):
                    pool.wait_ge(c.o_hi_made, 2 * t + hh + 1)
                    nc.gpsimd.tensor_tensor(o_s[:, hh, 1, :, :], ot[:, t, 8 * hh:8 * hh + 8, :],
                                            o_s[:, hh, 0, :, :].bitcast(F32), ALU.subtract).then_inc(c.o_lo_made, 1)

            for hf in range(2):
                for r in range(RT):
                    n = RROWS[r]
                    for k in range(1, FOLD):
                        pool.wait_ge(g.gu_made, 12 * hf + 4 * r + k + 1)
                        if (hf, r, k) != (0, 0, 1):
                            pool.wait_ge(g.fold_added, 3 * (3 * hf + r) + k - 1)
                        at = lambda q: (12 * hf + 4 * r + q) % 8
                        nc.gpsimd.tensor_tensor(fs[0:n, hf, r, :], gu[0:n, at(0), :] if k == 1 else fs[0:n, hf, r, :],
                                                gu[0:n, at(k), :], ALU.add).then_inc(g.fold_added, 1)

        @block.scalar
        def _(act):
            def lat_view(t):
                return bank[2 + t % 2]

            def weights_hi(w, first=False):
                act.wait_ge(a.wq_made, w + 1)
                if not first:
                    act.wait_ge(a.q_made, 4 * w)
                pv = bank[XB][:, 0:4 * RKV].rearrange("p (k h n) -> p k h n", k=2, h=2)
                rv = sq[:, SQ_COLS - 4 * ROPE:SQ_COLS].rearrange("p (k h n) -> p k h n", k=2, h=2)
                nc.scalar.activation(w1_hi[:, :, 0:RKV], pv[:, 0], ACT.Copy)
                nc.scalar.activation(w1_hi[:, :, RKV:P], rv[:, 0], ACT.Copy)
                nc.scalar.activation(w2[:, :, 0:RKV], pv[:, 1], ACT.Copy)
                nc.scalar.activation(w2[:, :, RKV:P], rv[:, 1], ACT.Copy).then_inc(a.wq_hi_made, 1)

            def query_hi(gi, b, h, s_done=None):
                act.wait_ge(a.pe_added, gi + 1)
                if s_done is not None:
                    act.wait_ge(a.s_made, s_done)
                nc.scalar.activation(qt_hi[:, b, h, :], qrot[:, h, :], ACT.Copy).then_inc(a.qt_hi_made, 1)

            def exponent(U, k, s_first=False, old=None):
                n = P * (k % QB + 1)
                act.wait_ge(a.s_masked, U + 1)
                if not s_first:
                    act.wait_ge(a.p_turned, U - 3)
                if old is not None:
                    act.wait_ge(a.rinv_made, old)
                nc.scalar.activation(pr[:, k % 4, 0:n], ss[:, k % 2, 0:n], ACT.Exp, bias=negmax[:, k % 8:k % 8 + 1],
                                     scale=-1.0, accum_out=rsum[:, k:k + 1]).then_inc(a.exp_made, 1)

            def move_p(U, k, old=None):
                i, h, b = k % QB, k // QB % 2, k // UNITS
                act.wait_ge(a.p_turned, U + 1)
                if old is not None:
                    act.wait_ge(a.o_made, old)
                nc.scalar.activation(pt[:, b, h, 0:i + 1, i * P:(i + 1) * P],
                                     bank[2 + k % 2][:, 0:(i + 1) * P].rearrange("p (j q) -> p j q", q=P),
                                     ACT.Copy).then_inc(a.p_moved, 1)

            def move_r(m, first=False):
                act.wait_ge(a.r_made, m + 1)
                if not first:
                    act.wait_ge(a.o_scaled, m)
                nc.scalar.activation(rsb[:, :], bank[XB][:, :], ACT.Copy).then_inc(a.r_moved, 1)

            def split_weights(q):
                act.wait_ge((c.wv_in0, c.wv_in1, c.wv_in2)[q // 2 % 3], 16 * (q // 6 + 1))
                nc.scalar.activation(wv[:, slot(q), 0, :], wv_raw[:, q // 2 % 3, q % 2, :], ACT.Copy)\
                  .then_inc(c.wv_hi_made, 1)

            def split_output(t, hh):
                if t:
                    act.wait_ge(c.o_used, 2 * t + hh - 1)
                if hh:
                    act.wait_ge(a.o_scaled, 2 * PAIRS - (1 if t < QB else 0))
                nc.scalar.activation(o_s[:, hh, 0, :, :], ot[:, t, 8 * hh:8 * hh + 8, :], ACT.Copy)\
                  .then_inc(c.o_hi_made, 1)

            def lora_hi(u):
                act.wait_ge(c.y_turned, u + 1)
                nc.scalar.activation(lg[0:96, u * P:(u + 1) * P], bank[4][0:96, 0:P], ACT.Copy,
                                     scale=cst[0:96, 3 * SEQ:3 * SEQ + 1])
                nc.scalar.activation(lu[0:96, u * P:(u + 1) * P], bank[4][0:96, 0:P], ACT.Copy,
                                     scale=cst[0:96, 3 * SEQ + 1:3 * SEQ + 2]).then_inc(c.lp_hi_made, 1)

            def second_deviation(u):
                act.wait_ge(c.dve_step, 7 * u + 7)
                nc.scalar.activation(st2[:, 8:9], st2[:, 7:8], ACT.Sqrt, bias=eps_ln).then_inc(c.std2_made, 1)

            def move_turned(u):
                act.wait_ge(c.y_turned, u + 1)
                nc.scalar.activation(xft[:, u * P:(u + 1) * P], bank[3][:, 0:P], ACT.Copy).then_inc(c.xt2_moved, 1)

            def body(p, first=False, last=False):
                for k in range(PU):
                    if last and k == 6:
                        split_output(0, 0)
                    if last and k in (13, 14):
                        if k == 13:
                            act.wait_ge(a.o_made, 2 * PAIRS - 1)
                        split_weights(k - 7)
                    move_p(PU * p + k, k, 2 * p - 1 + k // UNITS if k % UNITS == 0 and not first else None)
                    n = k + 2
                    if n < PU:
                        exponent(PU * p + n, n, first and n < 4, 2 * p if n == UNITS and not first else None)
                    elif not last:
                        exponent(PU * p + n, n - PU, False, 2 * p + 1 if n == PU else None)
                    if k == (3 if first else 1) and not last:
                        weights_hi(p + 1)
                    if k in (2, 4):
                        h = (k - 2) // 2
                        query_hi(4 * p + 2 + h, 1, h, None if first else PU * (p - 1) + UNITS + QB * (h + 1))
                    if k in (10, 12) and not last:
                        h = (k - 10) // 2
                        query_hi(4 * p + 4 + h, 0, h, PU * p + QB * (h + 1))
                    if k == 5 and not first:
                        move_r(2 * p - 1)
                    if k == 12:
                        move_r(2 * p, first)
                    if k == 9:
                        act.wait_ge(a.wvo_made, p + 1)
                        if not first:
                            act.wait_ge(a.wvo_out, 16 * p)
                        nc.scalar.activation(vs[:, :], bank[XB][:, :], ACT.Copy).then_inc(a.wvo_moved, 1)

            act.wait_ge(f.eps_set, 1)
            nc.scalar.activation(eps[:, 2:3], eps_ln, ACT.Sqrt).then_inc(f.table_set, 1)
            def deviation(t):
                act.wait_ge(f.stats_made, t + 1)
                nc.scalar.activation(st1[:, t, 8:9], st1[:, t, 7:8], ACT.Sqrt, bias=eps_ln).then_inc(f.std_made, 1)

            deviation(0)
            for t in range(TB + 4):
                if 0 <= t - 3 < TB:
                    u = t - 3
                    act.wait_ge(f.lat_made, u + 1)
                    nc.scalar.activation(sqj[:, 0, :], lat_view(u)[:, 0:RQ], ACT.Square, scale=RQ ** -0.5,
                                         accum_out=st1[:, u, 10:11]).then_inc(f.squares_summed, 1)
                    nc.scalar.activation(sqj[:, 1, 0:RKV], lat_view(u)[:, RQ:RQ + RKV], ACT.Square, scale=RKV ** -0.5,
                                         accum_out=st1[:, u, 11:12]).then_inc(f.squares_summed, 1)
                    act.wait_ge(f.squares_summed, 2 * (u + 1))
                    nc.scalar.activation(st1[:, u, 12:14], st1[:, u, 10:12], ACT.Sqrt, bias=eps_rms)\
                      .then_inc(f.std_rms_made, 1)
                if 0 <= t - 1 < TB:
                    u = t - 1
                    act.wait_ge(f.x_turned, u + 1)
                    if u >= 4:
                        act.wait_ge(f.lat_made, u - 3)
                    nc.scalar.activation(xt_hi[:, u % 4, :, :], bank[u % 2][:, :].rearrange("p (c n) -> p c n", c=DC),
                                         ACT.Copy).then_inc(f.xt_hi_made, 1)
                if 0 <= t - 4 < TB:
                    u = t - 4
                    tq = bank[TQ[u % 2]]
                    act.wait_ge(f.qk_turned, u + 1)
                    nc.scalar.activation(ql_hi[:, :, u * P:(u + 1) * P],
                                         tq[:, 0:2 * P].rearrange("p (c n) -> p c n", c=2), ACT.Copy)
                    nc.scalar.activation(kt_hi[:, u * P:(u + 1) * P], tq[:, 2 * P:3 * P], ACT.Copy)\
                      .then_inc(f.qk_hi_made, 1)
                if t == 0:
                    act.wait_ge(f.wa_in, 16)
                    for k in range(DC):
                        nc.scalar.activation(wa_hi[:, k, :], wa[:, k, :], ACT.Copy).then_inc(f.wa_hi_made, 1)
                if t + 1 < TB:
                    deviation(t + 1)
                if t == 2:
                    weights_hi(0, first=True)
                if t in (TB + 1, TB + 3):
                    h = (t - TB - 1) // 2
                    query_hi(h, 0, h)
                if t == TB + 2:
                    exponent(0, 0, True)

            exponent(1, 1, True)
            body(0, first=True)
            with nc.scalar.Fori(1, PAIRS - 1) as p:
                body(p)
            body(PAIRS - 1, last=True)

            split_weights(8)
            split_weights(9)
            split_output(0, 1)
            move_r(2 * PAIRS - 1)
            for q in range(10, PAIRS):
                if q == 10:
                    act.wait_ge(a.o_made, 2 * PAIRS)
                if q == 14:
                    act.wait_ge(a.o_scaled, 2 * PAIRS)
                split_weights(q)
            for t in range(TB + 1):
                if 0 < t < TB:
                    split_output(t, 1)
                if 0 <= t - 1 < TB:
                    u = t - 1
                    act.wait_ge(c.dve_step, 7 * u + 2)
                    nc.scalar.activation(st2[:, 8:9], st2[:, 7:8], ACT.Sqrt, bias=eps_ln).then_inc(c.std1_made, 1)
                    act.wait_ge(c.dve_step, 7 * u + 4)
                    if u:
                        act.wait_ge(c.dots_made, u)
                    nc.scalar.activation(xn2[:, :], bank[product(u)][:, :], ACT.Identity, scale=st2[:, 9:10],
                                         bias=st2[:, 10:11]).then_inc(c.z_made, 1)
                    if t < TB:
                        second_deviation(u)
                if t + 1 < TB:
                    split_output(t + 1, 0)
                if 2 <= t < TB:
                    move_turned(t - 2)
                    lora_hi(t - 2)
                if t == 4:
                    act.wait_ge(c.o_used, 6)
                    act.wait_ge(c.o_lo_made, 3)
                    act.wait_ge(c.w13_in, 16)
                if t in (4, 5):
                    nc.scalar.activation(w13_hi[:, t - 4, :], w13[:, t - 4, :], ACT.Copy).then_inc(g.w_hi_made, 1)
                if t == 6:
                    act.wait_ge(c.o_lo_made, 7)
                    act.wait_ge(c.bs_in, 16)
                    nc.scalar.activation(bs_s[:, :], bs[:, :], ACT.Copy).then_inc(g.bs_hi_made, 1)
                    act.wait_ge(c.xt2_moved, QB)
                    nc.scalar.activation(xf_hi[:, 0:SEQ], xft[:, 0:SEQ], ACT.Copy).then_inc(g.xf_hi_made, 1)

            def down_hi(hf, r):
                n = RROWS[r]
                act.wait_ge(g.fold_added, 3 * (3 * hf + r + 1))
                nc.scalar.activation(fs_hi[0:n, hf, r, :], fs[0:n, hf, r, :], ACT.Copy).then_inc(g.fs_hi_made, 1)

            def lora_down_hi(hf):
                act.wait_ge(g.la_made, RT * (hf + 1))
                nc.scalar.activation(l2[:, hf, :], bank[3][:, :], ACT.Copy, scale=LORA_SCALE).then_inc(g.l2_hi_made, 1)

            for hf in range(2):
                for n in range(12):
                    G, rows = 12 * hf + n, RROWS[n // FOLD]
                    act.wait_ge(g.gate_made, G + 1)
                    if G >= 2:
                        act.wait_ge(g.gu_made, G - 1)
                    nc.scalar.activation(sg[0:rows, G % 2, :], bank[5 + G % 2][0:rows, :], ACT.Silu)\
                      .then_inc(g.silu_made, 1)
                    if G == 1:
                        second_deviation(TB - 1)
                        move_turned(TB - 2)
                        lora_hi(TB - 2)
                    if G == 5:
                        move_turned(TB - 1)
                    if G == 6:
                        lora_hi(TB - 1)
                        act.wait_ge(c.xt2_moved, TB)
                        nc.scalar.activation(xf_hi[:, SEQ:TOK], xft[:, SEQ:TOK], ACT.Copy).then_inc(g.xf_hi_made, 1)
                    if G == 9:
                        act.wait_ge(g.wd_in, 16)
                        nc.scalar.activation(wd_hi[:, :, :], wd[:, :, :], ACT.Copy).then_inc(g.wd_hi_made, 1)
                    if n in (7, 11):
                        down_hi(hf, n // FOLD - 1)
                    if G == 13:
                        down_hi(0, RT - 1)
                    if G == 14:
                        lora_down_hi(0)
                    if G == 7:
                        act.wait_ge(g.b2_in, 16)
                        nc.scalar.activation(b2_s[:, :], b2[:, :], ACT.Copy).then_inc(g.b2_hi_made, 1)
            down_hi(1, RT - 1)
            lora_down_hi(1)
            for t in range(TB):
                act.wait_ge(g.moments_made, t + 1)
                nc.scalar.activation(st3[:, t % 2, 8:9], st3[:, t % 2, 7:8], ACT.Sqrt, bias=eps_ln)\
                  .then_inc(g.std_made, 1)
                act.wait_ge(g.shift_made, t + 1)
                nc.scalar.activation(z2[:, t % 2, :], bank[YB[t % 3]][:, :], ACT.Identity, scale=st3[:, t % 2, 9:10],
                                     bias=st3[:, t % 2, 10:11]).then_inc(g.z_made, 1)

        @block.vector
        def _(dve):
            def weights_lo(w):
                dve.wait_ge(a.wq_hi_made, w + 1)
                pv = bank[XB][:, 0:4 * RKV].rearrange("p (k h n) -> p k h n", k=2, h=2)
                rv = sq[:, SQ_COLS - 4 * ROPE:SQ_COLS].rearrange("p (k h n) -> p k h n", k=2, h=2)
                for cols, src in ((slice(0, RKV), pv), (slice(RKV, P), rv)):
                    nc.vector.tensor_tensor(w1_lo[:, :, cols], src[:, 0], w1_hi[:, :, cols].bitcast(F32), ALU.subtract)
                    last = nc.vector.tensor_tensor(w2[64:P, :, cols], src[64:P, 1], w2[64:P, :, cols].bitcast(F32),
                                                   ALU.subtract)
                last.then_inc(a.wq_split, 1)

            def rotate_swapped(gi, h, first=False):
                dve.wait_ge(a.q_made, gi + 1)
                if not first:
                    dve.wait_ge(a.pe_added, gi - 1)
                G = bank[6 + h]
                nc.vector.tensor_tensor(qswp[64:96, h, :], G[96:128, :], sin1[96:128, :], ALU.mult)
                nc.vector.tensor_tensor(qswp[96:128, h, :], G[64:96, :], sin1[64:96, :], ALU.mult)

            def rotate_own(gi, h, first=False):
                if not first:
                    dve.wait_ge(a.qt_split, gi - 1)
                nc.vector.tensor_tensor(qrot[:, h, :], bank[6 + h][:, :], cos1, ALU.mult).then_inc(a.q_rotated, 1)

            def query_lo(gi, b, h):
                dve.wait_ge(a.qt_hi_made, gi + 1)
                nc.vector.tensor_tensor(qt_lo[:, b, h, :], qrot[:, h, :], qt_hi[:, b, h, :].bitcast(F32), ALU.subtract)\
                  .then_inc(a.qt_split, 1)

            def mask_and_max(U, k, first=False):
                n = P * (k % QB + 1)
                dve.wait_ge(a.s_made, U + 1)
                if not first:
                    dve.wait_ge(a.exp_made, U - 1)
                dve.sem_inc(a.s_seen, 1)
                nc.vector.tensor_tensor_reduce(out=ss[:, k % 2, 0:n], in0=bank[k % 2][:, 0:n], in1=mask[:, SEQ - n:SEQ],
                                               scale=-SCALE, scalar=3.4e38, op0=ALU.add, op1=ALU.min,
                                               accum_out=negmax[:, k % 8:k % 8 + 1]).then_inc(a.s_masked, 1)

            def invert(m, b, first=False):
                dve.wait_ge(a.exp_made, UNITS * (m + 1))
                if not first:
                    dve.wait_ge(a.rb_made, m)
                nc.vector.reciprocal(rinv, rsum[:, UNITS * b:UNITS * (b + 1)]).then_inc(a.rinv_made, 1)

            def scale_o(m, p, b):
                dve.wait_ge(a.r_moved, m + 1)
                dve.wait_ge(a.o_made, m + 1)
                nc.vector.tensor_tensor(ot[:, b * QB:(b + 1) * QB, bass.ds(p, 1), :].rearrange("p t a n -> p t (a n)"),
                                        bank[4][:, :].rearrange("p (t n) -> p t n", t=QB),
                                        rsb[:, :].rearrange("p (t n) -> p t n", t=QB), ALU.mult).then_inc(a.o_scaled, 1)

            def split_weights(q):
                raw = wv_raw[:, q // 2 % 3, q % 2, :]
                if q < 6:
                    dve.wait_ge((c.wv_in0, c.wv_in1, c.wv_in2)[q // 2], 16)
                    nc.vector.tensor_copy(wv[:, slot(q), 0, :], raw).then_inc(c.wv_copied, 1)
                    dve.wait_ge(c.wv_copied, q + 1)
                else:
                    dve.wait_ge(c.wv_hi_made, q - 5)
                nc.vector.tensor_tensor(wv[:, slot(q), 1, :], raw, wv[:, slot(q), 0, :].bitcast(F32), ALU.subtract)\
                  .then_inc(c.wv_split, 1)

            def split_output(t, hh):
                dve.wait_ge(c.o_hi_made, 2 * t + hh + 1)
                nc.vector.tensor_tensor(o_s[:, hh, 1, :, :], ot[:, t, 8 * hh:8 * hh + 8, :],
                                        o_s[:, hh, 0, :, :].bitcast(F32), ALU.subtract).then_inc(c.o_split, 1)

            def lora_lo(u):
                dve.wait_ge(c.lp_hi_made, u + 1)
                for k, l in enumerate((lg, lu)):
                    last = nc.vector.scalar_tensor_tensor(l[64:96, u * P:(u + 1) * P], bank[4][64:96, 0:P],
                                                          cst[64:96, 3 * SEQ + k:3 * SEQ + k + 1],
                                                          l[64:96, u * P:(u + 1) * P].bitcast(F32),
                                                          ALU.mult, ALU.subtract)
                last.then_inc(c.lp_split, 1)

            def body(p, first=False, last=False):
                for k in range(PU):
                    n = k + 2
                    if n < PU or not last:
                        mask_and_max(PU * p + n, n % PU)
                    if last and k == 7:
                        split_output(0, 0)
                    if last and k >= 8:
                        split_weights(k - 8)
                    if k == (4 if first else 2) and not last:
                        weights_lo(p + 1)
                    b, r, gi = (1, k, 4 * p + 2) if k < UNITS else (0, k - UNITS, 4 * p + 4)
                    if k < UNITS or not last:
                        if first and k in (1, 2):
                            rotate_swapped(gi + k - 1, k - 1)
                            if k == 1:
                                rotate_own(gi, 0)
                        elif first and k == 3:
                            rotate_own(gi + 1, 1)
                        elif r == 1:
                            rotate_swapped(gi + 1, 1)
                        elif r in (0, 2) and not (first and k == 0):
                            rotate_own(gi + r // 2, r // 2)
                        if r in (3, 5):
                            query_lo(gi + r // 2 - 1, b, r // 2 - 1)
                        if r == 7 and not last:
                            rotate_swapped(gi + 2, 0)
                    if k == 6 and not first:
                        scale_o(2 * p - 1, p - 1, 1)
                    if k == 13:
                        scale_o(2 * p, p, 0)
                    if k == 7:
                        invert(2 * p, 0, first)
                    if k == 15:
                        invert(2 * p + 1, 1)

            nc.vector.memset(eps_ln, LN_EPS)
            nc.vector.memset(eps_rms, RMS_EPS).then_inc(f.eps_set, 1)
            def moments(t):
                dve.wait_ge(x_in[t], 16)
                nc.vector.bn_stats(st1[:, t, 0:6], xa[:, t, :]).then_inc(f.stats_made_raw, 1)
                dve.wait_ge(f.stats_made_raw, t + 1)
                nc.vector.bn_aggr(st1[:, t, 6:8], st1[:, t, 0:6]).then_inc(f.stats_made, 1)

            def normalise(t):
                dve.wait_ge(f.std_made, t + 1)
                nc.vector.reciprocal(st1[:, t, 9:10], st1[:, t, 8:9]).then_inc(f.rstd_made, 1)
                dve.wait_ge(f.rstd_made, t + 1)
                nc.vector.tensor_scalar(xn[:, t, :], xa[:, t, :], st1[:, t, 6:7], st1[:, t, 9:10],
                                        ALU.subtract, ALU.mult).then_inc(f.xn_made, 1)

            moments(0)
            for t in range(TB + 4):
                if 0 <= t - 2 < TB:
                    u = t - 2
                    dve.wait_ge(f.xt_hi_made, u + 1)
                    nc.vector.tensor_tensor(xt_lo[:, u % 4, :, :], bank[u % 2][:, :].rearrange("p (c n) -> p c n", c=DC),
                                            xt_hi[:, u % 4, :, :].bitcast(F32), ALU.subtract).then_inc(f.xt_split, 1)
                if 0 <= t - 3 < TB:
                    u = t - 3
                    lat, q = bank[2 + u % 2], u % QB
                    if u == 0:
                        dve.wait_ge(f.lnw_in, 16)
                        dve.wait_ge(f.kcs_in, 16)
                    dve.wait_ge(f.std_rms_made, u + 1)
                    nc.vector.reciprocal(st1[:, u, 14:16], st1[:, u, 12:14]).then_inc(f.rstd_rms_made, 1)
                    nc.vector.tensor_tensor(kra[:, u, :], lat[:, RQ + RKV:LAT], kcs[:, q, 0, :], ALU.mult)\
                      .then_inc(f.krot_parts, 1)
                    nc.vector.tensor_tensor(krb[:, u, 0:HR], lat[:, LAT - HR:LAT], kcs[:, q, 1, 0:HR], ALU.mult)\
                      .then_inc(f.krot_parts, 1)
                    nc.vector.tensor_tensor(krb[:, u, HR:ROPE], lat[:, RQ + RKV:LAT - HR], kcs[:, q, 1, HR:ROPE],
                                            ALU.mult).then_inc(f.krot_parts, 1)
                    dve.wait_ge(f.rstd_rms_made, u + 1)
                    rq, rc = st1[:, u, 14:15], st1[:, u, 15:16]
                    nc.vector.scalar_tensor_tensor(qn[:, u, 0:RQ], lat[:, 0:RQ], rq, lnw[:, 0:RQ], ALU.mult, ALU.mult)
                    nc.vector.scalar_tensor_tensor(qn[:, u, RQ:2 * P], lat[:, P:RQ], rq, lnw[:, P:RQ], ALU.mult, ALU.mult)\
                      .then_inc(f.qn_made, 1)
                    nc.vector.scalar_tensor_tensor(kvn[:, u, 0:RKV], lat[:, RQ:RQ + RKV], rc, lnw[:, RQ:RQ + RKV],
                                                   ALU.mult, ALU.mult)
                    dve.wait_ge(f.krot_parts, 3 * (u + 1))
                    nc.vector.tensor_tensor(kvn[:, u, RKV:P], kra[:, u, :], krb[:, u, :], ALU.add).then_inc(f.kvn_made, 1)
                if t < TB:
                    normalise(t)
                if t + 1 < TB:
                    moments(t + 1)
                if t == 2:
                    weights_lo(0)
                if 0 <= t - 4 < TB:
                    u = t - 4
                    tq = bank[TQ[u % 2]]
                    dve.wait_ge(f.qk_hi_made, u + 1)
                    nc.vector.tensor_tensor(ql_lo[:, :, u * P:(u + 1) * P],
                                            tq[:, 0:2 * P].rearrange("p (c n) -> p c n", c=2),
                                            ql_hi[:, :, u * P:(u + 1) * P].bitcast(F32), ALU.subtract)
                    nc.vector.tensor_tensor(kt_lo[:, u * P:(u + 1) * P], tq[:, 2 * P:3 * P],
                                            kt_hi[:, u * P:(u + 1) * P].bitcast(F32), ALU.subtract)\
                      .then_inc(f.qk_split, 1)
                if t == TB:
                    dve.wait_ge(f.cst_in, 16)
                if t in (TB, TB + 1):
                    rotate_swapped(t - TB, t - TB, first=True)
                    rotate_own(t - TB, t - TB, first=True)
                if t in (TB + 1, TB + 3):
                    h = (t - TB - 1) // 2
                    query_lo(h, 0, h)
                if t in (TB + 2, TB + 3):
                    mask_and_max(t - TB - 2, t - TB - 2, first=True)

            body(0, first=True)
            with nc.vector.Fori(1, PAIRS - 1) as p:
                body(p)
            body(PAIRS - 1, last=True)
            split_weights(8)
            split_weights(9)
            split_output(0, 1)
            scale_o(2 * PAIRS - 1, PAIRS - 1, 1)

            steps = [0]

            def step(ins, sem):
                steps[0] += 1
                ins.then_inc(sem, 1)
                dve.wait_ge(sem, steps[0])

            def statistics(st, src, sem):
                step(nc.vector.bn_stats(st[:, 0:6], src), sem)
                step(nc.vector.bn_aggr(st[:, 6:8], st[:, 0:6]), sem)

            def normalise_sum(u):
                dve.wait_ge(c.std2_made, u + 1)
                nc.vector.reciprocal(st2[:, 11:12], st2[:, 8:9]).then_inc(c.rstd2_made, 1)
                dve.wait_ge(c.rstd2_made, u + 1)
                nc.vector.tensor_scalar(xn2[:, :], x1[:, u, :], st2[:, 6:7], st2[:, 11:12],
                                        ALU.subtract, ALU.mult).then_inc(c.xn2_made, 1)
                dve.wait_ge(c.xn2_made, u + 1)
                if u:
                    dve.wait_ge(c.y_turned, u)
                nc.vector.tensor_reduce(fold[:, :], xn2[:, :].rearrange("p (c n) -> p n c", c=DC), AX.X, ALU.add)\
                  .then_inc(c.fold_made, 1)

            def lora_dots(u, js):
                if u == 0:
                    dve.wait_ge(c.a13_in, 16)
                    dve.wait_ge(c.lt_zero, 1)
                for j in js:
                    if u or j >= 2:
                        dve.wait_ge(c.dots_raw, 2 * RANK * u + j - 1)
                    nc.vector.tensor_tensor_reduce(out=dot[:, j % 2, :], in0=xn2[:, :], in1=a13[:, j, :], scale=1.0, scalar=0.0,
                                                   op0=ALU.mult, op1=ALU.add, accum_out=lt[:, j:j + 1])\
                      .then_inc(c.dots_raw, 1)
                if 2 * RANK - 1 in js:
                    dve.wait_ge(c.dots_raw, 2 * RANK * (u + 1))
                    nc.vector.tensor_copy(lt[:, 32:96].rearrange("p (g n) -> p g n", n=32)[:, :, 0:2 * RANK],
                                          lt[:, 0:2 * RANK].unsqueeze(1).to_broadcast([P, 2, 2 * RANK]))\
                      .then_inc(c.dots_made, 1)

            for q in range(10, PAIRS):
                split_weights(q)
            split_output(1, 0)
            nc.vector.memset(lt[:, :], 0.0).then_inc(c.lt_zero, 1)
            for t in range(TB + 1):
                if 0 <= t - 1 < TB:
                    dve.wait_ge(c.o_used, 2 * t)
                    statistics(st2, bank[product(t - 1)][:, :], c.dve_step)
                if 0 <= t - 1 < TB:
                    u = t - 1
                    dve.wait_ge(c.std1_made, u + 1)
                    step(nc.vector.reciprocal(st2[:, 9:10], st2[:, 8:9]), c.dve_step)
                    step(nc.vector.tensor_scalar(st2[:, 10:11], st2[:, 6:7], st2[:, 9:10], -1.0, ALU.mult, ALU.mult),
                         c.dve_step)
                    dve.wait_ge(c.z_made, u + 1)
                    if u == 0:
                        dve.wait_ge(c.x1_in, 16)
                    step(nc.vector.tensor_tensor(x1[:, u, :], x1[:, u, :], xn2[:, :], ALU.add), c.dve_step)
                    statistics(st2, x1[:, u, :], c.dve_step)
                    if t < TB:
                        normalise_sum(u)
                        lora_dots(u, range(2 * RANK))
                if 2 <= t < TB:
                    lora_lo(t - 2)
                if t in (4, 5):
                    dve.wait_ge(g.w_hi_made, t - 3)
                    nc.vector.tensor_tensor(w13_lo[:, t - 4, :], w13[:, t - 4, :], w13_hi[:, t - 4, :].bitcast(F32),
                                            ALU.subtract).then_inc(g.w_split, 1)
                if t == 6:
                    dve.wait_ge(g.bs_hi_made, 1)
                    nc.vector.tensor_tensor(bs_s[32:64, :], bs[32:64, :], bs_s[32:64, :].bitcast(F32), ALU.subtract)\
                      .then_inc(g.bs_split, 1)
                    dve.wait_ge(g.xf_hi_made, 1)
                    nc.vector.tensor_tensor(xf_lo[:, 0:SEQ], xft[:, 0:SEQ], xf_hi[:, 0:SEQ].bitcast(F32), ALU.subtract)\
                      .then_inc(g.xf_split, 1)


            def down_lo(hf, r):
                n = RROWS[r]
                dve.wait_ge(g.fs_hi_made, 3 * hf + r + 1)
                nc.vector.tensor_tensor(fs_lo[0:n, hf, r, :], fs[0:n, hf, r, :], fs_hi[0:n, hf, r, :].bitcast(F32),
                                        ALU.subtract).then_inc(g.fs_split, 1)

            def lora_down_lo(hf):
                dve.wait_ge(g.l2_hi_made, hf + 1)
                nc.vector.scalar_tensor_tensor(l2[:, hf, :], bank[3][:, :], cst[:, 3 * SEQ + 2:3 * SEQ + 3],
                                               l2[:, hf, :].bitcast(F32), ALU.mult, ALU.subtract).then_inc(g.l2_split, 1)

            for hf in range(2):
                for n in range(12):
                    G, rows = 12 * hf + n, RROWS[n // FOLD]
                    dve.wait_ge(g.silu_made, G + 1)
                    dve.wait_ge(g.up_made, G + 1)
                    if G >= 8:
                        dve.wait_ge(g.la_made, G // 4 - 1)
                        dve.wait_ge(g.fold_added, 3 * (G // 4 - 1))
                    nc.vector.tensor_tensor(gu[0:rows, G % 8, :], bank[(7, 2)[G % 2]][0:rows, :], sg[0:rows, G % 2, :],
                                            ALU.mult).then_inc(g.gu_made, 1)
                    if G == 1:
                        normalise_sum(TB - 1)
                        lora_lo(TB - 2)
                    if G in (2, 3):
                        lora_dots(TB - 1, (2 * G - 4, 2 * G - 3))
                    if G == 6:
                        lora_lo(TB - 1)
                        dve.wait_ge(g.xf_hi_made, 2)
                        nc.vector.tensor_tensor(xf_lo[:, SEQ:TOK], xft[:, SEQ:TOK], xf_hi[:, SEQ:TOK].bitcast(F32),
                                                ALU.subtract).then_inc(g.xf_split, 1)
                    if G == 10:
                        dve.wait_ge(g.wd_hi_made, 1)
                        nc.vector.tensor_tensor(wd_lo[:, :, :], wd[:, :, :], wd_hi[:, :, :].bitcast(F32), ALU.subtract)\
                          .then_inc(g.wd_split, 1)
                    if G == 8:
                        dve.wait_ge(g.b2_hi_made, 1)
                        nc.vector.scalar_tensor_tensor(b2[:, :], b2[:, :], cst[:, 3 * SEQ + 3:3 * SEQ + 4],
                                                       b2_s[:, :].bitcast(F32), ALU.mult, ALU.subtract)\
                          .then_inc(g.b2_lo_made, 1)
                        dve.wait_ge(g.b2_lo_made, 1)
                        nc.vector.tensor_scalar(b2_s[:, :], b2[:, :], cst[:, 3 * SEQ + 4:3 * SEQ + 5], None, ALU.mult)\
                          .then_inc(g.b2_split, 1)
                    if n == 8:
                        down_lo(hf, 0)
                    if G == 13:
                        down_lo(0, 1)
                    if G == 14:
                        down_lo(0, 2)
                    if G == 15:
                        lora_down_lo(0)
            down_lo(1, 1)
            down_lo(1, 2)
            lora_down_lo(1)
            for t in range(TB + 1):
                if t < TB:
                    st = st3[:, t % 2, :]
                    dve.wait_ge(g.y_made, t + 1)
                    nc.vector.bn_stats(st[:, 0:6], bank[YB[t % 3]][:, :]).then_inc(g.moments_raw, 1)
                    dve.wait_ge(g.moments_raw, t + 1)
                    nc.vector.bn_aggr(st[:, 6:8], st[:, 0:6]).then_inc(g.moments_made, 1)
                if t:
                    u = t - 1
                    dve.wait_ge(g.z_made, u + 1)
                    if u >= 2:
                        dve.wait_ge((g.out_sent0, g.out_sent1)[u % 2], 16 * (u // 2))
                    nc.vector.tensor_tensor(yo[:, u % 2, :], x1[:, u, :], z2[:, u % 2, :], ALU.add).then_inc(g.out_made, 1)
                if t < TB:
                    dve.wait_ge(g.std_made, t + 1)
                    nc.vector.reciprocal(st[:, 9:10], st[:, 8:9]).then_inc(g.rstd_made, 1)
                    dve.wait_ge(g.rstd_made, t + 1)
                    nc.vector.tensor_scalar(st[:, 10:11], st[:, 6:7], st[:, 9:10], -1.0, ALU.mult, ALU.mult)\
                      .then_inc(g.shift_made, 1)

        @block.tensor
        def _(pe):
            def three(out, w_hi, w_lo, x_hi, x_lo, start, stop):
                nc.tensor.matmul(out, w_hi, x_hi, start=start, stop=False)
                nc.tensor.matmul(out, w_hi, x_lo, start=False, stop=False)
                return nc.tensor.matmul(out, w_lo, x_hi, start=False, stop=stop)

            def absorb_query(w):
                pe.wait_ge(a.sq_in, 16 * (w + 1))
                for k in range(2):
                    for h in range(2):
                        last = nc.tensor.matmul(bank[XB][:, (2 * k + h) * RKV:(2 * k + h + 1) * RKV],
                                                sq[:, (2 * h + k) * P:(2 * h + k + 1) * P],
                                                sq[:, 4 * P + h * RKV:4 * P + (h + 1) * RKV], start=True, stop=True)
                last.then_inc(a.wq_made, 1)

            def query(gi, b, h, w=None, first=False):
                if w is not None:
                    pe.wait_ge(a.wq_split, w + 1)
                if not first:
                    pe.wait_ge(a.q_rotated, gi - 1)
                out, tok = bank[6 + h][:, :], slice(b * SEQ, (b + 1) * SEQ)
                three(out, w1_hi[:, h, :], w1_lo[:, h, :], ql_hi[:, 0, tok], ql_lo[:, 0, tok], True, False)
                nc.tensor.matmul(out, w2[:, h, :], ql_hi[:, 1, tok], start=False, stop=False)
                nc.tensor.matmul(out, w2[:, h, :], ql_lo[:, 1, tok], start=False, stop=True).then_inc(a.q_made, 1)

            def scores(U, k, gi, first=False):
                i, h, b = k % QB, k // QB % 2, k // UNITS
                if i == 0:
                    pe.wait_ge(a.qt_split, gi + 1)
                if not first:
                    pe.wait_ge(a.s_masked, U - 1)
                keys = slice(b * SEQ, b * SEQ + (i + 1) * P)
                three(bank[k % 2][:, 0:(i + 1) * P], qt_hi[:, b, h, i * P:(i + 1) * P], qt_lo[:, b, h, i * P:(i + 1) * P],
                      kt_hi[:, keys], kt_lo[:, keys], True, True).then_inc(a.s_made, 1)

            def turn_p(U, k, first=False):
                pe.wait_ge(a.exp_made, U + 1)
                if not first:
                    pe.wait_ge(a.p_moved, U - 1)
                for j in range(k % QB + 1):
                    last = nc.tensor.transpose(bank[2 + k % 2][:, j * P:(j + 1) * P], pr[:, k % 4, j * P:(j + 1) * P],
                                               ident[:, :])
                last.then_inc(a.p_turned, 1)

            def output(m, b, js, first=False):
                if 0 in js:
                    pe.wait_ge(a.p_moved, UNITS * (m + 1))
                    if not first:
                        pe.wait_ge(a.o_scaled, m)
                for j in js:
                    for h in range(2):
                        last = nc.tensor.matmul(bank[4][RKV * h:RKV * (h + 1), j * P:SEQ], kvn[:, QB * b + j, 0:RKV],
                                                pt[:, b, h, j, j * P:SEQ], start=(j == 0), stop=(j == QB - 1),
                                                skip_group_check=True)
                if QB - 1 in js:
                    last.then_inc(a.o_made, 1)

            def turn_r(m):
                pe.wait_ge(a.rb_made, m + 1)
                for i in range(QB):
                    last = nc.tensor.transpose(bank[XB][:, i * P:(i + 1) * P], rb[:, i, :, :].rearrange("p h n -> p (h n)"),
                                               ident[:, :])
                last.then_inc(a.r_made, 1)

            def absorb_output(p):
                pe.wait_ge(a.sv_in, 16 * (p + 1))
                for h in range(2):
                    last = nc.tensor.matmul(bank[XB][RKV * h:RKV * (h + 1), :], sv[:, h * RKV:(h + 1) * RKV],
                                            sv[:, 2 * RKV + h * D:2 * RKV + (h + 1) * D], start=True, stop=True)
                last.then_inc(a.wvo_made, 1)

            def project(t, hh, ks=range(PAIRS // 2)):
                if 2 * t + hh < 3:
                    pe.wait_ge(c.o_split, 2 * t + hh + 1)
                else:
                    pe.wait_ge(c.o_lo_made, 2 * t + hh - 2)
                if t >= 2 and hh == 0:
                    pe.wait_ge(c.z_made, t - 1)
                for k in ks:
                    q = 8 * hh + k
                    if t == 0:
                        pe.wait_ge(c.wv_split, q + 1)
                    last = three(bank[product(t)][:, :], o_s[:, hh, 0, k, :], o_s[:, hh, 1, k, :],
                                 wv[:, slot(q), 0, :], wv[:, slot(q), 1, :], q == 0, q == PAIRS - 1)
                if PAIRS // 2 - 1 in ks:
                    last.then_inc(c.o_used, 1)

            def body(p, first=False, last=False):
                for k in range(PU):
                    n = k + 2
                    if n < PU:
                        scores(PU * p + n, n, 4 * p + n // QB)
                    elif not last:
                        scores(PU * p + n, n - PU, 4 * p + 4)
                    if k == (2 if first else 0) and not last:
                        if first:
                            pe.wait_ge(f.qk_split, TB - 1)
                        else:
                            pe.wait_ge(a.r_moved, 2 * p - 1)
                        absorb_query(p + 1)
                    if k == 1 and not first:
                        output(2 * p - 1, 1, [0])
                    if k == 2 and not first:
                        output(2 * p - 1, 1, [1])
                    if k == 3 and not first:
                        output(2 * p - 1, 1, [2, 3])
                    if k == 4 and not first:
                        if last:
                            pe.wait_ge(a.r_moved, 2 * p - 1)
                        else:
                            pe.wait_ge(a.wq_split, p + 2)
                        turn_r(2 * p - 1)
                    if k == 8:
                        if first:
                            pe.wait_ge(a.wq_split, p + 2)
                        else:
                            pe.wait_ge(a.r_moved, 2 * p)
                        absorb_output(p)
                    if k in (5, 7) and not last:
                        query(4 * p + 4 + k // 7, 0, k // 7, p + 1)
                    if k == 9:
                        output(2 * p, 0, [0], first)
                    if k == 10:
                        output(2 * p, 0, [1, 2, 3])
                    if last and k in (11, 12, 13, 14, 15):
                        project(0, 0, {11: (0,), 12: (1,), 13: (2,), 14: (3, 4), 15: (5,)}[k])
                    if k == 11:
                        pe.wait_ge(a.wvo_moved, p + 1)
                        turn_r(2 * p)
                    if k in (13, 15) and not last:
                        query(4 * p + 6 + k // 15, 1, k // 15)
                    turn_p(PU * p + k, k, first and k < 2)
                    if first and k < 2:
                        if k == 0:
                            pe.wait_ge(f.qk_split, TB)
                        query(2 + k, 1, k)

            pe.wait_ge(f.ident_made, 1)
            for t in range(TB + 4):
                if 0 <= t - 1 < TB:
                    u = t - 1
                    pe.wait_ge(f.xn_made, u + 1)
                    if u >= 2:
                        pe.wait_ge(f.xt_split, u - 1)
                    for k in range(DC):
                        last = nc.tensor.transpose(bank[u % 2][:, k * P:(k + 1) * P], xn[:, u, k * P:(k + 1) * P],
                                                   ident[:, :])
                    last.then_inc(f.x_turned, 1)
                if 0 <= t - 4 < TB:
                    u = t - 4
                    tq = bank[TQ[u % 2]]
                    pe.wait_ge(f.qn_made, u + 1)
                    pe.wait_ge(f.kvn_made, u + 1)
                    if u == 0:
                        pe.wait_ge(a.wq_split, 1)
                    if u >= 2:
                        pe.wait_ge(f.qk_split, u - 1)
                    nc.tensor.transpose(tq[:, 0:P], qn[:, u, 0:P], ident[:, :])
                    nc.tensor.transpose(tq[:, P:2 * P], qn[:, u, P:2 * P], ident[:, :])
                    nc.tensor.transpose(tq[:, 2 * P:3 * P], kvn[:, u, :], ident[:, :]).then_inc(f.qk_turned, 1)
                if t == 2:
                    absorb_query(0)
                if t == TB:
                    pe.wait_ge(f.qk_split, QB)
                    for h in range(2):
                        query(h, 0, h, 0 if h == 0 else None, first=True)
                if 0 <= t - 2 < TB:
                    u = t - 2
                    pe.wait_ge(f.xt_split, u + 1)
                    if u >= 2:
                        pe.wait_ge(f.kvn_made, u - 1)
                    for k in range(DC):
                        if u == 0:
                            pe.wait_ge(f.wa_split, k + 1)
                        last = three(bank[2 + u % 2][:, 0:LAT], xt_hi[:, u % 4, k, :], xt_lo[:, u % 4, k, :],
                                     wa_hi[:, k, :], wa_lo[:, k, :], k == 0, k == DC - 1)
                    last.then_inc(f.lat_made, 1)
                if t in (TB + 2, TB + 3):
                    scores(t - TB - 2, t - TB - 2, 0, first=True)

            body(0, first=True)
            with nc.tensor.Fori(1, PAIRS - 1) as p:
                body(p)
            body(PAIRS - 1, last=True)
            output(2 * PAIRS - 1, 1, [0, 1, 2, 3])

            def turn_y(u):
                pe.wait_ge(c.fold_made, u + 1)
                pe.wait_ge(c.dots_made, u + 1)
                if u:
                    pe.wait_ge(c.xt2_moved, u)
                    pe.wait_ge(c.lp_split, u)
                nc.tensor.transpose(bank[3][:, 0:P], fold[:, :], ident[:, :])
                nc.tensor.transpose(bank[4][0:96, 0:P], lt[:, :], ident[:, :]).then_inc(c.y_turned, 1)

            pe.wait_ge(a.r_moved, 2 * PAIRS - 1)
            turn_r(2 * PAIRS - 1)
            pe.wait_ge(a.s_masked, PU * PAIRS)
            project(0, 0, (6, 7))
            project(0, 1)
            for t in range(1, TB):
                project(t, 0)
                if t >= 2:
                    turn_y(t - 2)
                project(t, 1)

            def gate_or_up(which, G, n, hf):
                r, k = n // FOLD, n % FOLD
                rows, j, tok = RROWS[r], k * W2C + r * P, slice(hf * SEQ, (hf + 1) * SEQ)
                out = bank[5 + G % 2 if which == 0 else (7, 2)[G % 2]][0:rows, :]
                three(out, w13_hi[:, which, j:j + rows], w13_lo[:, which, j:j + rows], xf_hi[:, tok], xf_lo[:, tok],
                      True, False)
                return nc.tensor.matmul(out, bs_s[:, j:j + rows], (lg, lu)[which][0:96, tok], start=False, stop=True)

            def lora_down(hf, r):
                G, rows = 12 * hf + 4 * r, RROWS[r]
                pe.wait_ge(g.a2_in, 16)
                pe.wait_ge(g.gu_made, G + 4)
                if hf and r == 0:
                    pe.wait_ge(g.l2_split, 1)
                for k in range(FOLD):
                    last = nc.tensor.matmul(bank[3][32 * k:32 * k + 32, :], a2[0:rows, r, k, :], gu[0:rows, (G + k) % 8, :],
                                            start=(r == 0), stop=(r == RT - 1), tile_position=(0, 32 * k),
                                            skip_group_check=True)
                last.then_inc(g.la_made, 1)

            pe.wait_ge(g.xf_split, 1)
            pe.wait_ge(g.bs_split, 1)
            pe.wait_ge(c.lp_split, QB)
            for hf in range(2):
                for n in range(12):
                    G = 12 * hf + n
                    if G == 0:
                        pe.wait_ge(g.w_split, 2)
                    if G == 12:
                        pe.wait_ge(g.xf_split, 2)
                        pe.wait_ge(c.lp_split, TB)
                    if G >= 2:
                        pe.wait_ge(g.silu_made, G - 1)
                    gate_or_up(0, G, n, hf).then_inc(g.gate_made, 1)
                    if G >= 2:
                        pe.wait_ge(g.gu_made, G - 1)
                    gate_or_up(1, G, n, hf).then_inc(g.up_made, 1)
                    if G == 0:
                        turn_y(TB - 2)
                    if G == 5:
                        turn_y(TB - 1)
                    if G == 7:
                        pe.wait_ge(c.xt2_moved, TB)
                    if n in (5 if hf else 7, 9):
                        lora_down(hf, n // 8)
                    if G == 13:
                        lora_down(0, RT - 1)
            pe.wait_ge(g.wd_split, 1)
            pe.wait_ge(g.b2_split, 1)
            for t in range(TB):
                if t == 1:
                    lora_down(1, RT - 1)
                hf, q = t // QB, t % QB * P
                pe.wait_ge(g.fs_split, 3 * (hf + 1))
                pe.wait_ge(g.l2_split, hf + 1)
                if t >= 3:
                    pe.wait_ge(g.z_made, t - 2)
                for r in range(RT):
                    n = RROWS[r]
                    three(bank[YB[t % 3]][:, :], fs_hi[0:n, hf, r, q:q + P], fs_lo[0:n, hf, r, q:q + P], wd_hi[0:n, r, :],
                          wd_lo[0:n, r, :], r == 0, False)
                nc.tensor.matmul(bank[YB[t % 3]][:, :], l2[:, hf, q:q + P], b2_s[:, :], start=False, stop=True)\
                  .then_inc(g.y_made, 1)


def kernel(**inputs):
    import concourse.bacc as bacc
    from concourse.bass_utils import run_bass_kernel_spmd

    I = {k.removeprefix("L0_"): np.asarray(v) for k, v in inputs.items()}
    x = I["attn_hidden_states"]
    f32 = np.float32
    evens_odds = np.r_[0:ROPE:2, 1:ROPE:2]

    def put(shape, *parts):
        a = np.zeros(shape, f32)
        for at, v in parts:
            a[at] = v
        return a

    wkv_a = np.concatenate([I["attn_Wkv_a"][:, :RKV], I["attn_Wkv_a"][:, RKV:][:, evens_odds]], 1)
    wa = np.concatenate([I["attn_Wq_a"], wkv_a], 1).reshape(DC, P, LAT).transpose(1, 0, 2)
    lnw = np.broadcast_to(np.concatenate([I["attn_q_a_ln_w"], I["attn_kv_a_ln_w"]]), (P, RQ + RKV))

    inv = (1.0 / f32(10000.0) ** (np.arange(0, ROPE, 2, dtype=f32) / f32(ROPE))).astype(f32)
    ang = np.outer(np.arange(SEQ, dtype=f32), inv).astype(f32)
    cos, sin = np.cos(ang).astype(f32), np.sin(ang).astype(f32)
    cst = np.zeros((P, 3 * SEQ + 8), f32)
    cst[:, SEQ - P:SEQ] = np.where(np.arange(P)[None, :] > np.arange(P)[:, None], f32(-BIG), f32(0))
    cst[:64, SEQ:2 * SEQ] = 1
    cst[64:, SEQ:2 * SEQ] = np.concatenate([cos.T, cos.T])
    cst[64:96, 2 * SEQ:3 * SEQ] = sin.T
    cst[96:128, 2 * SEQ:3 * SEQ] = -sin.T
    for g in range(3):
        cst[32 * g:32 * g + 2, 3 * SEQ] = LORA_SCALE
        cst[32 * g + 2:32 * g + 4, 3 * SEQ + 1] = LORA_SCALE
    for k in range(FOLD):
        cst[32 * k + RANK:32 * k + 2 * RANK, 3 * SEQ + 2] = LORA_SCALE
        cst[32 * k + 2 * RANK:32 * k + 3 * RANK, 3 * SEQ + 3] = 1
        cst[32 * k:32 * k + 3 * RANK, 3 * SEQ + 4] = [1] * RANK + [-1] * 2 * RANK
    kcs = np.concatenate([cos, cos, -sin, sin], 1).reshape(QB, P, 2, ROPE).transpose(1, 0, 2, 3)

    wq = I["attn_Wq_b"].reshape(RQ, H, NOPE + ROPE)
    wkv = I["attn_Wkv_b"].reshape(RKV, H, NOPE + VD)
    qT = wq[:, :, :NOPE].transpose(1, 2, 0)
    qT = np.concatenate([qT, qT[:, :, P:]], 2).reshape(PAIRS, 2, NOPE, 2 * P).transpose(0, 2, 1, 3)
    kT = wkv[:, :, :NOPE].transpose(1, 2, 0).reshape(PAIRS, 2, NOPE, RKV).transpose(0, 2, 1, 3)
    pe = wq[:, :, NOPE:][:, :, evens_odds].reshape(RQ, PAIRS, 2, ROPE).transpose(1, 0, 2, 3)
    sq = np.concatenate([qT.reshape(PAIRS, P, -1), kT.reshape(PAIRS, P, -1), pe[:, :P].reshape(PAIRS, P, -1),
                         np.concatenate([pe[:, P:], pe[:, P:]], 1).reshape(PAIRS, P, -1)], 2)
    vT = wkv[:, :, NOPE:].transpose(1, 2, 0).reshape(PAIRS, 2, VD, RKV).transpose(0, 2, 1, 3)
    wo = I["attn_Wo"].reshape(PAIRS, 2, VD, D).transpose(0, 2, 1, 3)
    sv = np.concatenate([vT.reshape(PAIRS, P, -1), wo.reshape(PAIRS, P, -1)], 2)

    w13 = np.stack([I["ffn_w1q"].T, I["ffn_w3q"].T], 1)
    bs = put((96, HID), *[(slice(32 * g + 2 * k, 32 * g + 2 * k + 2), I[n].T)
                          for g in range(3) for k, n in enumerate(("ffn_b1", "ffn_b3"))])
    a13 = np.broadcast_to(np.concatenate([I["ffn_a1"], I["ffn_a3"]]), (P, 2 * RANK, D))
    a2r = I["ffn_a2"].reshape(RANK, FOLD, W2C)
    a2 = put((P, RT, FOLD, 32), *[((slice(0, RROWS[r]), r, slice(None), slice(g * RANK, (g + 1) * RANK)),
                                   a2r[:, :, r * P:r * P + RROWS[r]].transpose(2, 1, 0)) for r in range(RT)
                                  for g in range(3)])
    w2 = put((P, RT, D), *[((slice(0, RROWS[r]), r), I["ffn_w2q"].T[r * P:r * P + RROWS[r]]) for r in range(RT)])
    b2 = put((P, D), *[(slice(32 * k + g * RANK, 32 * k + (g + 1) * RANK), I["ffn_b2"].T)
                       for k in range(FOLD) for g in range(3)])

    nc = bacc.Bacc("TRN2", target_bir_lowering=False, num_devices=1)
    arrays = dict(x=x, wa=wa, lnw=lnw, cst=cst, kcs=kcs, sq=sq, sv=sv, w13=w13, bs=bs, a13=a13, a2=a2, w2=w2, b2=b2)
    arrays = {k: np.ascontiguousarray(v) for k, v in arrays.items()}
    args = [nc.dram_tensor(k, v.shape, F32, kind="ExternalInput").ap() for k, v in arrays.items()]
    out = nc.dram_tensor("out", x.shape, F32, kind="ExternalOutput").ap()
    build(nc, *args, out)
    r = run_bass_kernel_spmd(nc, [arrays], core_ids=[0])
    return r.results[0]["out"]
```
